# Optimizing a Trainium2 kernel written in Bass

```python
import numpy as np
import jax
import jax.numpy as jnp

def _softmax(x, axis=-1):
    return jax.nn.softmax(x, axis=axis)

def _gelu(x):
    return jax.nn.gelu(x, approximate=True)

def _silu(x):
    return jax.nn.silu(x)

def _sigmoid(x):
    return jax.nn.sigmoid(x)

def _layernorm(x, axis=-1, eps=1e-05):
    m = jnp.mean(x, axis=axis, keepdims=True)
    v = jnp.var(x, axis=axis, keepdims=True)
    return (x - m) / jnp.sqrt(v + eps)

def _scatter_add(tgt, idx, src, axis=0):
    return tgt.at[idx].add(src)

def _segment_sum(src, seg, n):
    return jax.ops.segment_sum(src, seg, n)
kernel_name = 'mk_sandwich_d1_jaxref_r4_856e08'

def setup_inputs(seed: int=0):
    np.random.seed(seed)
    _w = jnp.asarray

    def _L0_attn_setup():
        import jax, jax.numpy as jnp
        import numpy as np
        B_, L_, D_MODEL, D_INNER, N_, DT_RANK, K_ = (2, 512, 512, 1024, 16, 128, 4)

        def _causal_depthwise_conv(x, w, b):
            K = w.shape[0]
            L = x.shape[1]
            padded = jnp.pad(x, ((0, 0), (K - 1, 0), (0, 0)))
            out = sum((w[k] * padded[:, k:k + L, :] for k in range(K)))
            return out + b

        def _selective_scan(x, delta, Bm, Cm, A):
            b, L, d = x.shape
            n = A.shape[1]

            def step(h, inp):
                dt_t, B_t, C_t, x_t = inp
                dA = jnp.exp(dt_t[..., None] * A)
                h = dA * h + (dt_t * x_t)[..., None] * B_t[:, None, :]
                y = jnp.einsum('bdn,bn->bd', h, C_t)
                return (h, y)
            xs = (delta.transpose(1, 0, 2), Bm.transpose(1, 0, 2), Cm.transpose(1, 0, 2), x.transpose(1, 0, 2))
            h0 = jnp.zeros((b, d, n), x.dtype)
            _, ys = jax.lax.scan(step, h0, xs)
            return ys.transpose(1, 0, 2)
        key = jax.random.key(seed)
        ks = jax.random.split(key, 12)
        sc = lambda fan_in: 1.0 / np.sqrt(fan_in)
        hidden_states = jax.random.normal(ks[0], (B_, L_, D_MODEL), dtype=jnp.float32)
        W_in = jax.random.normal(ks[1], (D_MODEL, 2 * D_INNER), jnp.float32) * sc(D_MODEL)
        b_in = jnp.zeros((2 * D_INNER,), jnp.float32)
        conv_w = jax.random.normal(ks[2], (K_, D_INNER), jnp.float32) * (1.0 / np.sqrt(K_ * D_INNER))
        conv_b = jnp.zeros((D_INNER,), jnp.float32)
        W_x = jax.random.normal(ks[3], (D_INNER, DT_RANK + 2 * N_), jnp.float32) * sc(D_INNER)
        W_dt = jax.random.normal(ks[4], (DT_RANK, D_INNER), jnp.float32) * sc(DT_RANK)
        b_dt = jnp.zeros((D_INNER,), jnp.float32)
        W_out = jax.random.normal(ks[5], (D_INNER, D_MODEL), jnp.float32) * sc(D_INNER)
        b_out = jnp.zeros((D_MODEL,), jnp.float32)
        a_log = jnp.log(jnp.tile(jnp.arange(1, N_ + 1, dtype=jnp.float32)[None, :], (D_INNER, 1)))
        d_param = jnp.ones((D_INNER,), jnp.float32)
        return {'hidden_states': hidden_states, 'W_in': W_in, 'b_in': b_in, 'conv_w': conv_w, 'conv_b': conv_b, 'W_x': W_x, 'W_dt': W_dt, 'b_dt': b_dt, 'W_out': W_out, 'b_out': b_out, 'a_log': a_log, 'd_param': d_param}
    _L0_attn_in = _L0_attn_setup()

    def _L0_ffn_setup():
        import jax, jax.numpy as jnp
        import numpy as np
        HIDDEN = 512
        INTER = 2048
        SCALE = 64.0

        def fwht(x):
            orig_shape = x.shape
            n = orig_shape[-1]
            x = x.reshape(-1, n)
            h = 1
            while h < n:
                x = x.reshape(-1, n // (2 * h), 2, h)
                a, b = (x[:, :, 0, :], x[:, :, 1, :])
                x = jnp.stack([a + b, a - b], axis=2).reshape(-1, n)
                h *= 2
            return (x / jnp.sqrt(jnp.asarray(n, x.dtype))).reshape(orig_shape)
        key = jax.random.key(seed)
        ks = jax.random.split(key, 8)
        inp = jax.random.normal(ks[0], (4, 512, HIDDEN), dtype=jnp.float32)
        SU_ug = jnp.where(jax.random.bernoulli(ks[1], 0.5, (HIDDEN,)), 1.0, -1.0).astype(jnp.float32)
        SU_dp = jnp.where(jax.random.bernoulli(ks[2], 0.5, (INTER,)), 1.0, -1.0).astype(jnp.float32)
        Wscale_ug = jax.random.uniform(ks[3], (2 * INTER,), jnp.float32, 0.5, 1.5)
        Wscale_dp = jax.random.uniform(ks[4], (HIDDEN,), jnp.float32, 0.5, 1.5)
        W_up = jax.random.normal(ks[5], (INTER, HIDDEN), dtype=jnp.float32) * 0.02
        W_gate = jax.random.normal(ks[6], (INTER, HIDDEN), dtype=jnp.float32) * 0.02
        W_down = jax.random.normal(ks[7], (HIDDEN, INTER), dtype=jnp.float32) * 0.02
        return {'input': inp, 'SU_ug': SU_ug, 'SU_dp': SU_dp, 'Wscale_ug': Wscale_ug, 'Wscale_dp': Wscale_dp, 'W_up': W_up, 'W_gate': W_gate, 'W_down': W_down}
    _L0_ffn_in = _L0_ffn_setup()
    _d = {'L0_attn_hidden_states': _L0_attn_in['hidden_states'], 'L0_attn_W_in': _L0_attn_in['W_in'], 'L0_attn_b_in': _L0_attn_in['b_in'], 'L0_attn_conv_w': _L0_attn_in['conv_w'], 'L0_attn_conv_b': _L0_attn_in['conv_b'], 'L0_attn_W_x': _L0_attn_in['W_x'], 'L0_attn_W_dt': _L0_attn_in['W_dt'], 'L0_attn_b_dt': _L0_attn_in['b_dt'], 'L0_attn_W_out': _L0_attn_in['W_out'], 'L0_attn_b_out': _L0_attn_in['b_out'], 'L0_attn_a_log': _L0_attn_in['a_log'], 'L0_attn_d_param': _L0_attn_in['d_param'], 'L0_ffn_SU_ug': _L0_ffn_in['SU_ug'], 'L0_ffn_SU_dp': _L0_ffn_in['SU_dp'], 'L0_ffn_Wscale_ug': _L0_ffn_in['Wscale_ug'], 'L0_ffn_Wscale_dp': _L0_ffn_in['Wscale_dp'], 'L0_ffn_W_up': _L0_ffn_in['W_up'], 'L0_ffn_W_gate': _L0_ffn_in['W_gate'], 'L0_ffn_W_down': _L0_ffn_in['W_down']}
    _x0 = _d['L0_attn_hidden_states']
    _d['L0_attn_hidden_states'] = jax.random.normal(jax.random.fold_in(jax.random.key(seed), 1), (4, 1024, 512), dtype=_x0.dtype)
    del _x0
    return _d

def reference(L0_attn_hidden_states, L0_attn_W_in, L0_attn_b_in, L0_attn_conv_w, L0_attn_conv_b, L0_attn_W_x, L0_attn_W_dt, L0_attn_b_dt, L0_attn_W_out, L0_attn_b_out, L0_attn_a_log, L0_attn_d_param, L0_ffn_SU_ug, L0_ffn_SU_dp, L0_ffn_Wscale_ug, L0_ffn_Wscale_dp, L0_ffn_W_up, L0_ffn_W_gate, L0_ffn_W_down):

    def _L0_attn_ref(hidden_states, W_in, b_in, conv_w, conv_b, W_x, W_dt, b_dt, W_out, b_out, a_log, d_param):
        import jax, jax.numpy as jnp
        import numpy as np
        B_, L_, D_MODEL, D_INNER, N_, DT_RANK, K_ = (2, 512, 512, 1024, 16, 128, 4)

        def _causal_depthwise_conv(x, w, b):
            K = w.shape[0]
            L = x.shape[1]
            padded = jnp.pad(x, ((0, 0), (K - 1, 0), (0, 0)))
            out = sum((w[k] * padded[:, k:k + L, :] for k in range(K)))
            return out + b

        def _selective_scan(x, delta, Bm, Cm, A):
            b, L, d = x.shape
            n = A.shape[1]

            def step(h, inp):
                dt_t, B_t, C_t, x_t = inp
                dA = jnp.exp(dt_t[..., None] * A)
                h = dA * h + (dt_t * x_t)[..., None] * B_t[:, None, :]
                y = jnp.einsum('bdn,bn->bd', h, C_t)
                return (h, y)
            xs = (delta.transpose(1, 0, 2), Bm.transpose(1, 0, 2), Cm.transpose(1, 0, 2), x.transpose(1, 0, 2))
            h0 = jnp.zeros((b, d, n), x.dtype)
            _, ys = jax.lax.scan(step, h0, xs)
            return ys.transpose(1, 0, 2)
        proj = hidden_states @ W_in + b_in
        hidden, gate = jnp.split(proj, 2, axis=-1)
        conv_out = jax.nn.silu(_causal_depthwise_conv(hidden, conv_w, conv_b))
        xproj = conv_out @ W_x
        dt_in, Bm, Cm = jnp.split(xproj, [DT_RANK, DT_RANK + N_], axis=-1)
        delta = jax.nn.softplus(dt_in @ W_dt + b_dt)
        A = -jnp.exp(a_log)
        y = _selective_scan(conv_out, delta, Bm, Cm, A)
        y = y + conv_out * d_param
        y = y * jax.nn.silu(gate)
        return y @ W_out + b_out

    def _L0_ffn_ref(input, SU_ug, SU_dp, Wscale_ug, Wscale_dp, W_up, W_gate, W_down):
        import jax, jax.numpy as jnp
        import numpy as np
        HIDDEN = 512
        INTER = 2048
        SCALE = 64.0

        def fwht(x):
            orig_shape = x.shape
            n = orig_shape[-1]
            x = x.reshape(-1, n)
            h = 1
            while h < n:
                x = x.reshape(-1, n // (2 * h), 2, h)
                a, b = (x[:, :, 0, :], x[:, :, 1, :])
                x = jnp.stack([a + b, a - b], axis=2).reshape(-1, n)
                h *= 2
            return (x / jnp.sqrt(jnp.asarray(n, x.dtype))).reshape(orig_shape)
        n = SU_ug.shape[0]
        x = input.reshape(-1, n)
        x = fwht(x * SU_ug) / SCALE
        x_up = x @ W_up.T * (Wscale_ug[:INTER] * SCALE)
        x_gate = x @ W_gate.T * (Wscale_ug[INTER:] * SCALE)
        x = jax.nn.silu(x_gate) * x_up
        x = fwht(x * SU_dp) / SCALE
        x = x @ W_down.T * (Wscale_dp * SCALE)
        return x.reshape(input.shape)
    x = L0_attn_hidden_states
    x = x + _layernorm(_L0_attn_ref(_layernorm(x, axis=-1), L0_attn_W_in, L0_attn_b_in, L0_attn_conv_w, L0_attn_conv_b, L0_attn_W_x, L0_attn_W_dt, L0_attn_b_dt, L0_attn_W_out, L0_attn_b_out, L0_attn_a_log, L0_attn_d_param), axis=-1)
    x = x + _layernorm(_L0_ffn_ref(_layernorm(x, axis=-1), L0_ffn_SU_ug, L0_ffn_SU_dp, L0_ffn_Wscale_ug, L0_ffn_Wscale_dp, L0_ffn_W_up, L0_ffn_W_gate, L0_ffn_W_down), axis=-1)
    return x

_drawn_inputs = setup_inputs


def setup_inputs(seed=0):
    import zlib

    import numpy as np

    out = dict(_drawn_inputs(seed))
    spreads = {'L0_attn_b_in': (0.0, 0.1),
     'L0_attn_conv_b': (0.0, 0.1),
     'L0_attn_b_dt': (0.0, 0.8),
     'L0_attn_b_out': (0.0, 0.1),
     'L0_attn_d_param': (1.0, 0.2)}
    factors = {'L0_attn_W_x': 8.0, 'L0_attn_W_dt': 8.0, 'L0_attn_a_log': 8.0}
    for name, (base, spread) in spreads.items():
        noise = np.random.default_rng([zlib.crc32(name.encode()), seed]).standard_normal(out[name].shape)
        drawn = base * np.exp(spread * noise) if base else spread * noise
        out[name] = jnp.asarray(drawn.astype(out[name].dtype))
    for name, factor in factors.items():
        out[name] = (out[name] * factor).astype(out[name].dtype)
    return out
```

```python
import concourse.bass as bass
from concourse import mybir
from contextlib import ExitStack

F32 = mybir.dt.float32
F32R = mybir.dt.float32r
ALU = mybir.AluOpType
ACT = mybir.ActivationFunctionType

P = 128
DM, DI, NST, DTR, KC = 512, 1024, 16, 128, 4
FF = 2048
BATCH, SEQ = 4, 1024
TOK = BATCH * SEQ
EPS = 1e-5
BIG = 3.0e38

T = 256
TB = T // P
NCH = TOK // T
CPB = SEQ // T
KT = DM // P
DT = DI // P
HALO = KC - 1


def wait_first(eng, sem, value, passed):
    eng.wait_ge(sem, value)
    eng.sem_inc(passed, 1)


def mamba_block(nc, x, W, scratch_bc, x2):
    ctx = ExitStack()
    with ctx:
        def sb(name, shape, dt=F32):
            return ctx.enter_context(nc.sbuf_tensor(name, shape, dt))

        def pb(name, shape):
            return ctx.enter_context(nc.psum_tensor(name, shape, F32))

        def sem(name):
            return ctx.enter_context(nc.semaphore(name))

        w_in = sb("w_in", [P, KT, 2 * DI])
        w_x = sb("w_x", [P, DT, DTR + 2 * NST])
        w_dt = sb("w_dt", [P, DI])
        w_out = sb("w_out", [P, DT, DM])
        taps = sb("taps", [P, DT, KC])
        diag = sb("diag", [P, DT * KC, P])
        ident = sb("ident", [P, P])
        b_in = sb("b_in", [P, 2 * DT])
        b_conv = sb("b_conv", [P, DT])
        b_dt = sb("b_dt", [P, DT])
        d_skip = sb("d_skip", [P, DT])
        b_out = sb("b_out", [1, DM])
        ones = sb("ones", [1, P])
        a_neg = sb("a_neg", [P, DT, NST])
        lim = sb("lim", [P, NCH + 1, 2])
        lim_now = sb("lim_now", [P, 2])
        half = sb("half", [P, TB])
        xb = sb("xb", [P, TB, DM])
        stats = sb("stats", [P, TB, 6])
        mv = sb("mv", [P, TB, 2])
        veps = sb("veps", [P, TB])
        rstd = sb("rstd", [P, TB])
        stats2 = sb("stats2", [P, TB, 6])
        mv2 = sb("mv2", [P, TB, 2])
        veps2 = sb("veps2", [P, TB])
        rstd2 = sb("rstd2", [P, TB])
        shift2 = sb("shift2", [P, TB])
        xnT = [sb(f"xnT{i}", [P, KT, T]) for i in range(2)]
        hid = sb("hid", [P, DT, HALO + T])
        soft_e = hid[:, :, 0:T]
        soft_w = sb("soft_w", [P, DT, T])
        conv = [sb(f"conv{i}", [P, DT, T]) for i in range(2)]
        delta = [sb(f"delta{i}", [P, DT, T]) for i in range(2)]
        gate = sb("gate", [P, DT, T])
        u = sb("u", [P, DT, T])
        dtin = soft_w[:, 0, :]
        bc = soft_w[0:2 * NST, 1, :]
        bcT = [sb(f"bcT{i}", [P, TB, 2 * NST]) for i in range(2)]
        NBG = 2
        NG = NST // NBG
        bb = [sb(f"bb{i}", [P, NBG, T]) for i in range(2)]
        dbx = [sb(f"dbx{i}", [P, DT, T]) for i in range(2)]
        h = [sb(f"h{i}", [P, DT, T]) for i in range(2)]
        da = sb("da", [P, DT, T])
        carry = sb("carry", [P, NST, DT])
        acc = sb("acc", [P, TB, DI])

        hT = [pb(f"hT{i}", [P, DI]) for i in range(2)]
        pM = pb("pM", [P, 4, T])
        pX = pb("pX", [P, 2, DM])

        loaded = sem("loaded"); setup_d = sem("setup_d"); setup_p = sem("setup_p"); setup_a = sem("setup_a")
        x_in = sem("x_in"); res_in = sem("res_in"); x2_stored = sem("x2_stored")
        stats_done = sem("stats_done"); mv_done = sem("mv_done"); veps_done = sem("veps_done")
        rstd_done = sem("rstd_done"); xn_done = sem("xn_done")
        halo_done = sem("halo_done"); lim_done = sem("lim_done")
        m_filled = sem("m_filled"); m_evac = sem("m_evac")
        conv_done = sem("conv_done"); gate_done = sem("gate_done")
        bc_stored = sem("bc_stored")
        bb_in = [sem("bb_in0"), sem("bb_in1")]
        e_done = sem("e_done"); w_done = sem("w_done"); q_done = sem("q_done"); ln_done = sem("ln_done")
        lq_done = sem("lq_done"); delta_done = sem("delta_done"); u_done = sem("u_done")
        da_done = sem("da_done"); dbx_done = sem("dbx_done"); scan_done = sem("scan_done")
        carry_done = sem("carry_done"); h_turned = sem("h_turned"); acc_done = sem("acc_done")
        y_turned = sem("y_turned"); y_skip = sem("y_skip"); y_gated = sem("y_gated"); out_mm = sem("out_mm")
        st2_done = sem("st2_done"); mv2_done = sem("mv2_done"); veps2_done = sem("veps2_done")
        rstd2_done = sem("rstd2_done"); shift2_done = sem("shift2_done"); res_done = sem("res_done")
        z_done = sem("z_done")
        NLOAD = 13
        sp_passed, pe_passed, dve_passed, pool_passed = (sem(f"{e}_passed") for e in ("sp", "pe", "dve", "pool"))

        FRONT_UNITS = ["xT"] * KT + ["hid"] * DT + ["conv"] * DT + ["dtin", "bc"] + ["bcT"] * TB + ["dt"] * DT
        U_FRONT, U_ALL = len(FRONT_UNITS), len(FRONT_UNITS) + DT
        assert U_FRONT % 4 == 0 and U_ALL % 4 == 0
        O_XT, O_HID, O_CONV = 0, KT, KT + DT
        O_DTIN = O_CONV + DT
        O_BC = O_DTIN + 1
        O_BCT = O_BC + 1
        O_DT = O_BCT + TB
        O_GATE = U_FRONT

        def unit(c, i):
            if isinstance(c, int) and c < 0:
                return i
            return c * U_ALL + (U_FRONT + i)

        def gate_unit(c, i, has_front):
            return unit(c, i + (O_GATE if has_front else 0))

        block = ctx.enter_context(nc.Block())

        def schedule(iteration, front0, epilogue):
            front0()
            iteration(0, 0, False, True)

            def pair(p):
                for j in range(2):
                    iteration(2 * p + (1 + j), (1 + j) % 2, True, True)
            return pair, lambda: (iteration(NCH - 1, (NCH - 1) % 2, True, False), epilogue())

        def run(eng, iteration, front0, epilogue):
            pair, finish = schedule(iteration, front0, epilogue)
            with eng.Fori(0, (NCH - 2) // 2) as p:
                pair(p)
            finish()

        @block.sync
        def _(sp):
            sp.dma_start(xb[:, :, :], x[0, :, :].rearrange("(a p) m -> p a m", p=P)).then_inc(x_in, 16)
            sp.dma_start(w_in[:, :, :], W["W_in"].rearrange("(k p) n -> p k n", p=P)).then_inc(loaded, 16)
            for dst, name in ((taps[:, :, :], "conv_w"), (b_in[:, :], "b_in"), (b_conv[:, :], "conv_b"),
                              (b_dt[:, :], "b_dt"), (d_skip[:, :], "d_param"), (a_neg[:, :, :], "a_log")):
                sp.dma_start(dst, W[name]).then_inc(loaded, 16)
            sp.dma_start(ident[:, :], W["ident"]).then_inc(loaded, 16)
            sp.dma_start(w_x[:, :, :], W["W_x"].rearrange("(k p) n -> p k n", p=P)).then_inc(loaded, 16)
            sp.dma_start(w_dt[:, :], W["W_dt"]).then_inc(loaded, 16)
            sp.dma_start(w_out[:, :, :], W["W_out"].rearrange("(k p) n -> p k n", p=P)).then_inc(loaded, 16)
            sp.dma_start(b_out[:, :], W["b_out"].rearrange("(a n) -> a n", a=1)).then_inc(loaded, 16)
            sp.dma_start(ones[:, :], W["ones"]).then_inc(loaded, 16)

            def b_rows(c, g):
                sp.dma_start(bb[g % 2][:, :, :],
                             scratch_bc[bass.ds(c, 1), NBG * g:NBG * (g + 1), :].broadcast_to([P, NBG, T])
                             ).then_inc(bb_in[g % 2], 16)

            def front_store(c1, first):
                wait_first(sp, m_evac, unit(c1 - 1, O_BC) + 1, sp_passed)
                sp.dma_start(scratch_bc[bass.ds(c1, 1), :, :].rearrange("a n t -> (a n) t"), bc[:, :]).then_inc(bc_stored, 16)
                wait_first(sp, bc_stored, 16 * (c1 + 1), sp_passed)
                for g in range(2):
                    if not first:
                        wait_first(sp, dbx_done, (c1 - 1) * NST + NST - NBG + NBG * g, sp_passed)
                    b_rows(c1, g)

            def front0():
                front_store(0, True)

            def iteration(c, par, has_back, has_front):
                if has_front:
                    if isinstance(c, int) and c == 0:
                        wait_first(sp, m_filled, KT, sp_passed)
                    elif not isinstance(c, int):
                        wait_first(sp, m_filled, unit(c - 1, O_XT + KT - 1) + 1, sp_passed)
                    sp.dma_start(xb[:, :, :], x[bass.ds(c + 1, 1), :, :].rearrange("q (a p) m -> p (q a) m", p=P)).then_inc(x_in, 16)
                if has_back:
                    if has_front:
                        wait_first(sp, m_filled, unit(c, O_XT + KT - 1) + 1, sp_passed)
                    sp.dma_start(xb[:, :, :], x[bass.ds(c - 1, 1), :, :].rearrange("q (a p) m -> p (q a) m", p=P)).then_inc(res_in, 16)
                def more_rows(groups):
                    for g in groups:
                        wait_first(sp, dbx_done, c * NST + NBG * (g - 1), sp_passed)
                        b_rows(c, g)

                more_rows(range(2, 6))
                if has_back:
                    wait_first(sp, z_done, TB * c, sp_passed)
                    sp.dma_start(x2[bass.ds(c - 1, 1), :, :].rearrange("q (a p) m -> p (q a) m", p=P), xb[:, :, :]).then_inc(x2_stored, 16)
                    wait_first(sp, x2_stored, 16 * c, sp_passed)
                more_rows(range(6, NG))
                if has_front:
                    front_store(c + 1, False)

            def epilogue():
                sp.dma_start(xb[:, :, :], x[NCH - 1, :, :].rearrange("(a p) m -> p a m", p=P)).then_inc(res_in, 16)
                wait_first(sp, z_done, TB * NCH, sp_passed)
                sp.dma_start(x2[NCH - 1, :, :].rearrange("(a p) m -> p a m", p=P), xb[:, :, :]).then_inc(x2_stored, 16)
                wait_first(sp, x2_stored, 16 * NCH, sp_passed)

            run(sp, iteration, front0, epilogue)

        @block.tensor
        def _(pe):
            def take(i, number):
                if i % 2 == 0 and not (isinstance(number, int) and number < 4):
                    pe.wait_ge(m_evac, number - 2)

            def slot_of(i):
                return i % 4

            def xT(c, kt, par):
                n = unit(c, O_XT + kt)
                if kt == 0:
                    pe.wait_ge(xn_done, TB * (c + 2))
                take(kt, n)
                for tb in range(TB):
                    mm = pe.transpose(pM[:, slot_of(O_XT + kt), tb * P:(tb + 1) * P],
                                      xb[:, tb, kt * P:(kt + 1) * P], ident[:, :])
                mm.then_inc(m_filled, 1)

            def in_proj(c, i, column, src):
                take(i, unit(c, i))
                for kt in range(KT):
                    mm = pe.matmul(pM[:, slot_of(i), :], w_in[:, kt, column:column + P], src[:, kt, :],
                                   start=(kt == 0), stop=(kt == KT - 1))
                mm.then_inc(m_filled, 1)

            def hidden(c, dt, par):
                if dt == 0:
                    pe.wait_ge(m_evac, unit(c, O_XT + KT - 1) + 1)
                in_proj(c, O_HID + dt, dt * P, xnT[1 - par])

            def conv_taps(c, dt):
                if dt == 0:
                    pe.wait_ge(m_evac, unit(c, O_HID + DT - 1) + 1)
                take(O_CONV + dt, unit(c, O_CONV + dt))
                for k in range(KC):
                    mm = pe.matmul(pM[:, slot_of(O_CONV + dt), :], diag[:, dt * KC + k, :], hid[:, dt, k:k + T],
                                   start=(k == 0), stop=(k == KC - 1))
                mm.then_inc(m_filled, 1)

            def x_proj(c, par):
                pe.wait_ge(conv_done, c + 2)
                for i, lo, m in ((O_DTIN, 0, DTR), (O_BC, DTR, 2 * NST)):
                    take(i, unit(c, i))
                    for dt in range(DT):
                        mm = pe.matmul(pM[0:m, slot_of(i), :], w_x[:, dt, lo:lo + m], conv[1 - par][:, dt, :],
                                       start=(dt == 0), stop=(dt == DT - 1))
                    mm.then_inc(m_filled, 1)

            def dt_proj(c):
                pe.wait_ge(m_evac, unit(c, O_BC) + 1)
                take(O_BCT, unit(c, O_BCT))
                pe.sem_inc(pe_passed, 1)
                for tb in range(TB):
                    pe.transpose(pM[:, slot_of(O_BCT + tb), 0:2 * NST], bc[:, tb * P:(tb + 1) * P],
                                 ident[0:2 * NST, 0:2 * NST]).then_inc(m_filled, 1)
                for dt in range(DT):
                    take(O_DT + dt, unit(c, O_DT + dt))
                    pe.matmul(pM[:, slot_of(O_DT + dt), :], w_dt[:, dt * P:(dt + 1) * P], dtin[:, :],
                              start=True, stop=True).then_inc(m_filled, 1)

            def gates(c, dt, par, has_front):
                n = gate_unit(c, dt, has_front)
                take(dt, n)
                for kt in range(KT):
                    mm = pe.matmul(pM[:, slot_of(dt), :], w_in[:, kt, DI + dt * P:DI + (dt + 1) * P], xnT[par][:, kt, :],
                                   start=(kt == 0), stop=(kt == KT - 1))
                mm.then_inc(m_filled, 1)

            def turn_h(c, n):
                for tb in range(TB):
                    i = TB * n + tb
                    if tb == 0:
                        pe.wait_ge(scan_done, c * (NST * DT) + DT * (n + 1))
                    if not (isinstance(c, int) and c == 0 and i < 2):
                        pe.wait_ge(acc_done, c * (NST * TB) + i - 1)
                    for dt in range(DT):
                        mm = pe.transpose(hT[i % 2][:, dt * P:(dt + 1) * P], h[n % 2][:, dt, tb * P:(tb + 1) * P], ident[:, :])
                    mm.then_inc(h_turned, 1)

            def turn_y(c):
                pe.wait_ge(acc_done, c * (NST * TB))
                for j in range(DT // 2):
                    if j >= 2:
                        pe.wait_ge(y_skip, (c - 1) * DT + 2 * (j - 1))
                    for a in range(2):
                        for tb in range(TB):
                            mm = pe.transpose(pX[:, j % 2, a * T + tb * P:a * T + (tb + 1) * P],
                                              acc[:, tb, (2 * j + a) * P:(2 * j + a + 1) * P], ident[:, :])
                    mm.then_inc(y_turned, 1)

            def out_proj(c, tb, par):
                if tb == 0:
                    pe.wait_ge(y_gated, c)
                for dt in range(DT):
                    pe.matmul(pX[:, tb, :], conv[1 - par][:, dt, tb * P:(tb + 1) * P], w_out[:, dt, :],
                              start=(dt == 0), stop=False)
                pe.matmul(pX[:, tb, :], ones[:, :], b_out[:, :], start=False, stop=True).then_inc(out_mm, 1)

            def iteration(c, par, has_back, has_front):
                for n in range(NST):
                    if n:
                        turn_h(c, n - 1)
                    elif has_back:
                        turn_h(c - 1, NST - 1)
                    if has_back and n == 1:
                        turn_y(c)
                    if has_back and n in (3, 4):
                        out_proj(c, n - 3, par)
                    if has_front:
                        if n == 1:
                            for kt in range(KT):
                                xT(c, kt, par)
                        for dt in {1: (0, 1), 2: (2, 3, 4, 5), 5: (6, 7)}.get(n, ()):
                            hidden(c, dt, par)
                        for dt in {6: (0, 1, 2, 3), 7: (4, 5, 6, 7)}.get(n, ()):
                            conv_taps(c, dt)
                        if n == 9:
                            x_proj(c, par)
                        if n == 10:
                            dt_proj(c)
                    for dt in {11: (0, 1), 12: (2, 3), 13: (4, 5), 14: (6, 7)}.get(n, ()):
                        gates(c, dt, par, has_front)

            def front0():
                pe.wait_ge(loaded, 16 * NLOAD)
                for kt in range(KT):
                    xT(-1, kt, 1)
                for dt in range(DT):
                    hidden(-1, dt, 1)
                pe.wait_ge(setup_d, DT * KC)
                for dt in range(DT):
                    conv_taps(-1, dt)
                x_proj(-1, 1)
                dt_proj(-1)

            def epilogue():
                turn_h(NCH - 1, NST - 1)
                turn_y(NCH)
                for tb in range(TB):
                    out_proj(NCH, tb, NCH % 2)

            run(pe, iteration, front0, epilogue)

        @block.scalar
        def _(act):
            def full(i, number):
                act.wait_ge(m_filled, number + (2 if i % 2 == 0 else 1))

            def xT(c, par):
                for kt in range(KT):
                    full(kt, unit(c, O_XT + kt))
                    act.activation(xnT[1 - par][:, kt, :], pM[:, kt, :], ACT.Copy).then_inc(m_evac, 1)

            def hidden(c, dt, par):
                if dt == 0:
                    act.wait_ge(halo_done, c + 2)
                full(O_HID + dt, unit(c, O_HID + dt))
                act.activation(hid[:, dt, HALO:], pM[:, (O_HID + dt) % 4, :], ACT.Identity,
                               bias=b_in[:, dt:dt + 1]).then_inc(m_evac, 1)

            def conv_out(c, dt, par):
                if dt == 0 and not (isinstance(c, int) and c < 1):
                    act.wait_ge(out_mm, TB * c)
                full(O_CONV + dt, unit(c, O_CONV + dt))
                act.activation(conv[1 - par][:, dt, :], pM[:, (O_CONV + dt) % 4, :], ACT.Identity,
                               bias=b_conv[:, dt:dt + 1]).then_inc(m_evac, 1)

            def conv_silu(c, par):
                act.wait_ge(m_evac, unit(c, O_CONV + DT - 1) + 1)
                act.activation(conv[1 - par][:, :, :], conv[1 - par][:, :, :], ACT.Silu).then_inc(conv_done, 1)

            def x_proj(c):
                full(O_DTIN, unit(c, O_DTIN))
                act.activation(dtin[:, :], pM[:, O_DTIN % 4, :], ACT.Copy).then_inc(m_evac, 1)
                full(O_BC, unit(c, O_BC))
                if not (isinstance(c, int) and c < 0):
                    act.wait_ge(bc_stored, 16 * (c + 1))
                act.activation(bc[:, :], pM[0:2 * NST, O_BC % 4, :], ACT.Copy).then_inc(m_evac, 1)

            def dt_proj(c, par):
                for tb in range(TB):
                    full(O_BCT + tb, unit(c, O_BCT + tb))
                    act.activation(bcT[1 - par][:, tb, :], pM[:, (O_BCT + tb) % 4, 0:2 * NST], ACT.Copy).then_inc(m_evac, 1)
                for dt in range(DT):
                    full(O_DT + dt, unit(c, O_DT + dt))
                    act.activation(delta[1 - par][:, dt, :], pM[:, (O_DT + dt) % 4, :], ACT.Identity,
                                   bias=b_dt[:, dt:dt + 1]).then_inc(m_evac, 1)

            def soft_exp(c, par):
                act.wait_ge(m_evac, unit(c, O_DT + DT - 1) + 1)
                act.activation(soft_e, delta[1 - par][:, :, :], ACT.Abs).then_inc(e_done, 1)
                act.wait_ge(e_done, 2 * (c + 1) + 1)
                act.activation(soft_e, soft_e, ACT.Exp, scale=-1.0).then_inc(e_done, 1)

            def soft_ln(c):
                act.wait_ge(q_done, c + 2)
                act.activation(soft_w[:, :, :], soft_w[:, :, :], ACT.Ln).then_inc(ln_done, 1)

            def exps(c, n, par, tiles):
                if n == 0:
                    act.wait_ge(delta_done, c + 1)
                for dt in tiles:
                    i = DT * n + dt
                    if not (isinstance(c, int) and c == 0 and n == 0):
                        act.wait_ge(scan_done, c * (NST * DT) + i - DT + 1)
                    act.activation(da[:, dt, :], delta[par][:, dt, :], ACT.Exp,
                                   scale=a_neg[:, dt, n:n + 1]).then_inc(da_done, 1)

            def gates(c, dt, has_front):
                if dt == 0 and not (isinstance(c, int) and c == 0):
                    act.wait_ge(y_gated, c)
                full(dt, gate_unit(c, dt, has_front))
                act.activation(gate[:, dt, :], pM[:, dt % 4, :], ACT.Identity,
                               bias=b_in[:, DT + dt:DT + dt + 1]).then_inc(m_evac, 1)

            def iteration(c, par, has_back, has_front):
                for n in range(NST):
                    if has_front and n == 14:
                        soft_ln(c)
                    exps(c, n, par, range(DT // 2))
                    if has_front:
                        if n == 2:
                            xT(c, par)
                        for dt in {3: (0, 1), 4: (2, 3, 4, 5), 6: (6, 7)}.get(n, ()):
                            hidden(c, dt, par)
                        for dt in {8: (0, 1, 2, 3), 9: (4, 5, 6, 7)}.get(n, ()):
                            conv_out(c, dt, par)
                        if n == 11:
                            x_proj(c)
                    for dt in {13: (0, 1), 14: (2, 3), 15: (4, 5)}.get(n, ()):
                        gates(c, dt, has_front)
                    exps(c, n, par, range(DT // 2, DT))
                    if has_front:
                        if n == 9:
                            conv_silu(c, par)
                        if n == 12:
                            dt_proj(c, par)
                            soft_exp(c, par)
                for dt in (6, 7):
                    gates(c, dt, has_front)
                act.wait_ge(m_evac, gate_unit(c, DT - 1, has_front) + 1)
                act.activation(gate[:, :, :], gate[:, :, :], ACT.Silu).then_inc(gate_done, 1)

            def front0():
                act.wait_ge(loaded, 16 * NLOAD)
                act.activation(a_neg[:, :, :], a_neg[:, :, :], ACT.Exp).then_inc(setup_a, 1)
                xT(-1, 1)
                for dt in range(DT):
                    hidden(-1, dt, 1)
                for dt in range(DT):
                    conv_out(-1, dt, 1)
                conv_silu(-1, 1)
                x_proj(-1)
                dt_proj(-1, 1)
                soft_exp(-1, 1)
                soft_ln(-1)
                act.wait_ge(setup_d, DT * KC + 1)

            run(act, iteration, front0, lambda: None)

        @block.vector
        def _(dve):
            def norm_stats(c):
                dve.wait_ge(x_in, 16 * (c + 2))
                for tb in range(TB):
                    dve.bn_stats(stats[:, tb, :], xb[:, tb, :]).then_inc(stats_done, 1)
                for tb in range(TB):
                    wait_first(dve, stats_done, TB * (c + 1) + tb + 1, dve_passed)
                    dve.bn_aggr(mv[:, tb, :], stats[:, tb, :]).then_inc(mv_done, 1)

            def norm(c):
                dve.wait_ge(rstd_done, c + 2)
                for tb in range(TB):
                    dve.tensor_scalar(xb[:, tb, :], xb[:, tb, :], mv[:, tb, 0:1], rstd[:, tb:tb + 1],
                                      ALU.subtract, ALU.mult).then_inc(xn_done, 1)

            def halo(c):
                if not (isinstance(c, int) and c < 1):
                    dve.wait_ge(carry_done, c * NST)
                dve.tensor_copy(lim_now[:, :], lim[:, bass.ds(c + 1, 1), :].rearrange("p a b -> p (a b)")).then_inc(lim_done, 1)
                dve.wait_ge(lim_done, c + 2)
                if not (isinstance(c, int) and c < 0):
                    dve.wait_ge(m_evac, unit(c - 1, O_DT + DT - 1) + 1)
                dve.tensor_scalar(hid[:, :, 0:HALO], hid[:, :, T:T + HALO], lim_now[:, 0:1], lim_now[:, 1:2],
                                  ALU.max, ALU.min).then_inc(halo_done, 1)

            def soft_q(c):
                dve.wait_ge(w_done, c + 2)
                dve.scalar_tensor_tensor(soft_e, soft_w[:, :, :], -1.0, soft_e, ALU.add, ALU.subtract).then_inc(q_done, 1)

            def soft_end(c, par):
                dve.wait_ge(ln_done, c + 2)
                dve.tensor_tensor(soft_w[:, :, :], soft_w[:, :, :], soft_e, ALU.subtract).then_inc(lq_done, 1)
                dve.wait_ge(lq_done, c + 2)
                dve.scalar_tensor_tensor(delta[1 - par][:, :, :], delta[1 - par][:, :, :], 0.0, soft_w[:, :, :],
                                         ALU.max, ALU.add).then_inc(delta_done, 1)

            def scans(c, n):
                dve.wait_ge(dbx_done, c * NST + n + 1)
                if not (isinstance(c, int) and c == 0 and n < 2):
                    dve.wait_ge(h_turned, c * (NST * TB) + TB * (n - 1))
                    dve.wait_ge(carry_done, c * NST + n - 1)
                for dt in range(DT):
                    dve.wait_ge(da_done, c * (NST * DT) + DT * n + dt + 1)
                    dve.tensor_tensor_scan(h[n % 2][:, dt, :], da[:, dt, :], dbx[n % 2][:, dt, :],
                                           carry[:, n, dt:dt + 1], ALU.mult, ALU.add).then_inc(scan_done, 1)

            def add_h(c, n, par):
                for tb in range(TB):
                    i = TB * n + tb
                    cn = bcT[par][:, tb, NST + n:NST + n + 1]
                    dve.wait_ge(h_turned, c * (NST * TB) + i + 1)
                    if n == 0:
                        if not (isinstance(c, int) and c == 0):
                            dve.wait_ge(y_turned, (DT // 2) * c)
                        dve.tensor_scalar(acc[:, tb, :], hT[i % 2][:, :], cn, None, ALU.mult).then_inc(acc_done, 1)
                    else:
                        dve.wait_ge(acc_done, c * (NST * TB) + i - TB + 1)
                        dve.scalar_tensor_tensor(acc[:, tb, :], hT[i % 2][:, :], cn, acc[:, tb, :],
                                                 ALU.mult, ALU.add).then_inc(acc_done, 1)

            def skip(c, par):
                for j in range(DT // 2):
                    dve.wait_ge(y_turned, (DT // 2) * (c - 1) + j + 1)
                    for a in range(2):
                        dt = 2 * j + a
                        dve.scalar_tensor_tensor(conv[1 - par][:, dt, :], conv[1 - par][:, dt, :], d_skip[:, dt:dt + 1],
                                                 pX[:, j % 2, a * T:(a + 1) * T], ALU.mult, ALU.add).then_inc(y_skip, 1)

            def out_stats(c, tb):
                dve.wait_ge(out_mm, TB * (c - 1) + tb + 1)
                dve.bn_stats(stats2[:, tb, :], pX[:, tb, :]).then_inc(st2_done, 1)
                wait_first(dve, st2_done, TB * (c - 1) + tb + 1, dve_passed)
                dve.bn_aggr(mv2[:, tb, :], stats2[:, tb, :]).then_inc(mv2_done, 1)

            def out_norm(c):
                dve.wait_ge(rstd2_done, c)
                dve.wait_ge(res_in, 16 * c)
                for tb in range(TB):
                    dve.scalar_tensor_tensor(shift2[:, tb:tb + 1], mv2[:, tb, 0:1], -1.0, rstd2[:, tb:tb + 1],
                                             ALU.mult, ALU.mult).then_inc(shift2_done, 1)
                for tb in range(TB):
                    dve.wait_ge(shift2_done, TB * (c - 1) + tb + 1)
                    dve.tensor_scalar(xb[:, tb, :], xb[:, tb, :], shift2[:, tb:tb + 1], None, ALU.add).then_inc(res_done, 1)
                for tb in range(TB):
                    dve.wait_ge(res_done, TB * (c - 1) + tb + 1)
                    dve.scalar_tensor_tensor(xb[:, tb, :], pX[:, tb, :], rstd2[:, tb:tb + 1], xb[:, tb, :],
                                             ALU.mult, ALU.add).then_inc(z_done, 1)

            def iteration(c, par, has_back, has_front):
                for n in range(NST):
                    if n == 0 and has_front:
                        norm_stats(c)
                    scans(c, n)
                    if n == 0:
                        if has_back:
                            add_h(c - 1, NST - 1, 1 - par)
                        if has_front:
                            halo(c)
                            norm(c)
                    if n == 1 and has_back:
                        skip(c, par)
                    if n:
                        add_h(c, n - 1, par)
                    if has_back and n in (4, 5):
                        out_stats(c, n - 4)
                    if has_back and n == 6:
                        out_norm(c)
                    if has_front and n == 12:
                        soft_q(c)
                    if has_front and n == 13:
                        soft_end(c, par)

            def front0():
                dve.wait_ge(setup_p, 5 + NCH // CPB + 1)
                norm_stats(-1)
                halo(-1)
                norm(-1)
                dve.wait_ge(loaded, 16 * NLOAD)
                for dt in range(DT):
                    for k in range(KC):
                        dve.tensor_scalar(diag[:, dt * KC + k, :], ident[:, :], taps[:, dt, k:k + 1], None,
                                          ALU.mult).then_inc(setup_d, 1)
                dve.wait_ge(setup_a, 1)
                dve.tensor_scalar(a_neg[:, :, :], a_neg[:, :, :], -1.0, None, ALU.mult).then_inc(setup_d, 1)
                soft_q(-1)
                soft_end(-1, 1)

            def epilogue():
                add_h(NCH - 1, NST - 1, (NCH - 1) % 2)
                skip(NCH, NCH % 2)
                for tb in range(TB):
                    out_stats(NCH, tb)
                out_norm(NCH)

            run(dve, iteration, front0, epilogue)

        @block.gpsimd
        def _(pool):
            def rsqrt(c, which):
                m, ve, r, sm, sv, sr = ((mv, veps, rstd, mv_done, veps_done, rstd_done),
                                        (mv2, veps2, rstd2, mv2_done, veps2_done, rstd2_done))[which]
                wait_first(pool, sm, TB * (c + 1), pool_passed)
                pool.tensor_scalar(ve[:, :], m[:, :, 1], EPS, 1.0, ALU.add, ALU.mult).then_inc(sv, 1)
                pool.wait_ge(sv, c + 1)
                pool.tensor_tensor(r[:, :], ve[:, :], half[:, :], ALU.pow).then_inc(sr, 1)

            def b_times_u(c, n, par):
                g = n // NBG
                if n % NBG == 0:
                    pool.wait_ge(bb_in[g % 2], 16 * ((NG // 2) * c + g // 2 + 1))
                if not (isinstance(c, int) and c == 0 and n < 2):
                    pool.wait_ge(scan_done, c * (NST * DT) + DT * (n - 1))
                rows = bb[g % 2][:, n % NBG:n % NBG + 1, :].broadcast_to([P, DT, T])
                pool.tensor_tensor(dbx[n % 2][:, :, :], u[:, :, :], rows, ALU.mult).then_inc(dbx_done, 1)

            def save(c, n):
                wait_first(pool, scan_done, c * (NST * DT) + DT * (n + 1), pool_passed)
                pool.tensor_scalar(carry[:, n, :], h[n % 2][:, :, T - 1], lim_now[:, 0:1], lim_now[:, 1:2],
                                   ALU.max, ALU.min).then_inc(carry_done, 1)

            def one_plus_e(c):
                pool.wait_ge(e_done, 2 * (c + 2))
                wait_first(pool, bc_stored, 16 * (c + 2), pool_passed)
                pool.tensor_scalar(soft_w[:, :, :], soft_e, 1.0, 1.0, ALU.add, ALU.mult).then_inc(w_done, 1)

            def make_u(c, par):
                pool.wait_ge(delta_done, c + 2)
                if not (isinstance(c, int) and c < 0):
                    pool.wait_ge(dbx_done, NST * (c + 1))
                pool.tensor_tensor(u[:, :, :], delta[1 - par][:, :, :], conv[1 - par][:, :, :], ALU.mult).then_inc(u_done, 1)

            def gating(c, par):
                pool.wait_ge(y_skip, DT * c)
                pool.wait_ge(gate_done, c)
                pool.tensor_tensor(conv[1 - par][:, :, :], conv[1 - par][:, :, :], gate[:, :, :], ALU.mult).then_inc(y_gated, 1)

            def iteration(c, par, has_back, has_front):
                pool.wait_ge(u_done, c + 1)
                for n in range(NST):
                    if n == 2 and has_front:
                        pool.wait_ge(lim_done, c + 2)
                    if n >= 2:
                        save(c, n - 2)
                    b_times_u(c, n, par)
                    if n == 1 and has_front:
                        rsqrt(c + 1, 0)
                    if n == 3 and has_back:
                        gating(c, par)
                    if has_back and n == 7:
                        rsqrt(c - 1, 1)
                    if has_front and n == 13:
                        one_plus_e(c)
                for n in (NST - 2, NST - 1):
                    save(c, n)
                    if n == NST - 2 and has_front:
                        make_u(c, par)

            def front0():
                pool.memset(hid[:, :, :], 0.0).then_inc(setup_p, 1)
                pool.memset(carry[:, :, :], 0.0).then_inc(setup_p, 1)
                pool.memset(half[:, :], -0.5).then_inc(setup_p, 1)
                pool.memset(lim[:, :, 0:1], -BIG).then_inc(setup_p, 1)
                pool.memset(lim[:, :, 1:2], BIG).then_inc(setup_p, 1)
                pool.wait_ge(setup_p, 5)
                for c in range(0, NCH + 1, CPB):
                    pool.memset(lim[:, c, :], 0.0).then_inc(setup_p, 1)
                rsqrt(0, 0)
                one_plus_e(-1)
                make_u(-1, 1)

            def epilogue():
                gating(NCH, NCH % 2)
                rsqrt(NCH - 1, 1)

            run(pool, iteration, front0, epilogue)


HT = FF // P
T2 = 512
TB2 = T2 // P
NCH2 = TOK // T2
HALVES = 2
FH = FF // HALVES
FT = FH // P


def hadamard_block(nc, W, scratch_w):
    ctx = ExitStack()
    with ctx:
        def sb(name, shape, dt=F32):
            return ctx.enter_context(nc.sbuf_tensor(name, shape, dt))

        def sem(name):
            return ctx.enter_context(nc.semaphore(name))

        TILES = 16
        JOBS = (("up", (4, 8)), ("gate", (4, 8)), ("down", (1, 2, 4, 8)))
        buf = [sb(f"had{i}", [P, TILES, DM]) for i in range(5)]
        scaled = [sb(f"scaled{i}", [P, DM]) for i in range(2)]
        h128 = sb("h128", [P, P])
        su_ug = sb("su_ug", [P, KT])
        su_dp = sb("su_dp", [P, HT])
        wscale = sb("wscale", [P, DM])
        ps = [ctx.enter_context(nc.psum_tensor(f"had_ps{i}", [P, DM], F32)) for i in range(4)]
        w_in = [sem(f"hw_in{i}") for i in range(len(JOBS))]
        small_in = sem("small_in")
        su_done = sem("su_done")
        plus_done = sem("plus_done")
        minus_done = sem("minus_done")
        rows_scaled = sem("rows_scaled")
        mm_done = sem("mm_done")
        evac = sem("had_evac")
        stored = [sem("had_stored0"), sem("had_stored1")]
        plan = []
        for j, (name, strides) in enumerate(JOBS):
            chain = [j]
            for s in range(len(strides)):
                chain.append(3 if s % 2 == 0 else j)
            plan.append(chain)
        before = [sum(len(s) for _, s in JOBS[:j]) for j in range(len(JOBS) + 1)]
        CUT = 3
        block = ctx.enter_context(nc.Block())

        def halves(t, stride):
            v = t[:, :, :].rearrange("p (g two s) m -> p g two (s m)", two=2, s=stride)
            return v[:, :, 0, :], v[:, :, 1, :]

        @block.sync
        def _(sp):
            for dst, src in ((h128[:, :], W["h128"]), (su_ug[:, :], W["SU_ug"]), (su_dp[:, :], W["SU_dp"]),
                             (wscale[:, :], W["Wscale_dp"].rearrange("(a n) -> a n", a=1).broadcast_to([P, DM]))):
                sp.dma_start(dst, src).then_inc(small_in, 16)
            for j, name in enumerate(("W_up", "W_gate")):
                sp.dma_start(buf[j][:, :, :].rearrange("p (k q) m -> p k (q m)", k=KT),
                             W[name].rearrange("(k p) f -> p k f", p=P)).then_inc(w_in[j], 16)
            sp.dma_start(buf[2][:, :, :], W["W_down"].rearrange("(k p) m -> p k m", p=P)).then_inc(w_in[2], 16)
            for i in range(len(JOBS) * TILES):
                j, t = divmod(i, TILES)
                sp.wait_ge(evac, i + 1)
                if j < 2:
                    dst = scratch_w[j][(t // 4) * P:(t // 4 + 1) * P, (t % 4) * DM:(t % 4 + 1) * DM]
                else:
                    dst = scratch_w[j][t * P:(t + 1) * P, :]
                sp.dma_start(dst, scaled[i % 2][:, :]).then_inc(stored[i % 2], 16)
            for i in range(2):
                sp.wait_ge(stored[i], 16 * len(JOBS) * TILES // 2)

        def butterflies(eng, j, s, mine):
            stride = JOBS[j][1][s]
            src, dst = buf[plan[j][s]], buf[plan[j][s + 1]]
            if s == 0:
                eng.wait_ge(w_in[j], 16)
                if j:
                    eng.wait_ge(mm_done, TILES * j)
                if j == 2:
                    eng.wait_ge(rows_scaled, 1)
            done = before[j] + s
            if done:
                eng.wait_ge(plus_done, done)
                eng.wait_ge(minus_done, done)
            (s0, s1), (d0, d1) = halves(src, stride), halves(dst, stride)
            cut = stride * DM * CUT // 8
            if mine == "plus":
                eng.tensor_tensor(d0, s0, s1, ALU.add)
                eng.tensor_tensor(d1[:, :, 0:cut], s0[:, :, 0:cut], s1[:, :, 0:cut], ALU.subtract).then_inc(plus_done, 1)
            else:
                eng.tensor_tensor(d1[:, :, cut:], s0[:, :, cut:], s1[:, :, cut:], ALU.subtract).then_inc(minus_done, 1)

        @block.vector
        def _(dve):
            dve.wait_ge(small_in, 64)
            dve.tensor_scalar(su_ug[:, :], su_ug[:, :], float(DM) ** -0.5, None, ALU.mult).then_inc(su_done, 1)
            dve.tensor_scalar(su_dp[:, :], su_dp[:, :], float(FF) ** -0.5, None, ALU.mult).then_inc(su_done, 1)
            for j in range(len(JOBS)):
                if j == 2:
                    dve.wait_ge(w_in[2], 16)
                    dve.tensor_tensor(buf[2][:, :, :], buf[2][:, :, :],
                                      wscale[:, :].rearrange("p (a m) -> p a m", a=1).broadcast_to([P, TILES, DM]),
                                      ALU.mult).then_inc(rows_scaled, 1)
                for s in range(len(JOBS[j][1])):
                    butterflies(dve, j, s, "plus")

        @block.gpsimd
        def _(pool):
            for j in range(len(JOBS)):
                for s in range(len(JOBS[j][1])):
                    butterflies(pool, j, s, "minus")

        @block.tensor
        def _(pe):
            pe.wait_ge(small_in, 64)
            for i in range(len(JOBS) * TILES):
                j, t = divmod(i, TILES)
                if t == 0:
                    pe.wait_ge(plus_done, before[j + 1])
                    pe.wait_ge(minus_done, before[j + 1])
                if i >= 4:
                    pe.wait_ge(evac, i - 3)
                pe.matmul(ps[i % 4][:, :], h128[:, :], buf[plan[j][-1]][:, t, :], start=True, stop=True).then_inc(mm_done, 1)

        @block.scalar
        def _(act):
            act.wait_ge(su_done, 2)
            for i in range(len(JOBS) * TILES):
                j, t = divmod(i, TILES)
                act.wait_ge(mm_done, i + 1)
                if i >= 2:
                    act.wait_ge(stored[i % 2], 16 * (i // 2))
                scale = su_ug[:, t // 4:t // 4 + 1] if j < 2 else su_dp[:, t:t + 1]
                act.activation(scaled[i % 2][:, :], ps[i % 4][:, :], ACT.Copy, scale=scale).then_inc(evac, 1)


def ffn_block(nc, x2, W, scratch_w, scratch_part, out):
    ctx = ExitStack()
    with ctx:
        def sb(name, shape, dt=F32):
            return ctx.enter_context(nc.sbuf_tensor(name, shape, dt))

        def pb(name):
            return ctx.enter_context(nc.psum_tensor(name, [P, T2], F32))

        def sem(name):
            return ctx.enter_context(nc.semaphore(name))

        wug = [sb(f"wug_{s}", [P, KT, 2 * FH], F32R) for s in ("hi", "lo")]
        wd = [sb(f"wd_{s}", [P, FT, DM], F32R) for s in ("hi", "lo")]
        stage = [sb(f"stage{i}", [P, FH]) for i in range(2)]
        xs = sb("xs", [P, TB2, DM])
        xT = [sb(f"xT_{s}", [P, KT, T2], F32R) for s in ("hi", "lo")]
        prod = [sb(f"prod_{s}", [P, FT, T2], F32R) for s in ("hi", "lo")]
        s_gate = [sb(f"s_gate{i}", [P, T2]) for i in range(2)]
        p = [sb(f"p{i}", [P, T2]) for i in range(2)]
        part = sb("part", [P, TB2, DM])
        res = sb("res", [P, TB2, DM])
        ident = sb("ident2", [P, P])
        scale_ug = sb("scale_ug", [P, 2 * HT])
        half = sb("half2", [P, TB2])
        stats, mv, veps, rstd = (sb(n, [P, TB2, k]) for n, k in (("fst", 6), ("fmv", 2), ("fve", 1), ("frs", 1)))
        ostats, omv, oveps, orstd = (sb(n, [P, TB2, k]) for n, k in (("ost", 6), ("omv", 2), ("ove", 1), ("ors", 1)))
        pT = [pb(f"pT{i}") for i in range(2)]
        pg = [pb(f"pg{i}") for i in range(2)]
        pu = [pb(f"pu{i}") for i in range(2)]
        po = [pb(f"po{i}") for i in range(2)]

        small_in = sem("f_small_in"); half_set = sem("half_set")
        stage_in = [sem("stage_in0"), sem("stage_in1")]
        w_hi = sem("w_hi"); w_lo = sem("w_lo")
        xs_in = sem("xs_in"); res_in = sem("f_res_in"); part_in = sem("part_in")
        st_done = sem("f_st"); mv_done = sem("f_mv"); veps_done = sem("f_veps"); rstd_done = sem("f_rstd"); xn_done = sem("f_xn")
        xT_filled = sem("xT_filled"); x_hi = sem("x_hi"); x_lo = sem("x_lo")
        gate_mm = sem("gate_mm"); up_mm = sem("up_mm"); silu_done = sem("silu_done"); p_done = sem("p_done")
        p_hi = sem("p_hi"); p_lo = sem("p_lo")
        down_mm = sem("down_mm"); o_evac = sem("o_evac"); part_stored = sem("part_stored")
        ost_done = sem("o_st"); omv_done = sem("o_mv"); oveps_done = sem("o_veps"); orstd_done = sem("o_rstd")
        sp_passed, dve_passed, pool_passed = (sem(f"f_{e}_passed") for e in ("sp", "dve", "pool"))
        o_normed = sem("o_normed"); o_done = sem("o_done"); out_stored = sem("out_stored")

        PIECES = 2 * KT + FT // 2

        def piece(half_no, q):
            if q < 2 * KT:
                kt, which = divmod(q, 2)
                src = scratch_w[which][kt * P:(kt + 1) * P, half_no * FH:(half_no + 1) * FH]
                return src, lambda s: wug[s][:, kt, which * FH:(which + 1) * FH]
            ft = 2 * (q - 2 * KT)
            src = scratch_w[2][half_no * FH + ft * P:half_no * FH + (ft + 2) * P, :].rearrange("(a p) m -> p a m", p=P)
            return src, lambda s: wd[s][:, ft:ft + 2, :].rearrange("p a m -> p (a m)")

        def run(eng, weights, first_front, step):
            for half_no in range(HALVES):
                weights(half_no)
                first_front(half_no * NCH2)
                step(half_no, 0, half_no * NCH2, True)
                with eng.Fori(1, NCH2 - 1) as ck:
                    step(half_no, ck, half_no * NCH2, True)
                step(half_no, NCH2 - 1, half_no * NCH2, False)

        def nothing(*_):
            return None

        block = ctx.enter_context(nc.Block())

        @block.sync
        def _(sp):
            sp.dma_start(ident[:, :], W["ident"]).then_inc(small_in, 16)
            sp.dma_start(scale_ug[:, :], W["Wscale_ug"]).then_inc(small_in, 16)

            def load_xs(chunk, step_no):
                if not (isinstance(step_no, int) and step_no == 0):
                    wait_first(sp, xT_filled, KT * step_no, sp_passed)
                sp.dma_start(xs[:, :, :], x2[bass.ds(chunk, 1), :, :].rearrange("c (a p) m -> p (c a) m", p=P)).then_inc(xs_in, 16)

            def step(half_no, ck, base, more):
                i = ck + base
                if more:
                    load_xs(ck + 1, i + 1)
                rows = lambda t: t[bass.ds(ck, 1), :, :].rearrange("c (a p) m -> p (c a) m", p=P)
                if half_no == 0:
                    wait_first(sp, o_evac, TB2 * (i + 1), sp_passed)
                    sp.dma_start(rows(scratch_part), part[:, :, :]).then_inc(part_stored, 16)
                else:
                    if not (isinstance(ck, int) and ck == 0):
                        wait_first(sp, o_normed, TB2 * ck, sp_passed)
                        wait_first(sp, out_stored, 16 * ck, sp_passed)
                    sp.dma_start(part[:, :, :], rows(scratch_part)).then_inc(part_in, 16)
                    sp.dma_start(res[:, :, :], rows(x2)).then_inc(res_in, 16)
                    wait_first(sp, o_done, TB2 * (ck + 1), sp_passed)
                    sp.dma_start(rows(out), res[:, :, :]).then_inc(out_stored, 16)

            def between(half_no):
                if half_no:
                    wait_first(sp, part_stored, 16 * NCH2, sp_passed)

            run(sp, between, lambda base: load_xs(0, base), step)
            wait_first(sp, out_stored, 16 * NCH2, sp_passed)

        @block.gpsimd
        def _(pool):
            pool.memset(half[:, :], -0.5).then_inc(half_set, 1)
            pool.wait_ge(half_set, 1)

            def weights(half_no):
                for q in range(PIECES):
                    n = half_no * PIECES + q
                    if n >= 2:
                        pool.wait_ge(w_lo, n - 1)
                    src, _ = piece(half_no, q)
                    dst = stage[q % 2][:, :] if q < 2 * KT else stage[q % 2][:, :].rearrange("p (a m) -> p a m", a=2)
                    pool.dma_start(dst, src).then_inc(stage_in[q % 2], 16)

            def rsqrt(count, m, ve, r, m_sem, v_sem, r_sem):
                wait_first(pool, m_sem, TB2 * count, pool_passed)
                pool.tensor_scalar(ve[:, :, 0], m[:, :, 1], EPS, 1.0, ALU.add, ALU.mult).then_inc(v_sem, 1)
                pool.wait_ge(v_sem, count)
                pool.tensor_tensor(r[:, :, 0], ve[:, :, 0], half[:, :], ALU.pow).then_inc(r_sem, 1)

            def front(step_no):
                rsqrt(step_no + 1, mv, veps, rstd, mv_done, veps_done, rstd_done)

            def step(half_no, ck, base, more):
                if more:
                    front(ck + base + 1)
                if half_no:
                    rsqrt(ck + 1, omv, oveps, orstd, omv_done, oveps_done, orstd_done)

            run(pool, weights, front, step)

        @block.tensor
        def _(pe):
            pe.wait_ge(small_in, 32)

            def front(step_no):
                pe.wait_ge(xn_done, TB2 * (step_no + 1))
                for kt in range(KT):
                    if kt >= 2:
                        pe.wait_ge(x_lo, KT * step_no + kt - 1)
                    for tb in range(TB2):
                        mm = pe.transpose(pT[kt % 2][:, tb * P:(tb + 1) * P], xs[:, tb, kt * P:(kt + 1) * P], ident[:, :])
                    mm.then_inc(xT_filled, 1)

            PASSES = ((0, 0), (0, 1), (1, 0))

            def step(half_no, ck, base, more):
                i = ck + base
                pe.wait_ge(x_lo, KT * (i + 1))
                for ft in range(FT):
                    for bank, which, freed, filled in ((pg, 1, silu_done, gate_mm), (pu, 0, p_done, up_mm)):
                        if ft >= 2:
                            pe.wait_ge(freed, FT * i + ft - 1)
                        for kt in range(KT):
                            for n, (a, b) in enumerate(PASSES):
                                lo = which * FH + ft * P
                                mm = pe.matmul(bank[ft % 2][:, :], wug[a][:, kt, lo:lo + P], xT[b][:, kt, :],
                                               start=(kt == 0 and n == 0), stop=(kt == KT - 1 and n == len(PASSES) - 1))
                        mm.then_inc(filled, 1)
                if more:
                    front(i + 1)
                pe.wait_ge(p_lo, FT * (i + 1))
                for tb in range(TB2):
                    if tb == 0 and not (isinstance(i, int) and i == 0):
                        pe.wait_ge(o_evac, TB2 * i)
                    elif tb >= 2:
                        pe.wait_ge(o_evac, TB2 * i + tb - 1)
                    for ft in range(FT):
                        for n, (a, b) in enumerate(PASSES):
                            mm = pe.matmul(po[tb % 2][:, :], prod[a][:, ft, tb * P:(tb + 1) * P], wd[b][:, ft, :],
                                           start=(ft == 0 and n == 0), stop=(ft == FT - 1 and n == len(PASSES) - 1))
                    mm.then_inc(down_mm, 1)

            run(pe, lambda half_no: pe.wait_ge(w_lo, PIECES * (half_no + 1)), front, step)

        @block.scalar
        def _(act):
            act.wait_ge(small_in, 32)

            def weights(half_no):
                for q in range(PIECES):
                    act.wait_ge(stage_in[q % 2], 16 * (half_no * PIECES // 2 + q // 2 + 1))
                    if half_no and q == 0:
                        act.wait_ge(up_mm, NCH2 * FT)
                    if half_no and q == 2 * KT:
                        act.wait_ge(down_mm, NCH2 * TB2)
                    _, dst = piece(half_no, q)
                    act.activation(dst(0), stage[q % 2][:, :], ACT.Copy).then_inc(w_hi, 1)

            def front(step_no):
                for kt in range(KT):
                    act.wait_ge(xT_filled, KT * step_no + kt + 1)
                    act.activation(xT[0][:, kt, :], pT[kt % 2][:, :], ACT.Copy).then_inc(x_hi, 1)

            def step(half_no, ck, base, more):
                i = ck + base
                for ft in range(FT):
                    f = half_no * FT + ft
                    act.wait_ge(gate_mm, FT * i + ft + 1)
                    if ft >= 2:
                        act.wait_ge(p_done, FT * i + ft - 1)
                    act.activation(s_gate[ft % 2][:, :], pg[ft % 2][:, :], ACT.Silu,
                                   scale=scale_ug[:, HT + f:HT + f + 1]).then_inc(silu_done, 1)
                    act.wait_ge(p_done, FT * i + ft + 1)
                    if ft == 0 and not (isinstance(i, int) and i == 0):
                        act.wait_ge(down_mm, TB2 * i)
                    act.activation(prod[0][:, ft, :], p[ft % 2][:, :], ACT.Copy).then_inc(p_hi, 1)
                if more:
                    front(i + 1)
                if half_no == 0:
                    for tb in range(TB2):
                        act.wait_ge(down_mm, TB2 * i + tb + 1)
                        if tb == 0 and not (isinstance(i, int) and i == 0):
                            act.wait_ge(part_stored, 16 * i)
                        act.activation(part[:, tb, :], po[tb % 2][:, :], ACT.Copy).then_inc(o_evac, 1)

            run(act, weights, front, step)

        @block.vector
        def _(dve):
            dve.wait_ge(small_in, 32)

            def weights(half_no):
                for q in range(PIECES):
                    dve.wait_ge(w_hi, half_no * PIECES + q + 1)
                    _, dst = piece(half_no, q)
                    dve.tensor_tensor(dst(1), stage[q % 2][:, :], dst(0).bitcast(F32), ALU.subtract).then_inc(w_lo, 1)

            def norm_stats(step_no):
                dve.wait_ge(xs_in, 16 * (step_no + 1))
                for tb in range(TB2):
                    dve.bn_stats(stats[:, tb, :], xs[:, tb, :]).then_inc(st_done, 1)
                for tb in range(TB2):
                    wait_first(dve, st_done, TB2 * step_no + tb + 1, dve_passed)
                    dve.bn_aggr(mv[:, tb, :], stats[:, tb, :]).then_inc(mv_done, 1)

            def norm(step_no):
                dve.wait_ge(rstd_done, step_no + 1)
                for tb in range(TB2):
                    dve.tensor_scalar(xs[:, tb, :], xs[:, tb, :], mv[:, tb, 0:1], rstd[:, tb, :],
                                      ALU.subtract, ALU.mult).then_inc(xn_done, 1)

            def split_x(step_no):
                for kt in range(KT):
                    dve.wait_ge(x_hi, KT * step_no + kt + 1)
                    dve.tensor_tensor(xT[1][:, kt, :], pT[kt % 2][:, :], xT[0][:, kt, :].bitcast(F32),
                                      ALU.subtract).then_inc(x_lo, 1)

            def front(step_no):
                norm_stats(step_no)
                norm(step_no)
                split_x(step_no)

            def step(half_no, ck, base, more):
                i = ck + base
                for ft in range(FT):
                    f = half_no * FT + ft
                    dve.wait_ge(silu_done, FT * i + ft + 1)
                    dve.wait_ge(up_mm, FT * i + ft + 1)
                    if ft >= 2:
                        dve.wait_ge(p_lo, FT * i + ft - 1)
                    dve.scalar_tensor_tensor(p[ft % 2][:, :], pu[ft % 2][:, :], scale_ug[:, f:f + 1], s_gate[ft % 2][:, :],
                                             ALU.mult, ALU.mult).then_inc(p_done, 1)
                    dve.wait_ge(p_hi, FT * i + ft + 1)
                    dve.tensor_tensor(prod[1][:, ft, :], p[ft % 2][:, :], prod[0][:, ft, :].bitcast(F32),
                                      ALU.subtract).then_inc(p_lo, 1)
                    if more and ft == 2:
                        norm_stats(i + 1)
                    if more and ft == 4:
                        norm(i + 1)
                if more:
                    split_x(i + 1)
                if half_no:
                    for tb in range(TB2):
                        if tb == 0:
                            dve.wait_ge(part_in, 16 * (ck + 1))
                        dve.wait_ge(down_mm, TB2 * i + tb + 1)
                        dve.tensor_tensor(part[:, tb, :], po[tb % 2][:, :], part[:, tb, :], ALU.add).then_inc(o_evac, 1)
                        dve.wait_ge(o_evac, TB2 * i + tb + 1)
                        dve.bn_stats(ostats[:, tb, :], part[:, tb, :]).then_inc(ost_done, 1)
                        wait_first(dve, ost_done, TB2 * ck + tb + 1, dve_passed)
                        dve.bn_aggr(omv[:, tb, :], ostats[:, tb, :]).then_inc(omv_done, 1)
                    dve.wait_ge(orstd_done, ck + 1)
                    dve.wait_ge(res_in, 16 * (ck + 1))
                    for tb in range(TB2):
                        dve.tensor_scalar(part[:, tb, :], part[:, tb, :], omv[:, tb, 0:1], orstd[:, tb, :],
                                          ALU.subtract, ALU.mult).then_inc(o_normed, 1)
                    for tb in range(TB2):
                        dve.wait_ge(o_normed, TB2 * ck + tb + 1)
                        dve.tensor_tensor(res[:, tb, :], res[:, tb, :], part[:, tb, :], ALU.add).then_inc(o_done, 1)

            run(dve, weights, front, step)


_INS = ['L0_attn_hidden_states', 'L0_attn_W_in', 'L0_attn_b_in', 'L0_attn_conv_w', 'L0_attn_conv_b', 'L0_attn_W_x',
        'L0_attn_W_dt', 'L0_attn_b_dt', 'L0_attn_W_out', 'L0_attn_b_out', 'L0_attn_a_log', 'L0_attn_d_param',
        'L0_ffn_SU_ug', 'L0_ffn_SU_dp', 'L0_ffn_Wscale_ug', 'L0_ffn_Wscale_dp', 'L0_ffn_W_up', 'L0_ffn_W_gate',
        'L0_ffn_W_down']


def kernel(**inputs):
    import numpy as np
    import concourse.bacc as bacc
    from concourse.bass_utils import run_bass_kernel_spmd

    nc = bacc.Bacc("TRN2", target_bir_lowering=False, num_devices=1)
    arrays, W = {}, {}

    def give(name, a):
        a = np.ascontiguousarray(a)
        arrays[f"in_{name}"] = a
        W[name] = nc.dram_tensor(f"in_{name}", a.shape, mybir.dt.from_np(a.dtype), kind="ExternalInput").ap()

    by_partition = ("b_in", "conv_b", "b_dt", "d_param", "SU_ug", "SU_dp", "Wscale_ug")
    for name in _INS:
        short = name.replace("L0_attn_", "").replace("L0_ffn_", "")
        a = np.asarray(inputs[name])
        if short == "conv_w":
            a = a.reshape(KC, DT, P).transpose(2, 1, 0)
        elif short == "a_log":
            a = a.reshape(DT, P, NST).transpose(1, 0, 2)
        elif short in ("W_up", "W_gate", "W_down"):
            a = a.T
        elif short in by_partition:
            a = a.reshape(-1, P).T
        give(short, a)
    give("ident", np.eye(P, dtype=np.float32))
    h = np.ones((1, 1), np.float32)
    while len(h) < P:
        h = np.block([[h, h], [h, -h]])
    give("h128", h)
    give("ones", np.ones((1, P), np.float32))
    out = nc.dram_tensor("out", (TOK, DM), F32, kind="ExternalOutput").ap()
    scratch_bc = nc.dram_tensor("scratch_bc", (NCH, 2 * NST, T), F32, kind="Internal").ap()
    x = W["hidden_states"].rearrange("b l m -> (b l) m").rearrange("(c t) m -> c t m", t=T)
    x2 = nc.dram_tensor("scratch_x2", (TOK, DM), F32, kind="Internal").ap()
    scratch_w = [nc.dram_tensor(f"scratch_w_{n}", shape, F32, kind="Internal").ap()
                 for n, shape in (("up", (DM, FF)), ("gate", (DM, FF)), ("down", (FF, DM)))]
    scratch_part = nc.dram_tensor("scratch_part", (NCH2, T2, DM), F32, kind="Internal").ap()
    hadamard_block(nc, W, scratch_w)
    mamba_block(nc, x, W, scratch_bc, x2.rearrange("(c t) m -> c t m", t=T))
    ffn_block(nc, x2.rearrange("(c t) m -> c t m", t=T2), W, scratch_w, scratch_part,
              out.rearrange("(c t) m -> c t m", t=T2))
    r = run_bass_kernel_spmd(nc, [arrays], core_ids=[0])
    return r.results[0]["out"].reshape(BATCH, SEQ, DM)
```

```python
import concourse.bass as bass
from concourse import mybir
from contextlib import ExitStack

F32 = mybir.dt.float32
F32R = mybir.dt.float32r
ALU = mybir.AluOpType
ACT = mybir.ActivationFunctionType

P = 128
DM, DI, NST, DTR, KC = 512, 1024, 16, 128, 4
FF = 2048
BATCH, SEQ = 4, 1024
TOK = BATCH * SEQ
EPS = 1e-5
BIG = 3.0e38

T = 256
TB = T // P
NCH = TOK // T
CPB = SEQ // T
KT = DM // P
DT = DI // P
HALO = KC - 1


def wait_first(eng, sem, value, passed):
    eng.wait_ge(sem, value)
    eng.sem_inc(passed, 1)


def mamba_block(nc, x, W, scratch_bc, x2):
    ctx = ExitStack()
    with ctx:
        def sb(name, shape, dt=F32):
            return ctx.enter_context(nc.sbuf_tensor(name, shape, dt))

        def pb(name, shape):
            return ctx.enter_context(nc.psum_tensor(name, shape, F32))

        def sem(name):
            return ctx.enter_context(nc.semaphore(name))

        w_in = sb("w_in", [P, KT, 2 * DI])
        w_x = sb("w_x", [P, DT, DTR + 2 * NST])
        w_dt = sb("w_dt", [P, DI])
        w_out = sb("w_out", [P, DT, DM])
        taps = sb("taps", [P, DT, KC])
        diag = sb("diag", [P, DT * KC, P])
        ident = sb("ident", [P, P])
        b_in = sb("b_in", [P, 2 * DT])
        b_conv = sb("b_conv", [P, DT])
        b_dt = sb("b_dt", [P, DT])
        d_skip = sb("d_skip", [P, DT])
        b_out = sb("b_out", [1, DM])
        ones = sb("ones", [1, P])
        a_neg = sb("a_neg", [P, DT, NST])
        lim = sb("lim", [P, NCH + 1, 2])
        lim_now = sb("lim_now", [P, 2])
        half = sb("half", [P, TB])
        xb = sb("xb", [P, TB, DM])
        stats = sb("stats", [P, TB, 6])
        mv = sb("mv", [P, TB, 2])
        veps = sb("veps", [P, TB])
        rstd = sb("rstd", [P, TB])
        stats2 = sb("stats2", [P, TB, 6])
        mv2 = sb("mv2", [P, TB, 2])
        veps2 = sb("veps2", [P, TB])
        rstd2 = sb("rstd2", [P, TB])
        shift2 = sb("shift2", [P, TB])
        xnT = [sb(f"xnT{i}", [P, KT, T]) for i in range(2)]
        hid = sb("hid", [P, DT, HALO + T])
        soft_e = hid[:, :, 0:T]
        soft_w = sb("soft_w", [P, DT, T])
        conv = [sb(f"conv{i}", [P, DT, T]) for i in range(2)]
        delta = [sb(f"delta{i}", [P, DT, T]) for i in range(2)]
        gate = sb("gate", [P, DT, T])
        u = sb("u", [P, DT, T])
        dtin = soft_w[:, 0, :]
        bc = soft_w[0:TB * 2 * NST, 1, 0:P]
        bcT = [sb(f"bcT{i}", [P, P // (2 * NST), 2 * NST]) for i in range(2)]
        NBG = 2
        NG = NST // NBG
        bb = [sb(f"bb{i}", [P, NBG, T]) for i in range(2)]
        dbx = [sb(f"dbx{i}", [P, DT, T]) for i in range(2)]
        h = [sb(f"h{i}", [P, DT, T]) for i in range(2)]
        da = sb("da", [P, DT, T])
        carry = sb("carry", [P, NST, DT])
        da0 = sb("da0", [P, NST, DT])
        acc = sb("acc", [P, TB, DI])

        hT = [pb(f"hT{i}", [P, DI]) for i in range(2)]
        pM = pb("pM", [P, 4, T])
        pX = pb("pX", [P, 2, DM])

        loaded = sem("loaded"); setup_d = sem("setup_d"); setup_p = sem("setup_p"); setup_a = sem("setup_a")
        x_in = sem("x_in"); res_in = sem("res_in"); x2_stored = sem("x2_stored")
        stats_done = sem("stats_done"); mv_done = sem("mv_done"); veps_done = sem("veps_done")
        rstd_done = sem("rstd_done"); xn_done = sem("xn_done")
        halo_done = sem("halo_done"); lim_done = sem("lim_done")
        m_filled = sem("m_filled"); m_evac = sem("m_evac")
        conv_done = sem("conv_done"); gate_done = sem("gate_done")
        bc_stored = sem("bc_stored")
        bb_in = [sem("bb_in0"), sem("bb_in1")]
        e_done = sem("e_done"); w_done = sem("w_done"); q_done = sem("q_done"); ln_done = sem("ln_done")
        lq_done = sem("lq_done"); delta_done = sem("delta_done"); u_done = sem("u_done")
        da_done = sem("da_done"); da0_raw = sem("da0_raw"); da0_done = sem("da0_done"); inject_done = sem("inject_done"); prod_done = sem("prod_done"); dbx_done = sem("dbx_done"); scan_done = sem("scan_done")
        carry_done = sem("carry_done"); h_turned = sem("h_turned"); acc_done = sem("acc_done")
        y_turned = sem("y_turned"); y_skip = sem("y_skip"); y_gated = sem("y_gated"); out_mm = sem("out_mm")
        st2_done = sem("st2_done"); mv2_done = sem("mv2_done"); veps2_done = sem("veps2_done")
        rstd2_done = sem("rstd2_done"); shift2_done = sem("shift2_done"); res_done = sem("res_done")
        z_done = sem("z_done")
        NLOAD = 13
        sp_passed, pe_passed, dve_passed, pool_passed = (sem(f"{e}_passed") for e in ("sp", "pe", "dve", "pool"))

        FRONT_UNITS = ["xT"] * KT + ["hid"] * DT + ["conv"] * DT + ["dtin", "bcT"] + ["bc"] * TB + ["dt"] * DT
        U_FRONT, U_ALL = len(FRONT_UNITS), len(FRONT_UNITS) + DT
        assert U_FRONT % 4 == 0 and U_ALL % 4 == 0
        O_XT, O_HID, O_CONV = 0, KT, KT + DT
        O_DTIN = O_CONV + DT
        O_BCT = O_DTIN + 1
        O_BC = O_BCT + 1
        O_DT = O_BC + TB
        O_GATE = U_FRONT

        def unit(c, i):
            if isinstance(c, int) and c < 0:
                return i
            return c * U_ALL + (U_FRONT + i)

        def gate_unit(c, i, has_front):
            return unit(c, i + (O_GATE if has_front else 0))

        PE_GATES = {12: (0, 1), 13: (2, 3), 14: (4, 5)}
        PE_GATES_LATE = {0: (6, 7)}
        PE_HID = {2: (0, 1, 2), 3: (3, 4, 5), 4: (6, 7)}
        PE_CONV = {5: (0, 1), 6: (2, 3), 7: (4, 5), 8: (6, 7)}
        PE_OUT = {4: (0, 1), 5: (2, 3), 6: (4, 5), 7: (6, 7), 8: (8, 9), 9: range(10, 15), 11: range(15, 18)}
        OUT_FIRST = (5, 11)
        ACT_HID_MID = {4: (0, 1), 5: (4, 5), 6: (6, 7)}
        ACT_HID_END = {4: (2, 3)}
        ACT_CONV = {7: (0, 1), 8: (2, 3), 9: (4, 5), 10: (6, 7)}
        block = ctx.enter_context(nc.Block())

        def schedule(iteration, front0, epilogue):
            front0()
            iteration(0, 0, False, True)

            def pair(p):
                for j in range(2):
                    iteration(2 * p + (1 + j), (1 + j) % 2, True, True)
            return pair, lambda: (iteration(NCH - 1, (NCH - 1) % 2, True, False), epilogue())

        def run(eng, iteration, front0, epilogue):
            pair, finish = schedule(iteration, front0, epilogue)
            with eng.Fori(0, (NCH - 2) // 2) as p:
                pair(p)
            finish()

        @block.sync
        def _(sp):
            sp.dma_start(xb[:, :, :], x[0, :, :].rearrange("(a p) m -> p a m", p=P)).then_inc(x_in, 16)
            sp.dma_start(w_in[:, :, :], W["W_in"].rearrange("(k p) n -> p k n", p=P)).then_inc(loaded, 16)
            for dst, name in ((taps[:, :, :], "conv_w"), (b_in[:, :], "b_in"), (b_conv[:, :], "conv_b"),
                              (b_dt[:, :], "b_dt"), (d_skip[:, :], "d_param"), (a_neg[:, :, :], "a_log")):
                sp.dma_start(dst, W[name]).then_inc(loaded, 16)
            sp.dma_start(ident[:, :], W["ident"]).then_inc(loaded, 16)
            sp.dma_start(w_x[:, :, :], W["W_x"].rearrange("(k p) n -> p k n", p=P)).then_inc(loaded, 16)
            sp.dma_start(w_dt[:, :], W["W_dt"]).then_inc(loaded, 16)
            sp.dma_start(w_out[:, :, :], W["W_out"].rearrange("(k p) n -> p k n", p=P)).then_inc(loaded, 16)
            sp.dma_start(b_out[:, :], W["b_out"].rearrange("(a n) -> a n", a=1)).then_inc(loaded, 16)
            sp.dma_start(ones[:, :], W["ones"]).then_inc(loaded, 16)

            def b_rows(c, g):
                sp.dma_start(bb[g % 2][:, :, :],
                             scratch_bc[bass.ds(c, 1), NBG * g:NBG * (g + 1), :].broadcast_to([P, NBG, T])
                             ).then_inc(bb_in[g % 2], 16)

            def store_bc(c1):
                wait_first(sp, m_evac, unit(c1 - 1, O_BC + TB - 1) + 1, sp_passed)
                for tb in range(TB):
                    sp.dma_start(scratch_bc[bass.ds(c1, 1), :, tb * P:(tb + 1) * P].rearrange("a n t -> (a n) t"),
                                 bc[2 * NST * tb:2 * NST * (tb + 1), :]).then_inc(bc_stored, 16)

            def first_rows(c1, g, first):
                if g == 0:
                    wait_first(sp, bc_stored, 16 * TB * (c1 + 1), sp_passed)
                if not first:
                    wait_first(sp, dbx_done, (c1 - 1) * NST + NST - NBG + NBG * g, sp_passed)
                b_rows(c1, g)

            def front0():
                store_bc(0)
                for g in range(2):
                    first_rows(0, g, True)

            def iteration(c, par, has_back, has_front):
                if has_front:
                    if isinstance(c, int) and c == 0:
                        wait_first(sp, m_filled, KT, sp_passed)
                    elif not isinstance(c, int):
                        wait_first(sp, m_filled, unit(c - 1, O_XT + KT - 1) + 1, sp_passed)
                    sp.dma_start(xb[:, :, :], x[bass.ds(c + 1, 1), :, :].rearrange("q (a p) m -> p (q a) m", p=P)).then_inc(x_in, 16)
                if has_back:
                    if has_front:
                        wait_first(sp, m_filled, unit(c, O_XT + KT - 1) + 1, sp_passed)
                    sp.dma_start(xb[:, :, :], x[bass.ds(c - 1, 1), :, :].rearrange("q (a p) m -> p (q a) m", p=P)).then_inc(res_in, 16)
                def more_rows(groups):
                    for g in groups:
                        wait_first(sp, dbx_done, c * NST + NBG * (g - 1), sp_passed)
                        b_rows(c, g)

                more_rows(range(2, NG))
                if has_front:
                    store_bc(c + 1)
                    first_rows(c + 1, 0, False)
                if has_back:
                    wait_first(sp, z_done, TB * c, sp_passed)
                    sp.dma_start(x2[bass.ds(c - 1, 1), :, :].rearrange("q (a p) m -> p (q a) m", p=P), xb[:, :, :]).then_inc(x2_stored, 16)
                if has_front:
                    first_rows(c + 1, 1, False)
                if has_back:
                    wait_first(sp, x2_stored, 16 * c, sp_passed)

            def epilogue():
                sp.dma_start(xb[:, :, :], x[NCH - 1, :, :].rearrange("(a p) m -> p a m", p=P)).then_inc(res_in, 16)
                wait_first(sp, z_done, TB * NCH, sp_passed)
                sp.dma_start(x2[NCH - 1, :, :].rearrange("(a p) m -> p a m", p=P), xb[:, :, :]).then_inc(x2_stored, 16)
                wait_first(sp, x2_stored, 16 * NCH, sp_passed)

            run(sp, iteration, front0, epilogue)

        @block.tensor
        def _(pe):
            def take(i, number):
                if i % 2 == 0 and not (isinstance(number, int) and number < 4):
                    pe.wait_ge(m_evac, number - 2)

            def slot_of(i):
                return i % 4

            def xT(c, kt, par):
                n = unit(c, O_XT + kt)
                if kt == 0:
                    pe.wait_ge(xn_done, TB * (c + 2))
                take(kt, n)
                for tb in range(TB):
                    mm = pe.transpose(pM[:, slot_of(O_XT + kt), tb * P:(tb + 1) * P],
                                      xb[:, tb, kt * P:(kt + 1) * P], ident[:, :])
                mm.then_inc(m_filled, 1)

            def in_proj(c, i, column, src):
                take(i, unit(c, i))
                for kt in range(KT):
                    mm = pe.matmul(pM[:, slot_of(i), :], w_in[:, kt, column:column + P], src[:, kt, :],
                                   start=(kt == 0), stop=(kt == KT - 1))
                mm.then_inc(m_filled, 1)

            def hidden(c, dt, par):
                if dt == 0:
                    pe.wait_ge(m_evac, unit(c, O_XT + KT - 1) + 1)
                in_proj(c, O_HID + dt, dt * P, xnT[1 - par])

            def conv_taps(c, dt):
                if dt == 0:
                    pe.wait_ge(m_evac, unit(c, O_HID + DT - 1) + 1)
                take(O_CONV + dt, unit(c, O_CONV + dt))
                for k in range(KC):
                    mm = pe.matmul(pM[:, slot_of(O_CONV + dt), :], diag[:, dt * KC + k, :], hid[:, dt, k:k + T],
                                   start=(k == 0), stop=(k == KC - 1))
                mm.then_inc(m_filled, 1)

            def x_proj(c, par):
                pe.wait_ge(conv_done, c + 2)
                take(O_DTIN, unit(c, O_DTIN))
                for dt in range(DT):
                    mm = pe.matmul(pM[:, slot_of(O_DTIN), :], w_x[:, dt, 0:DTR], conv[1 - par][:, dt, :],
                                   start=(dt == 0), stop=(dt == DT - 1))
                mm.then_inc(m_filled, 1)
                for tb in range(TB):
                    for dt in range(DT):
                        mm = pe.matmul(pM[:, slot_of(O_BCT), tb * 2 * NST:(tb + 1) * 2 * NST],
                                       conv[1 - par][:, dt, tb * P:(tb + 1) * P], w_x[:, dt, DTR:],
                                       start=(dt == 0), stop=(dt == DT - 1))
                mm.then_inc(m_filled, 1)

            def dt_proj(c, par):
                pe.wait_ge(m_evac, unit(c, O_BCT) + 1)
                for tb in range(TB):
                    take(O_BC + tb, unit(c, O_BC + tb))
                    pe.transpose(pM[:, slot_of(O_BC + tb), 0:P], bcT[1 - par][:, :, :].rearrange("p a n -> p (a n)"),
                                 ident[:, :]).then_inc(m_filled, 1)
                for dt in range(DT):
                    take(O_DT + dt, unit(c, O_DT + dt))
                    pe.matmul(pM[:, slot_of(O_DT + dt), :], w_dt[:, dt * P:(dt + 1) * P], dtin[:, :],
                              start=True, stop=True).then_inc(m_filled, 1)

            def gates(c, dt, par, has_front):
                n = gate_unit(c, dt, has_front)
                take(dt, n)
                for kt in range(KT):
                    mm = pe.matmul(pM[:, slot_of(dt), :], w_in[:, kt, DI + dt * P:DI + (dt + 1) * P], xnT[par][:, kt, :],
                                   start=(kt == 0), stop=(kt == KT - 1))
                mm.then_inc(m_filled, 1)

            def turn_h(c, n):
                for tb in range(TB):
                    i = TB * n + tb
                    if tb == 0:
                        pe.wait_ge(scan_done, c * (NST * 2) + 2 * (n + 1))
                    if not (isinstance(c, int) and c == 0 and i < 2):
                        pe.wait_ge(acc_done, c * (NST * TB) + i - 1)
                    for dt in range(DT):
                        mm = pe.transpose(hT[i % 2][:, dt * P:(dt + 1) * P], h[n % 2][:, dt, tb * P:(tb + 1) * P], ident[:, :])
                    mm.then_inc(h_turned, 1)

            def turn_y(c):
                pe.wait_ge(acc_done, c * (NST * TB))
                for j in range(DT // 2):
                    if j >= 2:
                        pe.wait_ge(y_skip, (c - 1) * DT + 2 * (j - 1))
                    for a in range(2):
                        for tb in range(TB):
                            mm = pe.transpose(pX[:, j % 2, a * T + tb * P:a * T + (tb + 1) * P],
                                              acc[:, tb, (2 * j + a) * P:(2 * j + a + 1) * P], ident[:, :])
                    mm.then_inc(y_turned, 1)

            def out_proj(c, steps):
                for i in steps:
                    tb, dt = divmod(i, DT + 1)
                    if i == 0:
                        pe.wait_ge(y_gated, c)
                    if dt < DT:
                        pe.matmul(pX[:, tb, :], gate[:, dt, tb * P:(tb + 1) * P], w_out[:, dt, :], start=(dt == 0), stop=False)
                    else:
                        pe.matmul(pX[:, tb, :], ones[:, :], b_out[:, :], start=False, stop=True).then_inc(out_mm, 1)

            def iteration(c, par, has_back, has_front):
                for n in range(NST):
                    if n:
                        turn_h(c, n - 1)
                    elif has_back:
                        turn_h(c - 1, NST - 1)
                    if has_back:
                        for dt in PE_GATES_LATE.get(n, ()):
                            gates(c - 1, dt, 1 - par, True)
                        if n == 1:
                            turn_y(c)
                        if n in OUT_FIRST:
                            out_proj(c, PE_OUT[n])
                    if has_front:
                        if n == 1:
                            for kt in range(KT):
                                xT(c, kt, par)
                        for dt in PE_HID.get(n, ()):
                            hidden(c, dt, par)
                        for dt in PE_CONV.get(n, ()):
                            conv_taps(c, dt)
                        if n == 10:
                            x_proj(c, par)
                        if n == 11:
                            dt_proj(c, par)
                    if has_back and n in PE_OUT and n not in OUT_FIRST:
                        out_proj(c, PE_OUT[n])
                    for dt in PE_GATES.get(n, ()):
                        gates(c, dt, par, has_front)

            def front0():
                pe.wait_ge(loaded, 16 * NLOAD)
                for kt in range(KT):
                    xT(-1, kt, 1)
                for dt in range(DT):
                    hidden(-1, dt, 1)
                pe.wait_ge(setup_d, DT * KC)
                for dt in range(DT):
                    conv_taps(-1, dt)
                x_proj(-1, 1)
                dt_proj(-1, 1)

            def epilogue():
                turn_h(NCH - 1, NST - 1)
                for dt in (6, 7):
                    gates(NCH - 1, dt, (NCH - 1) % 2, False)
                turn_y(NCH)
                out_proj(NCH, range(TB * (DT + 1)))

            run(pe, iteration, front0, epilogue)

        @block.scalar
        def _(act):
            def full(i, number):
                act.wait_ge(m_filled, number + (2 if i % 2 == 0 else 1))

            def xT(c, par):
                for kt in range(KT):
                    full(kt, unit(c, O_XT + kt))
                    act.activation(xnT[1 - par][:, kt, :], pM[:, kt, :], ACT.Copy).then_inc(m_evac, 1)

            def hidden(c, dt, par):
                if dt == 0:
                    act.wait_ge(halo_done, c + 2)
                full(O_HID + dt, unit(c, O_HID + dt))
                act.activation(hid[:, dt, HALO:], pM[:, (O_HID + dt) % 4, :], ACT.Identity,
                               bias=b_in[:, dt:dt + 1]).then_inc(m_evac, 1)

            def conv_out(c, dt, par):
                if dt == 0 and not (isinstance(c, int) and c < 1):
                    act.wait_ge(y_gated, c)
                full(O_CONV + dt, unit(c, O_CONV + dt))
                act.activation(conv[1 - par][:, dt, :], pM[:, (O_CONV + dt) % 4, :], ACT.Identity,
                               bias=b_conv[:, dt:dt + 1]).then_inc(m_evac, 1)

            def conv_silu(c, par):
                act.wait_ge(m_evac, unit(c, O_CONV + DT - 1) + 1)
                act.activation(conv[1 - par][:, :, :], conv[1 - par][:, :, :], ACT.Silu).then_inc(conv_done, 1)

            def x_proj(c, par):
                full(O_DTIN, unit(c, O_DTIN))
                if not (isinstance(c, int) and c < 0):
                    act.wait_ge(delta_done, c + 1)
                act.activation(dtin[:, :], pM[:, O_DTIN % 4, :], ACT.Copy).then_inc(m_evac, 1)
                full(O_BCT, unit(c, O_BCT))
                act.activation(bcT[1 - par][:, 0:TB, :],
                               pM[:, O_BCT % 4, 0:TB * 2 * NST].rearrange("p (a n) -> p a n", a=TB), ACT.Copy).then_inc(m_evac, 1)

            def dt_proj(c, par):
                for tb in range(TB):
                    rows = slice(tb * 2 * NST, (tb + 1) * 2 * NST)
                    full(O_BC + tb, unit(c, O_BC + tb))
                    act.activation(bc[rows, :], pM[rows, (O_BC + tb) % 4, 0:P], ACT.Copy).then_inc(m_evac, 1)
                for dt in range(DT):
                    full(O_DT + dt, unit(c, O_DT + dt))
                    act.activation(delta[1 - par][:, dt, :], pM[:, (O_DT + dt) % 4, :], ACT.Identity,
                                   bias=b_dt[:, dt:dt + 1]).then_inc(m_evac, 1)

            def soft_exp(c, par):
                act.wait_ge(m_evac, unit(c, O_DT + DT - 1) + 1)
                act.activation(soft_e, delta[1 - par][:, :, :], ACT.Abs).then_inc(e_done, 1)
                act.wait_ge(e_done, 2 * (c + 1) + 1)
                act.activation(soft_e, soft_e, ACT.Exp, scale=-1.0).then_inc(e_done, 1)

            def soft_ln(c):
                act.wait_ge(q_done, c + 2)
                act.activation(soft_w[:, :, :], soft_w[:, :, :], ACT.Ln).then_inc(ln_done, 1)

            def first_decay(c):
                act.wait_ge(da0_raw, c + 2)
                act.activation(da0[:, :, :], da0[:, :, :], ACT.Exp).then_inc(da0_done, 1)

            def exps(c, n, par, hf):
                if n == 0 and hf == 0:
                    act.wait_ge(delta_done, c + 1)
                if not (isinstance(c, int) and c == 0 and n == 0):
                    act.wait_ge(scan_done, c * (NST * 2) + 2 * n + hf - 1)
                for dt in range(hf * DT // 2, (hf + 1) * DT // 2):
                    e = act.activation(da[:, dt, 1:], delta[par][:, dt, 1:], ACT.Exp, scale=a_neg[:, dt, n:n + 1])
                e.then_inc(da_done, 1)

            def gates(c, dt, has_front):
                if dt == 0 and not (isinstance(c, int) and c == 0):
                    act.wait_ge(out_mm, TB * c)
                full(dt, gate_unit(c, dt, has_front))
                act.activation(gate[:, dt, :], pM[:, dt % 4, :], ACT.Identity,
                               bias=b_in[:, DT + dt:DT + dt + 1]).then_inc(m_evac, 1)

            def late_gates(c, has_front, which):
                for dt in which:
                    gates(c, dt, has_front)
                if which and which[-1] == DT - 1:
                    act.wait_ge(m_evac, gate_unit(c, DT - 1, has_front) + 1)
                    act.activation(gate[:, :, :], gate[:, :, :], ACT.Silu).then_inc(gate_done, 1)

            def iteration(c, par, has_back, has_front):
                for n in range(NST):
                    if has_front and n == 14:
                        soft_ln(c)
                    exps(c, n, par, 0)
                    if has_front:
                        for dt in ACT_HID_MID.get(n, ()):
                            hidden(c, dt, par)
                        for dt in ACT_CONV.get(n, ()):
                            conv_out(c, dt, par)
                        if n == 10:
                            conv_silu(c, par)
                        if n == 12:
                            x_proj(c, par)
                    for dt in {14: (0, 1), 15: (2, 3)}.get(n, ()):
                        gates(c, dt, has_front)
                    if has_back:
                        late_gates(c - 1, True, {0: (4, 5), 2: (6, 7)}.get(n, ()))
                    if n == 0 and not (isinstance(c, int) and c == 0):
                        first_decay(c - 1)
                    exps(c, n, par, 1)
                    if has_front:
                        if n == 2:
                            xT(c, par)
                        for dt in ACT_HID_END.get(n, ()):
                            hidden(c, dt, par)
                        if n == 12:
                            dt_proj(c, par)
                            soft_exp(c, par)

            def front0():
                act.wait_ge(loaded, 16 * NLOAD)
                act.activation(a_neg[:, :, :], a_neg[:, :, :], ACT.Exp).then_inc(setup_a, 1)
                xT(-1, 1)
                for dt in range(DT):
                    hidden(-1, dt, 1)
                for dt in range(DT):
                    conv_out(-1, dt, 1)
                conv_silu(-1, 1)
                x_proj(-1, 1)
                dt_proj(-1, 1)
                soft_exp(-1, 1)
                soft_ln(-1)
                act.wait_ge(setup_d, DT * KC + 1)
                first_decay(-1)

            def epilogue():
                late_gates(NCH - 1, False, (4, 5, 6, 7))

            run(act, iteration, front0, epilogue)

        @block.vector
        def _(dve):
            def norm_stats(c):
                dve.wait_ge(x_in, 16 * (c + 2))
                for tb in range(TB):
                    dve.bn_stats(stats[:, tb, :], xb[:, tb, :]).then_inc(stats_done, 1)
                for tb in range(TB):
                    wait_first(dve, stats_done, TB * (c + 1) + tb + 1, dve_passed)
                    dve.bn_aggr(mv[:, tb, :], stats[:, tb, :]).then_inc(mv_done, 1)

            def norm(c):
                dve.wait_ge(rstd_done, c + 2)
                for tb in range(TB):
                    dve.tensor_scalar(xb[:, tb, :], xb[:, tb, :], mv[:, tb, 0:1], rstd[:, tb:tb + 1],
                                      ALU.subtract, ALU.mult).then_inc(xn_done, 1)

            def halo(c):
                if not (isinstance(c, int) and c < 1):
                    dve.wait_ge(carry_done, c * NST)
                dve.tensor_copy(lim_now[:, :], lim[:, bass.ds(c + 1, 1), :].rearrange("p a b -> p (a b)")).then_inc(lim_done, 1)
                dve.wait_ge(lim_done, c + 2)
                if not (isinstance(c, int) and c < 0):
                    dve.wait_ge(m_evac, unit(c - 1, O_DT + DT - 1) + 1)
                dve.tensor_scalar(hid[:, :, 0:HALO], hid[:, :, T:T + HALO], lim_now[:, 0:1], lim_now[:, 1:2],
                                  ALU.max, ALU.min).then_inc(halo_done, 1)

            def soft_q(c):
                dve.wait_ge(w_done, c + 2)
                dve.scalar_tensor_tensor(soft_e, soft_w[:, :, :], -1.0, soft_e, ALU.add, ALU.subtract).then_inc(q_done, 1)

            def soft_end(c, par):
                dve.wait_ge(ln_done, c + 2)
                dve.tensor_tensor(soft_w[:, :, :], soft_w[:, :, :], soft_e, ALU.subtract).then_inc(lq_done, 1)
                dve.wait_ge(lq_done, c + 2)
                dve.scalar_tensor_tensor(delta[1 - par][:, :, :], delta[1 - par][:, :, :], 0.0, soft_w[:, :, :],
                                         ALU.max, ALU.add).then_inc(delta_done, 1)

            def scans(c, n):
                dve.wait_ge(dbx_done, c * NST + n + 1)
                if not (isinstance(c, int) and c == 0 and n < 2):
                    dve.wait_ge(h_turned, c * (NST * TB) + TB * (n - 1))
                    dve.wait_ge(carry_done, c * NST + n - 1)
                for hf in range(2):
                    tiles = slice(hf * DT // 2, (hf + 1) * DT // 2)
                    row = lambda t: t[:, tiles, :].rearrange("p d t -> p (d t)")
                    dve.wait_ge(da_done, c * (NST * 2) + 2 * n + hf + 1)
                    dve.tensor_tensor_scan(row(h[n % 2]), row(da), row(dbx[n % 2]), 0.0,
                                           ALU.mult, ALU.add).then_inc(scan_done, 1)

            def save(c, n):
                dve.wait_ge(scan_done, c * (NST * 2) + 2 * (n + 1))
                if not (isinstance(c, int) and c == 0):
                    dve.wait_ge(dbx_done, c * NST + n + 1)
                dve.tensor_scalar(carry[:, n, :], h[n % 2][:, :, T - 1], lim_now[:, 1:2], lim_now[:, 0:1],
                                  ALU.min, ALU.max).then_inc(carry_done, 1)

            def add_h(c, n, par):
                for tb in range(TB):
                    i = TB * n + tb
                    cn = bcT[par][:, tb, NST + n:NST + n + 1]
                    dve.wait_ge(h_turned, c * (NST * TB) + i + 1)
                    if n == 0:
                        if not (isinstance(c, int) and c == 0):
                            dve.wait_ge(y_turned, (DT // 2) * c)
                        dve.tensor_scalar(acc[:, tb, :], hT[i % 2][:, :], cn, None, ALU.mult).then_inc(acc_done, 1)
                    else:
                        dve.wait_ge(acc_done, c * (NST * TB) + i - TB + 1)
                        dve.scalar_tensor_tensor(acc[:, tb, :], hT[i % 2][:, :], cn, acc[:, tb, :],
                                                 ALU.mult, ALU.add).then_inc(acc_done, 1)

            def skip(c, par):
                for j in range(DT // 2):
                    dve.wait_ge(y_turned, (DT // 2) * (c - 1) + j + 1)
                    for a in range(2):
                        dt = 2 * j + a
                        dve.scalar_tensor_tensor(conv[1 - par][:, dt, :], conv[1 - par][:, dt, :], d_skip[:, dt:dt + 1],
                                                 pX[:, j % 2, a * T:(a + 1) * T], ALU.mult, ALU.add).then_inc(y_skip, 1)

            def out_stats(c, tb):
                dve.wait_ge(out_mm, TB * (c - 1) + tb + 1)
                dve.bn_stats(stats2[:, tb, :], pX[:, tb, :]).then_inc(st2_done, 1)
                wait_first(dve, st2_done, TB * (c - 1) + tb + 1, dve_passed)
                dve.bn_aggr(mv2[:, tb, :], stats2[:, tb, :]).then_inc(mv2_done, 1)

            def out_norm(c):
                dve.wait_ge(rstd2_done, c)
                dve.wait_ge(res_in, 16 * c)
                for tb in range(TB):
                    dve.scalar_tensor_tensor(shift2[:, tb:tb + 1], mv2[:, tb, 0:1], -1.0, rstd2[:, tb:tb + 1],
                                             ALU.mult, ALU.mult).then_inc(shift2_done, 1)
                for tb in range(TB):
                    dve.wait_ge(shift2_done, TB * (c - 1) + tb + 1)
                    dve.tensor_scalar(xb[:, tb, :], xb[:, tb, :], shift2[:, tb:tb + 1], None, ALU.add).then_inc(res_done, 1)
                for tb in range(TB):
                    dve.wait_ge(res_done, TB * (c - 1) + tb + 1)
                    dve.scalar_tensor_tensor(xb[:, tb, :], pX[:, tb, :], rstd2[:, tb:tb + 1], xb[:, tb, :],
                                             ALU.mult, ALU.add).then_inc(z_done, 1)

            def iteration(c, par, has_back, has_front):
                for n in range(NST):
                    if n == 0 and has_front:
                        norm_stats(c)
                    scans(c, n)
                    if n == 0:
                        if has_back:
                            add_h(c - 1, NST - 1, 1 - par)
                            save(c - 1, NST - 1)
                        if has_front:
                            halo(c)
                            norm(c)
                    if n == 1 and has_back:
                        skip(c, par)
                    if n:
                        add_h(c, n - 1, par)
                        save(c, n - 1)
                    if has_back and n in (9, 12):
                        out_stats(c, (n - 9) // 3)
                    if has_back and n == 13:
                        out_norm(c)
                    if has_front and n == 12:
                        soft_q(c)
                    if has_front and n == 13:
                        soft_end(c, par)

            def front0():
                dve.wait_ge(setup_p, 7 + NCH // CPB + 1)
                norm_stats(-1)
                halo(-1)
                norm(-1)
                dve.wait_ge(loaded, 16 * NLOAD)
                for dt in range(DT):
                    for k in range(KC):
                        dve.tensor_scalar(diag[:, dt * KC + k, :], ident[:, :], taps[:, dt, k:k + 1], None,
                                          ALU.mult).then_inc(setup_d, 1)
                dve.wait_ge(setup_a, 1)
                dve.tensor_scalar(a_neg[:, :, :], a_neg[:, :, :], -1.0, None, ALU.mult).then_inc(setup_d, 1)
                soft_q(-1)
                soft_end(-1, 1)

            def epilogue():
                add_h(NCH - 1, NST - 1, (NCH - 1) % 2)
                skip(NCH, NCH % 2)
                for tb in range(TB):
                    out_stats(NCH, tb)
                out_norm(NCH)

            run(dve, iteration, front0, epilogue)

        @block.gpsimd
        def _(pool):
            def rsqrt(c, which):
                m, ve, r, sm, sv, sr = ((mv, veps, rstd, mv_done, veps_done, rstd_done),
                                        (mv2, veps2, rstd2, mv2_done, veps2_done, rstd2_done))[which]
                wait_first(pool, sm, TB * (c + 1), pool_passed)
                pool.tensor_scalar(ve[:, :], m[:, :, 1], EPS, 1.0, ALU.add, ALU.mult).then_inc(sv, 1)
                pool.wait_ge(sv, c + 1)
                pool.tensor_tensor(r[:, :], ve[:, :], half[:, :], ALU.pow).then_inc(sr, 1)

            def b_times_u(c, n, par):
                g = n // NBG
                if n % NBG == 0:
                    pool.wait_ge(bb_in[g % 2], 16 * ((NG // 2) * c + g // 2 + 1))
                if not (isinstance(c, int) and c == 0 and n < 2):
                    pool.wait_ge(scan_done, c * (NST * 2) + 2 * (n - 1))
                rows = bb[g % 2][:, n % NBG:n % NBG + 1, :].broadcast_to([P, DT, T])
                if isinstance(c, int) and c == 0:
                    pool.tensor_tensor(dbx[n % 2][:, :, :], u[:, :, :], rows, ALU.mult).then_inc(dbx_done, 1)
                    return
                pool.tensor_tensor(dbx[n % 2][:, :, :], u[:, :, :], rows, ALU.mult).then_inc(prod_done, 1)
                if n == 0:
                    pool.wait_ge(da0_done, c + 1)
                pool.wait_ge(carry_done, (c - 1) * NST + n + 1)
                pool.tensor_tensor(da0[:, n, :], da0[:, n, :], carry[:, n, :], ALU.mult).then_inc(inject_done, 1)
                pool.wait_ge(inject_done, (c - 1) * NST + n + 1)
                pool.wait_ge(prod_done, (c - 1) * NST + n + 1)
                pool.tensor_tensor(dbx[n % 2][:, :, 0], dbx[n % 2][:, :, 0], da0[:, n, :], ALU.add).then_inc(dbx_done, 1)

            def decay0(c, par):
                pool.wait_ge(delta_done, c + 2)
                if isinstance(c, int) and c == -1:
                    pool.wait_ge(setup_d, DT * KC + 1)
                pool.tensor_tensor(da0[:, :, :], a_neg[:, :, :].rearrange("p d n -> p n d"),
                                   delta[1 - par][:, :, 0:1].rearrange("p d a -> p a d").broadcast_to([P, NST, DT]),
                                   ALU.mult).then_inc(da0_raw, 1)

            def one_plus_e(c):
                pool.wait_ge(e_done, 2 * (c + 2))
                wait_first(pool, bc_stored, 16 * TB * (c + 2), pool_passed)
                pool.tensor_scalar(soft_w[:, :, :], soft_e, 1.0, 1.0, ALU.add, ALU.mult).then_inc(w_done, 1)

            def make_u(c, par):
                pool.wait_ge(delta_done, c + 2)
                if not (isinstance(c, int) and c < 0):
                    pool.wait_ge(dbx_done, NST * (c + 1))
                pool.tensor_tensor(u[:, :, :], delta[1 - par][:, :, :], conv[1 - par][:, :, :], ALU.mult).then_inc(u_done, 1)

            def gating(c, par):
                pool.wait_ge(y_skip, DT * c)
                pool.wait_ge(gate_done, c)
                pool.tensor_tensor(gate[:, :, :], conv[1 - par][:, :, :], gate[:, :, :], ALU.mult).then_inc(y_gated, 1)

            def iteration(c, par, has_back, has_front):
                pool.wait_ge(u_done, c + 1)
                for n in range(NST):
                    b_times_u(c, n, par)
                    if n == 1 and has_front:
                        rsqrt(c + 1, 0)
                    if n == 3 and has_back:
                        gating(c, par)
                    if has_back and n == 13:
                        rsqrt(c - 1, 1)
                    if has_front and n == 13:
                        one_plus_e(c)
                if has_front:
                    make_u(c, par)
                    decay0(c, par)

            def front0():
                pool.memset(hid[:, :, :], 0.0).then_inc(setup_p, 1)
                pool.memset(da[:, :, 0:1], 0.0).then_inc(setup_p, 1)
                for t in bcT:
                    pool.memset(t[:, TB:, :], 0.0).then_inc(setup_p, 1)
                pool.memset(half[:, :], -0.5).then_inc(setup_p, 1)
                pool.memset(lim[:, :, 0:1], -BIG).then_inc(setup_p, 1)
                pool.memset(lim[:, :, 1:2], BIG).then_inc(setup_p, 1)
                pool.wait_ge(setup_p, 7)
                for c in range(0, NCH + 1, CPB):
                    pool.memset(lim[:, c, :], 0.0).then_inc(setup_p, 1)
                rsqrt(0, 0)
                one_plus_e(-1)
                make_u(-1, 1)
                decay0(-1, 1)

            def epilogue():
                gating(NCH, NCH % 2)
                rsqrt(NCH - 1, 1)

            run(pool, iteration, front0, epilogue)


HT = FF // P
T2 = 512
TB2 = T2 // P
NCH2 = TOK // T2
HALVES = 2
FH = FF // HALVES
FT = FH // P


def hadamard_block(nc, W, scratch_w):
    ctx = ExitStack()
    with ctx:
        def sb(name, shape, dt=F32):
            return ctx.enter_context(nc.sbuf_tensor(name, shape, dt))

        def sem(name):
            return ctx.enter_context(nc.semaphore(name))

        TILES = 16
        JOBS = (("up", (4, 8)), ("gate", (4, 8)), ("down", (1, 2, 4, 8)))
        buf = [sb(f"had{i}", [P, TILES, DM]) for i in range(5)]
        scaled = [sb(f"scaled{i}", [P, DM]) for i in range(2)]
        h128 = sb("h128", [P, P])
        su_ug = sb("su_ug", [P, KT])
        su_dp = sb("su_dp", [P, HT])
        wscale = sb("wscale", [P, DM])
        ps = [ctx.enter_context(nc.psum_tensor(f"had_ps{i}", [P, DM], F32)) for i in range(4)]
        w_in = [sem(f"hw_in{i}") for i in range(len(JOBS))]
        small_in = sem("small_in")
        su_done = sem("su_done")
        plus_done = sem("plus_done")
        minus_done = sem("minus_done")
        rows_scaled = sem("rows_scaled")
        mm_done = sem("mm_done")
        evac = sem("had_evac")
        stored = [sem("had_stored0"), sem("had_stored1")]
        plan = []
        for j, (name, strides) in enumerate(JOBS):
            chain = [j]
            for s in range(len(strides)):
                chain.append(3 if s % 2 == 0 else j)
            plan.append(chain)
        before = [sum(len(s) for _, s in JOBS[:j]) for j in range(len(JOBS) + 1)]
        CUT = 3
        block = ctx.enter_context(nc.Block())

        def halves(t, stride):
            v = t[:, :, :].rearrange("p (g two s) m -> p g two (s m)", two=2, s=stride)
            return v[:, :, 0, :], v[:, :, 1, :]

        @block.sync
        def _(sp):
            for dst, src in ((h128[:, :], W["h128"]), (su_ug[:, :], W["SU_ug"]), (su_dp[:, :], W["SU_dp"]),
                             (wscale[:, :], W["Wscale_dp"].rearrange("(a n) -> a n", a=1).broadcast_to([P, DM]))):
                sp.dma_start(dst, src).then_inc(small_in, 16)
            for j, name in enumerate(("W_up", "W_gate")):
                sp.dma_start(buf[j][:, :, :].rearrange("p (k q) m -> p k (q m)", k=KT),
                             W[name].rearrange("(k p) f -> p k f", p=P)).then_inc(w_in[j], 16)
            sp.dma_start(buf[2][:, :, :], W["W_down"].rearrange("(k p) m -> p k m", p=P)).then_inc(w_in[2], 16)
            for i in range(len(JOBS) * TILES):
                j, t = divmod(i, TILES)
                sp.wait_ge(evac, i + 1)
                if j < 2:
                    dst = scratch_w[j][(t // 4) * P:(t // 4 + 1) * P, (t % 4) * DM:(t % 4 + 1) * DM]
                else:
                    dst = scratch_w[j][t * P:(t + 1) * P, :]
                sp.dma_start(dst, scaled[i % 2][:, :]).then_inc(stored[i % 2], 16)
            for i in range(2):
                sp.wait_ge(stored[i], 16 * len(JOBS) * TILES // 2)

        def butterflies(eng, j, s, mine):
            stride = JOBS[j][1][s]
            src, dst = buf[plan[j][s]], buf[plan[j][s + 1]]
            if s == 0:
                eng.wait_ge(w_in[j], 16)
                if j:
                    eng.wait_ge(mm_done, TILES * j)
                if j == 2:
                    eng.wait_ge(rows_scaled, 1)
            done = before[j] + s
            if done:
                eng.wait_ge(plus_done, done)
                eng.wait_ge(minus_done, done)
            (s0, s1), (d0, d1) = halves(src, stride), halves(dst, stride)
            cut = stride * DM * CUT // 8
            if mine == "plus":
                eng.tensor_tensor(d0, s0, s1, ALU.add)
                eng.tensor_tensor(d1[:, :, 0:cut], s0[:, :, 0:cut], s1[:, :, 0:cut], ALU.subtract).then_inc(plus_done, 1)
            else:
                eng.tensor_tensor(d1[:, :, cut:], s0[:, :, cut:], s1[:, :, cut:], ALU.subtract).then_inc(minus_done, 1)

        @block.vector
        def _(dve):
            dve.wait_ge(small_in, 64)
            dve.tensor_scalar(su_ug[:, :], su_ug[:, :], float(DM) ** -0.5, None, ALU.mult).then_inc(su_done, 1)
            dve.tensor_scalar(su_dp[:, :], su_dp[:, :], float(FF) ** -0.5, None, ALU.mult).then_inc(su_done, 1)
            for j in range(len(JOBS)):
                if j == 2:
                    dve.wait_ge(w_in[2], 16)
                    dve.tensor_tensor(buf[2][:, :, :], buf[2][:, :, :],
                                      wscale[:, :].rearrange("p (a m) -> p a m", a=1).broadcast_to([P, TILES, DM]),
                                      ALU.mult).then_inc(rows_scaled, 1)
                for s in range(len(JOBS[j][1])):
                    butterflies(dve, j, s, "plus")

        @block.gpsimd
        def _(pool):
            for j in range(len(JOBS)):
                for s in range(len(JOBS[j][1])):
                    butterflies(pool, j, s, "minus")

        @block.tensor
        def _(pe):
            pe.wait_ge(small_in, 64)
            for i in range(len(JOBS) * TILES):
                j, t = divmod(i, TILES)
                if t == 0:
                    pe.wait_ge(plus_done, before[j + 1])
                    pe.wait_ge(minus_done, before[j + 1])
                if i >= 4:
                    pe.wait_ge(evac, i - 3)
                pe.matmul(ps[i % 4][:, :], h128[:, :], buf[plan[j][-1]][:, t, :], start=True, stop=True).then_inc(mm_done, 1)

        @block.scalar
        def _(act):
            act.wait_ge(su_done, 2)
            for i in range(len(JOBS) * TILES):
                j, t = divmod(i, TILES)
                act.wait_ge(mm_done, i + 1)
                if i >= 2:
                    act.wait_ge(stored[i % 2], 16 * (i // 2))
                scale = su_ug[:, t // 4:t // 4 + 1] if j < 2 else su_dp[:, t:t + 1]
                act.activation(scaled[i % 2][:, :], ps[i % 4][:, :], ACT.Copy, scale=scale).then_inc(evac, 1)


def ffn_block(nc, x2, W, scratch_w, scratch_part, out):
    ctx = ExitStack()
    with ctx:
        def sb(name, shape, dt=F32):
            return ctx.enter_context(nc.sbuf_tensor(name, shape, dt))

        def pb(name):
            return ctx.enter_context(nc.psum_tensor(name, [P, T2], F32))

        def sem(name):
            return ctx.enter_context(nc.semaphore(name))

        wug = [sb(f"wug_{s}", [P, KT, 2 * FH], F32R) for s in ("hi", "lo")]
        wd = [sb(f"wd_{s}", [P, FT, DM], F32R) for s in ("hi", "lo")]
        stage = [sb(f"stage{i}", [P, FH]) for i in range(2)]
        xs = sb("xs", [P, TB2, DM])
        xT = [sb(f"xT_{s}", [P, KT, T2], F32R) for s in ("hi", "lo")]
        prod = [sb(f"prod_{s}", [P, FT, T2], F32R) for s in ("hi", "lo")]
        s_gate = [sb(f"s_gate{i}", [P, T2]) for i in range(2)]
        p = [sb(f"p{i}", [P, T2]) for i in range(2)]
        part = sb("part", [P, TB2, DM])
        res = sb("res", [P, TB2, DM])
        ident = sb("ident2", [P, P])
        scale_ug = sb("scale_ug", [P, 2 * HT])
        half = sb("half2", [P, TB2])
        stats, mv, veps, rstd = (sb(n, [P, TB2, k]) for n, k in (("fst", 6), ("fmv", 2), ("fve", 1), ("frs", 1)))
        ostats, omv, oveps, orstd = (sb(n, [P, TB2, k]) for n, k in (("ost", 6), ("omv", 2), ("ove", 1), ("ors", 1)))
        pT = [pb(f"pT{i}") for i in range(2)]
        pg = [pb(f"pg{i}") for i in range(2)]
        pu = [pb(f"pu{i}") for i in range(2)]
        po = [pb(f"po{i}") for i in range(2)]

        small_in = sem("f_small_in"); half_set = sem("half_set")
        stage_in = [sem("stage_in0"), sem("stage_in1")]
        w_hi = sem("w_hi"); w_lo = sem("w_lo")
        xs_in = sem("xs_in"); res_in = sem("f_res_in"); part_in = sem("part_in")
        st_done = sem("f_st"); mv_done = sem("f_mv"); veps_done = sem("f_veps"); rstd_done = sem("f_rstd"); xn_done = sem("f_xn")
        xT_filled = sem("xT_filled"); x_hi = sem("x_hi"); x_lo = sem("x_lo")
        gate_mm = sem("gate_mm"); up_mm = sem("up_mm"); silu_done = sem("silu_done"); p_done = sem("p_done")
        p_hi = sem("p_hi"); p_lo = sem("p_lo")
        down_mm = sem("down_mm"); o_evac = sem("o_evac"); part_stored = sem("part_stored")
        ost_done = sem("o_st"); omv_done = sem("o_mv"); oveps_done = sem("o_veps"); orstd_done = sem("o_rstd")
        sp_passed, dve_passed, pool_passed = (sem(f"f_{e}_passed") for e in ("sp", "dve", "pool"))
        o_normed = sem("o_normed"); o_done = sem("o_done"); out_stored = sem("out_stored")

        PIECES = 2 * KT + FT // 2

        def piece(half_no, q):
            if q < 2 * KT:
                kt, which = divmod(q, 2)
                src = scratch_w[which][kt * P:(kt + 1) * P, half_no * FH:(half_no + 1) * FH]
                return src, lambda s: wug[s][:, kt, which * FH:(which + 1) * FH]
            ft = 2 * (q - 2 * KT)
            src = scratch_w[2][half_no * FH + ft * P:half_no * FH + (ft + 2) * P, :].rearrange("(a p) m -> p a m", p=P)
            return src, lambda s: wd[s][:, ft:ft + 2, :].rearrange("p a m -> p (a m)")

        def run(eng, weights, first_front, step):
            for half_no in range(HALVES):
                weights(half_no)
                first_front(half_no * NCH2)
                step(half_no, 0, half_no * NCH2, True)
                with eng.Fori(1, NCH2 - 1) as ck:
                    step(half_no, ck, half_no * NCH2, True)
                step(half_no, NCH2 - 1, half_no * NCH2, False)

        def nothing(*_):
            return None

        block = ctx.enter_context(nc.Block())

        @block.sync
        def _(sp):
            sp.dma_start(ident[:, :], W["ident"]).then_inc(small_in, 16)
            sp.dma_start(scale_ug[:, :], W["Wscale_ug"]).then_inc(small_in, 16)

            def load_xs(chunk, step_no):
                if not (isinstance(step_no, int) and step_no == 0):
                    wait_first(sp, xT_filled, KT * step_no, sp_passed)
                sp.dma_start(xs[:, :, :], x2[bass.ds(chunk, 1), :, :].rearrange("c (a p) m -> p (c a) m", p=P)).then_inc(xs_in, 16)

            def step(half_no, ck, base, more):
                i = ck + base
                if more:
                    load_xs(ck + 1, i + 1)
                rows = lambda t: t[bass.ds(ck, 1), :, :].rearrange("c (a p) m -> p (c a) m", p=P)
                if half_no == 0:
                    wait_first(sp, o_evac, TB2 * (i + 1), sp_passed)
                    sp.dma_start(rows(scratch_part), part[:, :, :]).then_inc(part_stored, 16)
                else:
                    if not (isinstance(ck, int) and ck == 0):
                        wait_first(sp, o_normed, TB2 * ck, sp_passed)
                        wait_first(sp, out_stored, 16 * ck, sp_passed)
                    sp.dma_start(part[:, :, :], rows(scratch_part)).then_inc(part_in, 16)
                    sp.dma_start(res[:, :, :], rows(x2)).then_inc(res_in, 16)
                    wait_first(sp, o_done, TB2 * (ck + 1), sp_passed)
                    sp.dma_start(rows(out), res[:, :, :]).then_inc(out_stored, 16)

            def between(half_no):
                if half_no:
                    wait_first(sp, part_stored, 16 * NCH2, sp_passed)

            run(sp, between, lambda base: load_xs(0, base), step)
            wait_first(sp, out_stored, 16 * NCH2, sp_passed)

        @block.gpsimd
        def _(pool):
            pool.memset(half[:, :], -0.5).then_inc(half_set, 1)
            pool.wait_ge(half_set, 1)

            def weights(half_no):
                for q in range(PIECES):
                    n = half_no * PIECES + q
                    if n >= 2:
                        pool.wait_ge(w_lo, n - 1)
                    src, _ = piece(half_no, q)
                    dst = stage[q % 2][:, :] if q < 2 * KT else stage[q % 2][:, :].rearrange("p (a m) -> p a m", a=2)
                    pool.dma_start(dst, src).then_inc(stage_in[q % 2], 16)

            def rsqrt(count, m, ve, r, m_sem, v_sem, r_sem):
                wait_first(pool, m_sem, TB2 * count, pool_passed)
                pool.tensor_scalar(ve[:, :, 0], m[:, :, 1], EPS, 1.0, ALU.add, ALU.mult).then_inc(v_sem, 1)
                pool.wait_ge(v_sem, count)
                pool.tensor_tensor(r[:, :, 0], ve[:, :, 0], half[:, :], ALU.pow).then_inc(r_sem, 1)

            def front(step_no):
                rsqrt(step_no + 1, mv, veps, rstd, mv_done, veps_done, rstd_done)

            def step(half_no, ck, base, more):
                if more:
                    front(ck + base + 1)
                if half_no:
                    rsqrt(ck + 1, omv, oveps, orstd, omv_done, oveps_done, orstd_done)

            run(pool, weights, front, step)

        @block.tensor
        def _(pe):
            pe.wait_ge(small_in, 32)

            def front(step_no):
                pe.wait_ge(xn_done, TB2 * (step_no + 1))
                for kt in range(KT):
                    if kt >= 2:
                        pe.wait_ge(x_lo, KT * step_no + kt - 1)
                    for tb in range(TB2):
                        mm = pe.transpose(pT[kt % 2][:, tb * P:(tb + 1) * P], xs[:, tb, kt * P:(kt + 1) * P], ident[:, :])
                    mm.then_inc(xT_filled, 1)

            PASSES = ((0, 0), (0, 1), (1, 0))

            def step(half_no, ck, base, more):
                i = ck + base
                pe.wait_ge(x_lo, KT * (i + 1))
                for ft in range(FT):
                    for bank, which, freed, filled in ((pg, 1, silu_done, gate_mm), (pu, 0, p_done, up_mm)):
                        if ft >= 2:
                            pe.wait_ge(freed, FT * i + ft - 1)
                        for kt in range(KT):
                            for n, (a, b) in enumerate(PASSES):
                                lo = which * FH + ft * P
                                mm = pe.matmul(bank[ft % 2][:, :], wug[a][:, kt, lo:lo + P], xT[b][:, kt, :],
                                               start=(kt == 0 and n == 0), stop=(kt == KT - 1 and n == len(PASSES) - 1))
                        mm.then_inc(filled, 1)
                if more:
                    front(i + 1)
                pe.wait_ge(p_lo, FT * (i + 1))
                for tb in range(TB2):
                    if tb == 0 and not (isinstance(i, int) and i == 0):
                        pe.wait_ge(o_evac, TB2 * i)
                    elif tb >= 2:
                        pe.wait_ge(o_evac, TB2 * i + tb - 1)
                    for ft in range(FT):
                        for n, (a, b) in enumerate(PASSES):
                            mm = pe.matmul(po[tb % 2][:, :], prod[a][:, ft, tb * P:(tb + 1) * P], wd[b][:, ft, :],
                                           start=(ft == 0 and n == 0), stop=(ft == FT - 1 and n == len(PASSES) - 1))
                    mm.then_inc(down_mm, 1)

            run(pe, lambda half_no: pe.wait_ge(w_lo, PIECES * (half_no + 1)), front, step)

        @block.scalar
        def _(act):
            act.wait_ge(small_in, 32)

            def weights(half_no):
                for q in range(PIECES):
                    act.wait_ge(stage_in[q % 2], 16 * (half_no * PIECES // 2 + q // 2 + 1))
                    if half_no and q == 0:
                        act.wait_ge(up_mm, NCH2 * FT)
                    if half_no and q == 2 * KT:
                        act.wait_ge(down_mm, NCH2 * TB2)
                    _, dst = piece(half_no, q)
                    act.activation(dst(0), stage[q % 2][:, :], ACT.Copy).then_inc(w_hi, 1)

            def front(step_no):
                for kt in range(KT):
                    act.wait_ge(xT_filled, KT * step_no + kt + 1)
                    act.activation(xT[0][:, kt, :], pT[kt % 2][:, :], ACT.Copy).then_inc(x_hi, 1)

            def step(half_no, ck, base, more):
                i = ck + base
                for ft in range(FT):
                    f = half_no * FT + ft
                    act.wait_ge(gate_mm, FT * i + ft + 1)
                    if ft >= 2:
                        act.wait_ge(p_done, FT * i + ft - 1)
                    act.activation(s_gate[ft % 2][:, :], pg[ft % 2][:, :], ACT.Silu,
                                   scale=scale_ug[:, HT + f:HT + f + 1]).then_inc(silu_done, 1)
                    act.wait_ge(p_done, FT * i + ft + 1)
                    if ft == 0 and not (isinstance(i, int) and i == 0):
                        act.wait_ge(down_mm, TB2 * i)
                    act.activation(prod[0][:, ft, :], p[ft % 2][:, :], ACT.Copy).then_inc(p_hi, 1)
                if more:
                    front(i + 1)
                if half_no == 0:
                    for tb in range(TB2):
                        act.wait_ge(down_mm, TB2 * i + tb + 1)
                        if tb == 0 and not (isinstance(i, int) and i == 0):
                            act.wait_ge(part_stored, 16 * i)
                        act.activation(part[:, tb, :], po[tb % 2][:, :], ACT.Copy).then_inc(o_evac, 1)

            run(act, weights, front, step)

        @block.vector
        def _(dve):
            dve.wait_ge(small_in, 32)

            def weights(half_no):
                for q in range(PIECES):
                    dve.wait_ge(w_hi, half_no * PIECES + q + 1)
                    _, dst = piece(half_no, q)
                    dve.tensor_tensor(dst(1), stage[q % 2][:, :], dst(0).bitcast(F32), ALU.subtract).then_inc(w_lo, 1)

            def norm_stats(step_no):
                dve.wait_ge(xs_in, 16 * (step_no + 1))
                for tb in range(TB2):
                    dve.bn_stats(stats[:, tb, :], xs[:, tb, :]).then_inc(st_done, 1)
                for tb in range(TB2):
                    wait_first(dve, st_done, TB2 * step_no + tb + 1, dve_passed)
                    dve.bn_aggr(mv[:, tb, :], stats[:, tb, :]).then_inc(mv_done, 1)

            def norm(step_no):
                dve.wait_ge(rstd_done, step_no + 1)
                for tb in range(TB2):
                    dve.tensor_scalar(xs[:, tb, :], xs[:, tb, :], mv[:, tb, 0:1], rstd[:, tb, :],
                                      ALU.subtract, ALU.mult).then_inc(xn_done, 1)

            def split_x(step_no):
                for kt in range(KT):
                    dve.wait_ge(x_hi, KT * step_no + kt + 1)
                    dve.tensor_tensor(xT[1][:, kt, :], pT[kt % 2][:, :], xT[0][:, kt, :].bitcast(F32),
                                      ALU.subtract).then_inc(x_lo, 1)

            def front(step_no):
                norm_stats(step_no)
                norm(step_no)
                split_x(step_no)

            def step(half_no, ck, base, more):
                i = ck + base
                for ft in range(FT):
                    f = half_no * FT + ft
                    dve.wait_ge(silu_done, FT * i + ft + 1)
                    dve.wait_ge(up_mm, FT * i + ft + 1)
                    if ft >= 2:
                        dve.wait_ge(p_lo, FT * i + ft - 1)
                    dve.scalar_tensor_tensor(p[ft % 2][:, :], pu[ft % 2][:, :], scale_ug[:, f:f + 1], s_gate[ft % 2][:, :],
                                             ALU.mult, ALU.mult).then_inc(p_done, 1)
                    dve.wait_ge(p_hi, FT * i + ft + 1)
                    dve.tensor_tensor(prod[1][:, ft, :], p[ft % 2][:, :], prod[0][:, ft, :].bitcast(F32),
                                      ALU.subtract).then_inc(p_lo, 1)
                    if more and ft == 2:
                        norm_stats(i + 1)
                    if more and ft == 4:
                        norm(i + 1)
                if more:
                    split_x(i + 1)
                if half_no:
                    for tb in range(TB2):
                        if tb == 0:
                            dve.wait_ge(part_in, 16 * (ck + 1))
                        dve.wait_ge(down_mm, TB2 * i + tb + 1)
                        dve.tensor_tensor(part[:, tb, :], po[tb % 2][:, :], part[:, tb, :], ALU.add).then_inc(o_evac, 1)
                        dve.wait_ge(o_evac, TB2 * i + tb + 1)
                        dve.bn_stats(ostats[:, tb, :], part[:, tb, :]).then_inc(ost_done, 1)
                        wait_first(dve, ost_done, TB2 * ck + tb + 1, dve_passed)
                        dve.bn_aggr(omv[:, tb, :], ostats[:, tb, :]).then_inc(omv_done, 1)
                    dve.wait_ge(orstd_done, ck + 1)
                    dve.wait_ge(res_in, 16 * (ck + 1))
                    for tb in range(TB2):
                        dve.tensor_scalar(part[:, tb, :], part[:, tb, :], omv[:, tb, 0:1], orstd[:, tb, :],
                                          ALU.subtract, ALU.mult).then_inc(o_normed, 1)
                    for tb in range(TB2):
                        dve.wait_ge(o_normed, TB2 * ck + tb + 1)
                        dve.tensor_tensor(res[:, tb, :], res[:, tb, :], part[:, tb, :], ALU.add).then_inc(o_done, 1)

            run(dve, weights, front, step)


_INS = ['L0_attn_hidden_states', 'L0_attn_W_in', 'L0_attn_b_in', 'L0_attn_conv_w', 'L0_attn_conv_b', 'L0_attn_W_x',
        'L0_attn_W_dt', 'L0_attn_b_dt', 'L0_attn_W_out', 'L0_attn_b_out', 'L0_attn_a_log', 'L0_attn_d_param',
        'L0_ffn_SU_ug', 'L0_ffn_SU_dp', 'L0_ffn_Wscale_ug', 'L0_ffn_Wscale_dp', 'L0_ffn_W_up', 'L0_ffn_W_gate',
        'L0_ffn_W_down']


def kernel(**inputs):
    import numpy as np
    import concourse.bacc as bacc
    from concourse.bass_utils import run_bass_kernel_spmd

    nc = bacc.Bacc("TRN2", target_bir_lowering=False, num_devices=1)
    arrays, W = {}, {}

    def give(name, a):
        a = np.ascontiguousarray(a)
        arrays[f"in_{name}"] = a
        W[name] = nc.dram_tensor(f"in_{name}", a.shape, mybir.dt.from_np(a.dtype), kind="ExternalInput").ap()

    by_partition = ("b_in", "conv_b", "b_dt", "d_param", "SU_ug", "SU_dp", "Wscale_ug")
    for name in _INS:
        short = name.replace("L0_attn_", "").replace("L0_ffn_", "")
        a = np.asarray(inputs[name])
        if short == "conv_w":
            a = a.reshape(KC, DT, P).transpose(2, 1, 0)
        elif short == "a_log":
            a = a.reshape(DT, P, NST).transpose(1, 0, 2)
        elif short in ("W_up", "W_gate", "W_down"):
            a = a.T
        elif short in by_partition:
            a = a.reshape(-1, P).T
        give(short, a)
    give("ident", np.eye(P, dtype=np.float32))
    h = np.ones((1, 1), np.float32)
    while len(h) < P:
        h = np.block([[h, h], [h, -h]])
    give("h128", h)
    give("ones", np.ones((1, P), np.float32))
    out = nc.dram_tensor("out", (TOK, DM), F32, kind="ExternalOutput").ap()
    scratch_bc = nc.dram_tensor("scratch_bc", (NCH, 2 * NST, T), F32, kind="Internal").ap()
    x = W["hidden_states"].rearrange("b l m -> (b l) m").rearrange("(c t) m -> c t m", t=T)
    x2 = nc.dram_tensor("scratch_x2", (TOK, DM), F32, kind="Internal").ap()
    scratch_w = [nc.dram_tensor(f"scratch_w_{n}", shape, F32, kind="Internal").ap()
                 for n, shape in (("up", (DM, FF)), ("gate", (DM, FF)), ("down", (FF, DM)))]
    scratch_part = nc.dram_tensor("scratch_part", (NCH2, T2, DM), F32, kind="Internal").ap()
    hadamard_block(nc, W, scratch_w)
    mamba_block(nc, x, W, scratch_bc, x2.rearrange("(c t) m -> c t m", t=T))
    ffn_block(nc, x2.rearrange("(c t) m -> c t m", t=T2), W, scratch_w, scratch_part,
              out.rearrange("(c t) m -> c t m", t=T2))
    r = run_bass_kernel_spmd(nc, [arrays], core_ids=[0])
    return r.results[0]["out"].reshape(BATCH, SEQ, DM)
```

```python
import concourse.bass as bass
from concourse import mybir
from contextlib import ExitStack

F32 = mybir.dt.float32
F32R = mybir.dt.float32r
ALU = mybir.AluOpType
ACT = mybir.ActivationFunctionType

P = 128
DM, DI, NST, DTR, KC = 512, 1024, 16, 128, 4
FF = 2048
BATCH, SEQ = 4, 1024
TOK = BATCH * SEQ
EPS = 1e-5
BIG = 3.0e38

T = 256
TB = T // P
NCH = TOK // T
CPB = SEQ // T
KT = DM // P
DT = DI // P
HALO = KC - 1


def wait_first(eng, sem, value, passed):
    eng.wait_ge(sem, value)
    eng.sem_inc(passed, 1)


def mamba_block(nc, x, W, scratch_bc, x2):
    ctx = ExitStack()
    with ctx:
        def sb(name, shape, dt=F32):
            return ctx.enter_context(nc.sbuf_tensor(name, shape, dt))

        def pb(name, shape):
            return ctx.enter_context(nc.psum_tensor(name, shape, F32))

        def sem(name):
            return ctx.enter_context(nc.semaphore(name))

        w_in = sb("w_in", [P, KT, 2 * DI])
        w_x = sb("w_x", [P, DT, DTR + 2 * NST])
        w_dt = sb("w_dt", [P, DI])
        w_out = sb("w_out", [P, DT, DM])
        taps = sb("taps", [P, DT, KC])
        diag = sb("diag", [P, DT * KC, P])
        ident = sb("ident", [P, P])
        b_in = sb("b_in", [P, 2 * DT])
        b_conv = sb("b_conv", [P, DT])
        b_dt = sb("b_dt", [P, DT])
        d_skip = sb("d_skip", [P, DT])
        b_out = sb("b_out", [1, DM])
        ones = sb("ones", [1, P])
        a_neg = sb("a_neg", [P, DT, NST])
        lim = sb("lim", [P, NCH + 1, 2])
        lim_now = sb("lim_now", [P, 2])
        half = sb("half", [P, TB])
        xb = sb("xb", [P, TB, DM])
        stats = sb("stats", [P, TB, 6])
        mv = sb("mv", [P, TB, 2])
        veps = sb("veps", [P, TB])
        rstd = sb("rstd", [P, TB])
        stats2 = sb("stats2", [P, TB, 6])
        mv2 = sb("mv2", [P, TB, 2])
        veps2 = sb("veps2", [P, TB])
        rstd2 = sb("rstd2", [P, TB])
        shift2 = sb("shift2", [P, TB])
        xnT = [sb(f"xnT{i}", [P, KT, T]) for i in range(2)]
        hid = sb("hid", [P, DT, HALO + T])
        soft_e = hid[:, :, 0:T]
        soft_w = sb("soft_w", [P, DT, T])
        conv = [sb(f"conv{i}", [P, DT, T]) for i in range(2)]
        delta = [sb(f"delta{i}", [P, DT, T]) for i in range(2)]
        gate = sb("gate", [P, DT, T])
        u = sb("u", [P, DT, T])
        dtin = soft_w[:, 0, :]
        bc = soft_w[0:TB * 2 * NST, 1, 0:P]
        bcT = [sb(f"bcT{i}", [P, P // (2 * NST), 2 * NST]) for i in range(2)]
        NBG = 2
        NG = NST // NBG
        bb = [sb(f"bb{i}", [P, NBG, T]) for i in range(2)]
        dbx = [sb(f"dbx{i}", [P, DT, T]) for i in range(2)]
        h = [sb(f"h{i}", [P, DT, T]) for i in range(2)]
        da = sb("da", [P, DT, T])
        carry = sb("carry", [P, NST, DT])
        da0 = sb("da0", [P, NST, DT])
        acc = sb("acc", [P, TB, DI])

        hT = [pb(f"hT{i}", [P, DI]) for i in range(2)]
        pM = pb("pM", [P, 4, T])
        pX = pb("pX", [P, 2, DM])

        loaded = sem("loaded"); loaded_late = sem("loaded_late")
        setup_d = sem("setup_d"); setup_p = sem("setup_p"); setup_a = sem("setup_a")
        x_in = sem("x_in"); res_in = sem("res_in"); x2_stored = sem("x2_stored")
        stats_done = sem("stats_done"); mv_done = sem("mv_done"); veps_done = sem("veps_done")
        rstd_done = sem("rstd_done"); xn_done = sem("xn_done")
        halo_done = sem("halo_done"); lim_done = sem("lim_done")
        m_filled = sem("m_filled"); m_evac = sem("m_evac")
        conv_done = sem("conv_done"); gate_done = sem("gate_done")
        bc_stored = sem("bc_stored")
        bb_in = [sem("bb_in0"), sem("bb_in1")]
        e_done = sem("e_done"); w_done = sem("w_done"); q_done = sem("q_done"); ln_done = sem("ln_done")
        lq_done = sem("lq_done"); delta_done = sem("delta_done"); u_done = sem("u_done")
        da_done = sem("da_done"); da0_raw = sem("da0_raw"); da0_done = sem("da0_done")
        inject_done = sem("inject_done"); prod_done = sem("prod_done"); dbx_done = sem("dbx_done")
        half_done = sem("half_done"); scan_done = sem("scan_done")
        carry_done = sem("carry_done"); h_turned = sem("h_turned"); acc_done = sem("acc_done")
        y_turned = sem("y_turned"); y_skip = sem("y_skip"); y_gated = sem("y_gated"); out_mm = sem("out_mm")
        st2_done = sem("st2_done"); mv2_done = sem("mv2_done"); veps2_done = sem("veps2_done")
        rstd2_done = sem("rstd2_done"); shift2_done = sem("shift2_done"); res_done = sem("res_done")
        z_done = sem("z_done")
        NLOAD, NLATE = 8, 6
        sp_passed, pe_passed, dve_passed, pool_passed = (sem(f"{e}_passed") for e in ("sp", "pe", "dve", "pool"))

        FRONT_UNITS = ["xT"] * KT + ["hid"] * DT + ["conv"] * DT + ["dtin", "bcT"] + ["bc"] * TB + ["dt"] * DT
        U_FRONT, U_ALL = len(FRONT_UNITS), len(FRONT_UNITS) + DT
        assert U_FRONT % 4 == 0 and U_ALL % 4 == 0
        O_XT, O_HID, O_CONV = 0, KT, KT + DT
        O_DTIN = O_CONV + DT
        O_BCT = O_DTIN + 1
        O_BC = O_BCT + 1
        O_DT = O_BC + TB
        O_GATE = U_FRONT

        def unit(c, i):
            if isinstance(c, int) and c < 0:
                return i
            return c * U_ALL + (U_FRONT + i)

        def gate_unit(c, i, has_front):
            return unit(c, i + (O_GATE if has_front else 0))

        PE_GATES = {14: (0, 1), 15: (2, 3, 4, 5)}
        PE_GATES_LATE = {0: (6,), 1: (7,)}
        PE_HID = {3: (0, 1, 2), 4: (3, 4, 5), 5: (6, 7)}
        PE_CONV = {5: (0,), 6: (1, 2, 3), 7: (4, 5, 6), 8: (7,)}
        PE_OUT_FIRST = {9: range(3)}
        PE_OUT = {11: range(3, 7), 12: range(7, 11), 13: range(11, 15), 14: range(15, 18)}
        ACT_GATES_LATE_MID = {0: (0, 1)}
        ACT_GATES_LATE_END = {0: (2, 3), 1: (4, 5), 2: (6, 7)}
        ACT_HID_MID = {5: (2, 3), 6: (4, 5)}
        ACT_HID_END = {4: (0, 1), 6: (6, 7)}
        ACT_CONV_MID = {8: (2, 3)}
        ACT_CONV_END = {7: (0, 1), 8: (4, 5), 9: (6, 7)}
        block = ctx.enter_context(nc.Block())

        def schedule(iteration, front0, epilogue):
            front0()
            iteration(0, 0, False, True)

            def pair(p):
                for j in range(2):
                    iteration(2 * p + (1 + j), (1 + j) % 2, True, True)
            return pair, lambda: (iteration(NCH - 1, (NCH - 1) % 2, True, False), epilogue())

        def run(eng, iteration, front0, epilogue):
            pair, finish = schedule(iteration, front0, epilogue)
            with eng.Fori(0, (NCH - 2) // 2) as p:
                pair(p)
            finish()

        @block.sync
        def _(sp):
            sp.dma_start(xb[:, :, :], x[0, :, :].rearrange("(a p) m -> p a m", p=P)).then_inc(x_in, 16)
            w_in_dram = W["W_in"].rearrange("(k p) n -> p k n", p=P)
            for dst, src in ((ident[:, :], W["ident"]), (taps[:, :, :], W["conv_w"]), (b_in[:, :], W["b_in"]),
                             (b_conv[:, :], W["conv_b"]), (b_dt[:, :], W["b_dt"]), (d_skip[:, :], W["d_param"]),
                             (a_neg[:, :, :], W["a_log"]), (w_in[:, :, 0:DI], w_in_dram[:, :, 0:DI])):
                sp.dma_start(dst, src).then_inc(loaded, 16)
            for dst, src in ((w_x[:, :, :], W["W_x"].rearrange("(k p) n -> p k n", p=P)), (w_dt[:, :], W["W_dt"]),
                             (w_in[:, :, DI:], w_in_dram[:, :, DI:]),
                             (w_out[:, :, :], W["W_out"].rearrange("(k p) n -> p k n", p=P)),
                             (b_out[:, :], W["b_out"].rearrange("(a n) -> a n", a=1)), (ones[:, :], W["ones"])):
                sp.dma_start(dst, src).then_inc(loaded_late, 16)

            def b_rows(c, g):
                sp.dma_start(bb[g % 2][:, :, :],
                             scratch_bc[bass.ds(c, 1), NBG * g:NBG * (g + 1), :].broadcast_to([P, NBG, T])
                             ).then_inc(bb_in[g % 2], 16)

            def store_bc(c1):
                wait_first(sp, m_evac, unit(c1 - 1, O_BC + TB - 1) + 1, sp_passed)
                for tb in range(TB):
                    sp.dma_start(scratch_bc[bass.ds(c1, 1), :, tb * P:(tb + 1) * P].rearrange("a n t -> (a n) t"),
                                 bc[2 * NST * tb:2 * NST * (tb + 1), :]).then_inc(bc_stored, 16)

            def first_rows(c1, g, first):
                if g == 0:
                    wait_first(sp, bc_stored, 16 * TB * (c1 + 1), sp_passed)
                if not first:
                    wait_first(sp, dbx_done, (c1 - 1) * NST + NST - NBG + NBG * g, sp_passed)
                b_rows(c1, g)

            def front0():
                store_bc(0)
                for g in range(2):
                    first_rows(0, g, True)

            def iteration(c, par, has_back, has_front):
                if has_front:
                    if isinstance(c, int) and c == 0:
                        wait_first(sp, m_filled, KT, sp_passed)
                    elif not isinstance(c, int):
                        wait_first(sp, m_filled, unit(c - 1, O_XT + KT - 1) + 1, sp_passed)
                    sp.dma_start(xb[:, :, :], x[bass.ds(c + 1, 1), :, :].rearrange("q (a p) m -> p (q a) m", p=P)).then_inc(x_in, 16)

                def more_rows(groups):
                    for g in groups:
                        wait_first(sp, dbx_done, c * NST + NBG * (g - 1), sp_passed)
                        b_rows(c, g)

                more_rows(range(2, 4))
                if has_back:
                    if has_front:
                        wait_first(sp, m_filled, unit(c, O_XT + KT - 1) + 1, sp_passed)
                    sp.dma_start(xb[:, :, :], x[bass.ds(c - 1, 1), :, :].rearrange("q (a p) m -> p (q a) m", p=P)).then_inc(res_in, 16)
                more_rows(range(4, NG - 1))
                if has_front:
                    store_bc(c + 1)
                more_rows([NG - 1])
                if has_front:
                    first_rows(c + 1, 0, False)
                    first_rows(c + 1, 1, False)
                if has_back:
                    wait_first(sp, z_done, TB * c, sp_passed)
                    sp.dma_start(x2[bass.ds(c - 1, 1), :, :].rearrange("q (a p) m -> p (q a) m", p=P), xb[:, :, :]).then_inc(x2_stored, 16)
                    wait_first(sp, x2_stored, 16 * c, sp_passed)

            def epilogue():
                sp.dma_start(xb[:, :, :], x[NCH - 1, :, :].rearrange("(a p) m -> p a m", p=P)).then_inc(res_in, 16)
                wait_first(sp, z_done, TB * NCH, sp_passed)
                sp.dma_start(x2[NCH - 1, :, :].rearrange("(a p) m -> p a m", p=P), xb[:, :, :]).then_inc(x2_stored, 16)
                wait_first(sp, x2_stored, 16 * NCH, sp_passed)

            run(sp, iteration, front0, epilogue)

        @block.tensor
        def _(pe):
            def take(i, number):
                if i % 2 == 0 and not (isinstance(number, int) and number < 4):
                    pe.wait_ge(m_evac, number - 2)

            def slot_of(i):
                return i % 4

            def xT(c, kt, par):
                n = unit(c, O_XT + kt)
                if kt == 0:
                    pe.wait_ge(xn_done, TB * (c + 2))
                take(kt, n)
                for tb in range(TB):
                    mm = pe.transpose(pM[:, slot_of(O_XT + kt), tb * P:(tb + 1) * P],
                                      xb[:, tb, kt * P:(kt + 1) * P], ident[:, :])
                mm.then_inc(m_filled, 1)

            def in_proj(c, i, column, src):
                take(i, unit(c, i))
                for kt in range(KT):
                    mm = pe.matmul(pM[:, slot_of(i), :], w_in[:, kt, column:column + P], src[:, kt, :],
                                   start=(kt == 0), stop=(kt == KT - 1))
                mm.then_inc(m_filled, 1)

            def hidden(c, dt, par):
                if dt == 0:
                    pe.wait_ge(m_evac, unit(c, O_XT + KT - 1) + 1)
                in_proj(c, O_HID + dt, dt * P, xnT[1 - par])

            def conv_taps(c, dt):
                if dt % 2 == 0:
                    pe.wait_ge(m_evac, unit(c, O_HID + dt + 1) + 1)
                take(O_CONV + dt, unit(c, O_CONV + dt))
                for k in range(KC):
                    mm = pe.matmul(pM[:, slot_of(O_CONV + dt), :], diag[:, dt * KC + k, :], hid[:, dt, k:k + T],
                                   start=(k == 0), stop=(k == KC - 1))
                mm.then_inc(m_filled, 1)

            def x_proj(c, par):
                pe.wait_ge(conv_done, c + 2)
                take(O_DTIN, unit(c, O_DTIN))
                for dt in range(DT):
                    mm = pe.matmul(pM[:, slot_of(O_DTIN), :], w_x[:, dt, 0:DTR], conv[1 - par][:, dt, :],
                                   start=(dt == 0), stop=(dt == DT - 1))
                mm.then_inc(m_filled, 1)

            def bc_proj(c, par):
                for tb in range(TB):
                    for dt in range(DT):
                        mm = pe.matmul(pM[:, slot_of(O_BCT), tb * 2 * NST:(tb + 1) * 2 * NST],
                                       conv[1 - par][:, dt, tb * P:(tb + 1) * P], w_x[:, dt, DTR:],
                                       start=(dt == 0), stop=(dt == DT - 1))
                mm.then_inc(m_filled, 1)

            def turn_bc(c, par):
                pe.wait_ge(m_evac, unit(c, O_BCT) + 1)
                for tb in range(TB):
                    take(O_BC + tb, unit(c, O_BC + tb))
                    pe.transpose(pM[:, slot_of(O_BC + tb), 0:P], bcT[1 - par][:, :, :].rearrange("p a n -> p (a n)"),
                                 ident[:, :]).then_inc(m_filled, 1)

            def dt_proj(c, par):
                for dt in range(DT):
                    take(O_DT + dt, unit(c, O_DT + dt))
                    pe.matmul(pM[:, slot_of(O_DT + dt), :], w_dt[:, dt * P:(dt + 1) * P], dtin[:, :],
                              start=True, stop=True).then_inc(m_filled, 1)

            def gates(c, dt, par, has_front):
                n = gate_unit(c, dt, has_front)
                take(dt, n)
                for kt in range(KT):
                    mm = pe.matmul(pM[:, slot_of(dt), :], w_in[:, kt, DI + dt * P:DI + (dt + 1) * P], xnT[par][:, kt, :],
                                   start=(kt == 0), stop=(kt == KT - 1))
                mm.then_inc(m_filled, 1)

            def turn_h(c, n):
                for tb in range(TB):
                    i = TB * n + tb
                    if tb == 0:
                        pe.wait_ge(scan_done, c * (NST * 2) + 2 * (n + 1))
                    if not (isinstance(c, int) and c == 0 and i < 2):
                        pe.wait_ge(acc_done, c * (NST * TB) + i - 1)
                    for dt in range(DT):
                        mm = pe.transpose(hT[i % 2][:, dt * P:(dt + 1) * P], h[n % 2][:, dt, tb * P:(tb + 1) * P], ident[:, :])
                    mm.then_inc(h_turned, 1)

            def turn_y(c):
                pe.wait_ge(acc_done, c * (NST * TB))
                for j in range(DT // 2):
                    if j >= 2:
                        pe.wait_ge(y_skip, (c - 1) * DT + 2 * (j - 1))
                    for a in range(2):
                        for tb in range(TB):
                            mm = pe.transpose(pX[:, j % 2, a * T + tb * P:a * T + (tb + 1) * P],
                                              acc[:, tb, (2 * j + a) * P:(2 * j + a + 1) * P], ident[:, :])
                    mm.then_inc(y_turned, 1)

            def out_proj(c, steps):
                for i in steps:
                    tb, dt = divmod(i, DT + 1)
                    if i == 0:
                        pe.wait_ge(y_gated, c)
                    if dt < DT:
                        pe.matmul(pX[:, tb, :], gate[:, dt, tb * P:(tb + 1) * P], w_out[:, dt, :], start=(dt == 0), stop=False)
                    else:
                        pe.matmul(pX[:, tb, :], ones[:, :], b_out[:, :], start=False, stop=True).then_inc(out_mm, 1)

            def iteration(c, par, has_back, has_front):
                for n in range(NST):
                    if n:
                        turn_h(c, n - 1)
                    elif has_back:
                        turn_h(c - 1, NST - 1)
                    if has_back:
                        if n == 1:
                            turn_y(c)
                        for dt in PE_GATES_LATE.get(n, ()):
                            gates(c - 1, dt, 1 - par, True)
                        out_proj(c, PE_OUT_FIRST.get(n, ()))
                    if has_front:
                        if n == 2:
                            for kt in range(KT):
                                xT(c, kt, par)
                        for dt in PE_HID.get(n, ()):
                            hidden(c, dt, par)
                        for dt in PE_CONV.get(n, ()):
                            conv_taps(c, dt)
                        if n == 9:
                            x_proj(c, par)
                        if n == 10:
                            bc_proj(c, par)
                        if n == 11:
                            turn_bc(c, par)
                            dt_proj(c, par)
                    if has_back:
                        out_proj(c, PE_OUT.get(n, ()))
                    for dt in PE_GATES.get(n, ()):
                        gates(c, dt, par, has_front)

            def front0():
                pe.wait_ge(loaded, 16 * NLOAD)
                for kt in range(KT):
                    xT(-1, kt, 1)
                for dt in range(DT):
                    hidden(-1, dt, 1)
                pe.wait_ge(setup_d, DT * KC)
                for dt in range(DT):
                    conv_taps(-1, dt)
                pe.wait_ge(loaded_late, 16 * NLATE)
                x_proj(-1, 1)
                bc_proj(-1, 1)
                turn_bc(-1, 1)
                dt_proj(-1, 1)

            def epilogue():
                turn_h(NCH - 1, NST - 1)
                for dt in sum(PE_GATES_LATE.values(), ()):
                    gates(NCH - 1, dt, (NCH - 1) % 2, False)
                turn_y(NCH)
                out_proj(NCH, range(TB * (DT + 1)))

            run(pe, iteration, front0, epilogue)

        @block.scalar
        def _(act):
            def full(i, number):
                act.wait_ge(m_filled, number + (2 if i % 2 == 0 else 1))

            def xT(c, par):
                for kt in range(KT):
                    full(kt, unit(c, O_XT + kt))
                    act.activation(xnT[1 - par][:, kt, :], pM[:, kt, :], ACT.Copy).then_inc(m_evac, 1)

            def hidden(c, dt, par):
                if dt == 0:
                    act.wait_ge(halo_done, c + 2)
                full(O_HID + dt, unit(c, O_HID + dt))
                act.activation(hid[:, dt, HALO:], pM[:, (O_HID + dt) % 4, :], ACT.Identity,
                               bias=b_in[:, dt:dt + 1]).then_inc(m_evac, 1)

            def conv_out(c, dt, par):
                if dt == 0 and not (isinstance(c, int) and c < 1):
                    act.wait_ge(y_gated, c)
                full(O_CONV + dt, unit(c, O_CONV + dt))
                act.activation(conv[1 - par][:, dt, :], pM[:, (O_CONV + dt) % 4, :], ACT.Identity,
                               bias=b_conv[:, dt:dt + 1]).then_inc(m_evac, 1)

            def conv_silu(c, par):
                act.wait_ge(m_evac, unit(c, O_CONV + DT - 1) + 1)
                act.activation(conv[1 - par][:, :, :], conv[1 - par][:, :, :], ACT.Silu).then_inc(conv_done, 1)

            def x_proj(c, par):
                full(O_DTIN, unit(c, O_DTIN))
                if not (isinstance(c, int) and c < 0):
                    act.wait_ge(delta_done, c + 1)
                act.activation(dtin[:, :], pM[:, O_DTIN % 4, :], ACT.Copy).then_inc(m_evac, 1)
                full(O_BCT, unit(c, O_BCT))
                act.activation(bcT[1 - par][:, 0:TB, :],
                               pM[:, O_BCT % 4, 0:TB * 2 * NST].rearrange("p (a n) -> p a n", a=TB), ACT.Copy).then_inc(m_evac, 1)

            def turn_bc(c):
                for tb in range(TB):
                    rows = slice(tb * 2 * NST, (tb + 1) * 2 * NST)
                    full(O_BC + tb, unit(c, O_BC + tb))
                    act.activation(bc[rows, :], pM[rows, (O_BC + tb) % 4, 0:P], ACT.Copy).then_inc(m_evac, 1)

            def dt_proj(c, par):
                for dt in range(DT):
                    full(O_DT + dt, unit(c, O_DT + dt))
                    act.activation(delta[1 - par][:, dt, :], pM[:, (O_DT + dt) % 4, :], ACT.Identity,
                                   bias=b_dt[:, dt:dt + 1]).then_inc(m_evac, 1)

            def soft_abs(c, par):
                act.wait_ge(m_evac, unit(c, O_DT + DT - 1) + 1)
                act.activation(soft_e, delta[1 - par][:, :, :], ACT.Abs).then_inc(e_done, 1)

            def soft_exp(c):
                act.wait_ge(e_done, 2 * (c + 1) + 1)
                act.activation(soft_e, soft_e, ACT.Exp, scale=-1.0).then_inc(e_done, 1)

            def soft_ln(c):
                act.wait_ge(q_done, c + 2)
                act.activation(soft_w[:, :, :], soft_w[:, :, :], ACT.Ln).then_inc(ln_done, 1)

            def first_decay(c):
                act.wait_ge(da0_raw, c + 2)
                act.activation(da0[:, :, :], da0[:, :, :], ACT.Exp).then_inc(da0_done, 1)

            def exps(c, n, par, hf):
                if n == 0 and hf == 0:
                    act.wait_ge(delta_done, c + 1)
                if not (isinstance(c, int) and c == 0 and n == 0):
                    act.wait_ge(scan_done, c * (NST * 2) + 2 * n + hf - 1)
                for dt in range(hf * DT // 2, (hf + 1) * DT // 2):
                    e = act.activation(da[:, dt, 1:], delta[par][:, dt, 1:], ACT.Exp, scale=a_neg[:, dt, n:n + 1])
                e.then_inc(da_done, 1)

            def gates(c, dt, has_front):
                if dt == 0 and not (isinstance(c, int) and c == 0):
                    act.wait_ge(out_mm, TB * c)
                full(dt, gate_unit(c, dt, has_front))
                act.activation(gate[:, dt, :], pM[:, dt % 4, :], ACT.Identity,
                               bias=b_in[:, DT + dt:DT + dt + 1]).then_inc(m_evac, 1)

            def late_gates(c, has_front, which):
                for dt in which:
                    gates(c, dt, has_front)
                if which and which[-1] == DT - 1:
                    act.wait_ge(m_evac, gate_unit(c, DT - 1, has_front) + 1)
                    act.activation(gate[:, :, :], gate[:, :, :], ACT.Silu).then_inc(gate_done, 1)

            def iteration(c, par, has_back, has_front):
                for n in range(NST):
                    if n == 0 and not (isinstance(c, int) and c == 0):
                        first_decay(c - 1)
                    exps(c, n, par, 0)
                    if has_back:
                        late_gates(c - 1, True, ACT_GATES_LATE_MID.get(n, ()))
                    if has_front:
                        for dt in ACT_HID_MID.get(n, ()):
                            hidden(c, dt, par)
                        for dt in ACT_CONV_MID.get(n, ()):
                            conv_out(c, dt, par)
                        if n == 12:
                            turn_bc(c)
                    exps(c, n, par, 1)
                    if has_back:
                        late_gates(c - 1, True, ACT_GATES_LATE_END.get(n, ()))
                    if has_front:
                        if n == 3:
                            xT(c, par)
                        for dt in ACT_HID_END.get(n, ()):
                            hidden(c, dt, par)
                        for dt in ACT_CONV_END.get(n, ()):
                            conv_out(c, dt, par)
                        if n == 9:
                            conv_silu(c, par)
                        if n == 11:
                            x_proj(c, par)
                        if n == 12:
                            dt_proj(c, par)
                            soft_abs(c, par)
                            soft_exp(c)
                        if n == 13:
                            soft_ln(c)

            def front0():
                act.wait_ge(loaded, 16 * NLOAD)
                act.activation(a_neg[:, :, :], a_neg[:, :, :], ACT.Exp).then_inc(setup_a, 1)
                xT(-1, 1)
                for dt in range(DT):
                    hidden(-1, dt, 1)
                for dt in range(DT):
                    conv_out(-1, dt, 1)
                conv_silu(-1, 1)
                x_proj(-1, 1)
                turn_bc(-1)
                dt_proj(-1, 1)
                soft_abs(-1, 1)
                soft_exp(-1)
                soft_ln(-1)
                act.wait_ge(setup_d, DT * KC + 1)
                first_decay(-1)

            def epilogue():
                late_gates(NCH - 1, False, range(DT))

            run(act, iteration, front0, epilogue)

        @block.vector
        def _(dve):
            def norm_stats(c):
                dve.wait_ge(x_in, 16 * (c + 2))
                for tb in range(TB):
                    dve.bn_stats(stats[:, tb, :], xb[:, tb, :]).then_inc(stats_done, 1)
                for tb in range(TB):
                    wait_first(dve, stats_done, TB * (c + 1) + tb + 1, dve_passed)
                    dve.bn_aggr(mv[:, tb, :], stats[:, tb, :]).then_inc(mv_done, 1)

            def norm(c):
                dve.wait_ge(rstd_done, c + 2)
                for tb in range(TB):
                    dve.tensor_scalar(xb[:, tb, :], xb[:, tb, :], mv[:, tb, 0:1], rstd[:, tb:tb + 1],
                                      ALU.subtract, ALU.mult).then_inc(xn_done, 1)

            def halo(c):
                if not (isinstance(c, int) and c < 1):
                    dve.wait_ge(carry_done, c * NST)
                dve.tensor_copy(lim_now[:, :], lim[:, bass.ds(c + 1, 1), :].rearrange("p a b -> p (a b)")).then_inc(lim_done, 1)
                dve.wait_ge(lim_done, c + 2)
                if not (isinstance(c, int) and c < 0):
                    dve.wait_ge(m_evac, unit(c - 1, O_DT + DT - 1) + 1)
                dve.tensor_scalar(hid[:, :, 0:HALO], hid[:, :, T:T + HALO], lim_now[:, 0:1], lim_now[:, 1:2],
                                  ALU.max, ALU.min).then_inc(halo_done, 1)

            def soft_q(c):
                dve.wait_ge(w_done, c + 2)
                dve.scalar_tensor_tensor(soft_e, soft_w[:, :, :], -1.0, soft_e, ALU.add, ALU.subtract).then_inc(q_done, 1)

            def soft_end(c, par):
                dve.wait_ge(ln_done, c + 2)
                dve.tensor_tensor(soft_w[:, :, :], soft_w[:, :, :], soft_e, ALU.subtract).then_inc(lq_done, 1)
                dve.wait_ge(lq_done, c + 2)
                dve.scalar_tensor_tensor(delta[1 - par][:, :, :], delta[1 - par][:, :, :], 0.0, soft_w[:, :, :],
                                         ALU.max, ALU.add).then_inc(delta_done, 1)

            def scans(c, n):
                if n:
                    dve.wait_ge(dbx_done, c * NST + n + 1)
                if not (isinstance(c, int) and c == 0 and n < 2):
                    dve.wait_ge(h_turned, c * (NST * TB) + TB * (n - 1))
                    dve.wait_ge(carry_done, c * NST + n - 1)
                for hf in range(2):
                    tiles = slice(hf * DT // 2, (hf + 1) * DT // 2)
                    row = lambda t: t[:, tiles, :].rearrange("p d t -> p (d t)")
                    dve.wait_ge(da_done, c * (NST * 2) + 2 * n + hf + 1)
                    if n == 0:
                        dve.wait_ge(*((half_done, c + 1) if hf == 0 else (dbx_done, c * NST + 1)))
                    dve.tensor_tensor_scan(row(h[n % 2]), row(da), row(dbx[n % 2]), 0.0,
                                           ALU.mult, ALU.add).then_inc(scan_done, 1)

            def save(c, n):
                dve.wait_ge(scan_done, c * (NST * 2) + 2 * (n + 1))
                if not (isinstance(c, int) and c == 0):
                    dve.wait_ge(dbx_done, c * NST + n + 1)
                dve.tensor_scalar(carry[:, n, :], h[n % 2][:, :, T - 1], lim_now[:, 1:2], lim_now[:, 0:1],
                                  ALU.min, ALU.max).then_inc(carry_done, 1)

            def add_h(c, n, par):
                for tb in range(TB):
                    i = TB * n + tb
                    cn = bcT[par][:, tb, NST + n:NST + n + 1]
                    dve.wait_ge(h_turned, c * (NST * TB) + i + 1)
                    if n == 0:
                        if not (isinstance(c, int) and c == 0):
                            dve.wait_ge(y_turned, (DT // 2) * c)
                        dve.tensor_scalar(acc[:, tb, :], hT[i % 2][:, :], cn, None, ALU.mult).then_inc(acc_done, 1)
                    else:
                        dve.wait_ge(acc_done, c * (NST * TB) + i - TB + 1)
                        dve.scalar_tensor_tensor(acc[:, tb, :], hT[i % 2][:, :], cn, acc[:, tb, :],
                                                 ALU.mult, ALU.add).then_inc(acc_done, 1)

            def skip(c, par):
                for j in range(DT // 2):
                    dve.wait_ge(y_turned, (DT // 2) * (c - 1) + j + 1)
                    for a in range(2):
                        dt = 2 * j + a
                        dve.scalar_tensor_tensor(conv[1 - par][:, dt, :], conv[1 - par][:, dt, :], d_skip[:, dt:dt + 1],
                                                 pX[:, j % 2, a * T:(a + 1) * T], ALU.mult, ALU.add).then_inc(y_skip, 1)

            def out_stats(c, tb):
                dve.wait_ge(out_mm, TB * (c - 1) + tb + 1)
                dve.bn_stats(stats2[:, tb, :], pX[:, tb, :]).then_inc(st2_done, 1)
                wait_first(dve, st2_done, TB * (c - 1) + tb + 1, dve_passed)
                dve.bn_aggr(mv2[:, tb, :], stats2[:, tb, :]).then_inc(mv2_done, 1)

            def out_norm(c):
                dve.wait_ge(rstd2_done, c)
                dve.wait_ge(res_in, 16 * c)
                for tb in range(TB):
                    dve.scalar_tensor_tensor(shift2[:, tb:tb + 1], mv2[:, tb, 0:1], -1.0, rstd2[:, tb:tb + 1],
                                             ALU.mult, ALU.mult).then_inc(shift2_done, 1)
                for tb in range(TB):
                    dve.wait_ge(shift2_done, TB * (c - 1) + tb + 1)
                    dve.tensor_scalar(xb[:, tb, :], xb[:, tb, :], shift2[:, tb:tb + 1], None, ALU.add).then_inc(res_done, 1)
                for tb in range(TB):
                    dve.wait_ge(res_done, TB * (c - 1) + tb + 1)
                    dve.scalar_tensor_tensor(xb[:, tb, :], pX[:, tb, :], rstd2[:, tb:tb + 1], xb[:, tb, :],
                                             ALU.mult, ALU.add).then_inc(z_done, 1)

            def iteration(c, par, has_back, has_front):
                for n in range(NST):
                    if n == 1 and has_front:
                        norm_stats(c)
                    if has_back and n == 0:
                        add_h(c - 1, NST - 1, 1 - par)
                        save(c - 1, NST - 1)
                    if n == 0 and has_front:
                        halo(c)
                    scans(c, n)
                    if n == 2 and has_front:
                        norm(c)
                    if has_back and n == 1:
                        skip(c, par)
                    if n:
                        add_h(c, n - 1, par)
                        save(c, n - 1)
                    if has_back and n in (13, 14):
                        out_stats(c, n - 13)
                    if has_back and n == 15:
                        out_norm(c)
                    if has_front and n == 12:
                        soft_q(c)
                    if has_front and n == 13:
                        soft_end(c, par)

            def front0():
                dve.wait_ge(setup_p, 7 + NCH // CPB + 1)
                norm_stats(-1)
                halo(-1)
                norm(-1)
                dve.wait_ge(loaded, 16 * NLOAD)
                for dt in range(DT):
                    for k in range(KC):
                        dve.tensor_scalar(diag[:, dt * KC + k, :], ident[:, :], taps[:, dt, k:k + 1], None,
                                          ALU.mult).then_inc(setup_d, 1)
                dve.wait_ge(setup_a, 1)
                dve.tensor_scalar(a_neg[:, :, :], a_neg[:, :, :], -1.0, None, ALU.mult).then_inc(setup_d, 1)
                soft_q(-1)
                soft_end(-1, 1)

            def epilogue():
                add_h(NCH - 1, NST - 1, (NCH - 1) % 2)
                skip(NCH, NCH % 2)
                for tb in range(TB):
                    out_stats(NCH, tb)
                out_norm(NCH)

            run(dve, iteration, front0, epilogue)

        @block.gpsimd
        def _(pool):
            def rsqrt(c, which):
                m, ve, r, sm, sv, sr = ((mv, veps, rstd, mv_done, veps_done, rstd_done),
                                        (mv2, veps2, rstd2, mv2_done, veps2_done, rstd2_done))[which]
                wait_first(pool, sm, TB * (c + 1), pool_passed)
                pool.tensor_scalar(ve[:, :], m[:, :, 1], EPS, 1.0, ALU.add, ALU.mult).then_inc(sv, 1)
                pool.wait_ge(sv, c + 1)
                pool.tensor_tensor(r[:, :], ve[:, :], half[:, :], ALU.pow).then_inc(sr, 1)

            def make_u(c, par, i):
                tiles = slice(i * DT // 2, (i + 1) * DT // 2)
                if i == 0:
                    pool.wait_ge(delta_done, c + 2)
                    if not (isinstance(c, int) and c < 0):
                        pool.wait_ge(dbx_done, NST * (c + 1))
                pool.tensor_tensor(u[:, tiles, :], delta[par][:, tiles, :], conv[par][:, tiles, :], ALU.mult).then_inc(u_done, 1)

            def product(c, n, tiles, done, products, states):
                g = n // NBG
                first = isinstance(c, int) and c == 0
                rows = bb[g % 2][:, n % NBG:n % NBG + 1, :].broadcast_to([P, tiles.stop - tiles.start, T])
                to = dbx[n % 2]
                pool.tensor_tensor(to[:, tiles, :], u[:, tiles, :], rows, ALU.mult).then_inc(done if first else prod_done, 1)
                if first:
                    return
                if states is not None:
                    pool.wait_ge(carry_done, states)
                    pool.tensor_tensor(da0[:, n, :], da0[:, n, :], carry[:, n, :], ALU.mult).then_inc(inject_done, 1)
                    pool.wait_ge(inject_done, states)
                pool.wait_ge(prod_done, products)
                pool.tensor_tensor(to[:, tiles, 0], to[:, tiles, 0], da0[:, n, tiles], ALU.add).then_inc(done, 1)

            def first_product(c, par, i):
                if i == 0:
                    pool.wait_ge(bb_in[0], 16 * ((NG // 2) * c + 1))
                    if not (isinstance(c, int) and c == 0):
                        pool.wait_ge(scan_done, (c - 1) * (NST * 2) + 2 * (NST - 1))
                make_u(c - 1, par, i)
                pool.wait_ge(u_done, 2 * c + i + 1)
                if i == 0 and not (isinstance(c, int) and c == 0):
                    pool.wait_ge(da0_done, c + 1)
                product(c, 0, slice(i * DT // 2, (i + 1) * DT // 2), (half_done, dbx_done)[i],
                        (c - 1) * (NST + 1) + i + 1, (c - 1) * NST + 1 if i == 0 else None)

            def b_times_u(c, n, par):
                g = n // NBG
                if n % NBG == 0:
                    pool.wait_ge(bb_in[g % 2], 16 * ((NG // 2) * c + g // 2 + 1))
                if not (isinstance(c, int) and c == 0 and n < 2):
                    pool.wait_ge(scan_done, c * (NST * 2) + 2 * (n - 1))
                product(c, n, slice(0, DT), dbx_done, (c - 1) * (NST + 1) + n + 2, (c - 1) * NST + n + 1)

            def decay0(c, par):
                pool.wait_ge(delta_done, c + 2)
                if not (isinstance(c, int) and c == -1):
                    pool.wait_ge(dbx_done, NST * (c + 1))
                if isinstance(c, int) and c == -1:
                    pool.wait_ge(setup_d, DT * KC + 1)
                pool.tensor_tensor(da0[:, :, :], a_neg[:, :, :].rearrange("p d n -> p n d"),
                                   delta[1 - par][:, :, 0:1].rearrange("p d a -> p a d").broadcast_to([P, NST, DT]),
                                   ALU.mult).then_inc(da0_raw, 1)

            def one_plus_e(c):
                pool.wait_ge(e_done, 2 * (c + 2))
                wait_first(pool, bc_stored, 16 * TB * (c + 2), pool_passed)
                pool.tensor_scalar(soft_w[:, :, :], soft_e, 1.0, 1.0, ALU.add, ALU.mult).then_inc(w_done, 1)

            def gating(c, par):
                pool.wait_ge(y_skip, DT * c)
                pool.wait_ge(gate_done, c)
                pool.tensor_tensor(gate[:, :, :], conv[1 - par][:, :, :], gate[:, :, :], ALU.mult).then_inc(y_gated, 1)

            def iteration(c, par, has_back, has_front):
                first_product(c, par, 1)
                for n in range(NST):
                    if n:
                        b_times_u(c, n, par)
                    if n == 3 and has_front:
                        rsqrt(c + 1, 0)
                    if n == 4 and has_back:
                        gating(c, par)
                    if has_front and n == 13:
                        one_plus_e(c)
                if has_front:
                    decay0(c, par)
                    first_product(c + 1, 1 - par, 0)
                if has_back:
                    rsqrt(c - 1, 1)

            def front0():
                pool.memset(hid[:, :, :], 0.0).then_inc(setup_p, 1)
                pool.memset(da[:, :, 0:1], 0.0).then_inc(setup_p, 1)
                for t in bcT:
                    pool.memset(t[:, TB:, :], 0.0).then_inc(setup_p, 1)
                pool.memset(half[:, :], -0.5).then_inc(setup_p, 1)
                pool.memset(lim[:, :, 0:1], -BIG).then_inc(setup_p, 1)
                pool.memset(lim[:, :, 1:2], BIG).then_inc(setup_p, 1)
                pool.wait_ge(setup_p, 7)
                for c in range(0, NCH + 1, CPB):
                    pool.memset(lim[:, c, :], 0.0).then_inc(setup_p, 1)
                rsqrt(0, 0)
                one_plus_e(-1)
                decay0(-1, 1)
                first_product(0, 0, 0)

            def epilogue():
                gating(NCH, NCH % 2)
                rsqrt(NCH - 1, 1)

            run(pool, iteration, front0, epilogue)


HT = FF // P
T2 = 512
TB2 = T2 // P
NCH2 = TOK // T2
HALVES = 2
FH = FF // HALVES
FT = FH // P


def hadamard_block(nc, W, scratch_w):
    ctx = ExitStack()
    with ctx:
        def sb(name, shape, dt=F32):
            return ctx.enter_context(nc.sbuf_tensor(name, shape, dt))

        def sem(name):
            return ctx.enter_context(nc.semaphore(name))

        TILES = 16
        JOBS = (("up", (4, 8)), ("gate", (4, 8)), ("down", (1, 2, 4, 8)))
        buf = [sb(f"had{i}", [P, TILES, DM]) for i in range(4)]
        GROUP = 4
        NS = 3
        scaled = [sb(f"scaled{i}", [P, GROUP, DM]) for i in range(NS)]
        h128 = sb("h128", [P, P])
        su_ug = sb("su_ug", [P, KT])
        su_dp = sb("su_dp", [P, HT])
        wscale = sb("wscale", [P, DM])
        ps = [ctx.enter_context(nc.psum_tensor(f"had_ps{i}", [P, DM], F32)) for i in range(4)]
        w_in = [sem(f"hw_in{i}") for i in range(len(JOBS))]
        small_in = sem("small_in")
        su_done = sem("su_done")
        plus_done = sem("plus_done")
        minus_done = sem("minus_done")
        mm_done = sem("mm_done")
        evac = sem("had_evac")
        down_evac = sem("had_down_evac")
        stored = [sem(f"had_stored{i}") for i in range(NS)]
        plan = []
        for j, (name, strides) in enumerate(JOBS):
            chain = [j]
            for s in range(len(strides)):
                chain.append(3 if s % 2 == 0 else j)
            plan.append(chain)
        before = [sum(len(s) for _, s in JOBS[:j]) for j in range(len(JOBS) + 1)]
        CUT = 3
        block = ctx.enter_context(nc.Block())

        def wait_buffer(eng, i):
            g = i // GROUP
            if i % GROUP == 0 and g >= NS:
                eng.wait_ge(stored[g % NS], 16 * (g // NS))

        def halves(t, stride):
            v = t[:, :, :].rearrange("p (g two s) m -> p g two (s m)", two=2, s=stride)
            return v[:, :, 0, :], v[:, :, 1, :]

        @block.sync
        def _(sp):
            for dst, src in ((h128[:, :], W["h128"]), (su_ug[:, :], W["SU_ug"]), (su_dp[:, :], W["SU_dp"]),
                             (wscale[:, :], W["Wscale_dp"].rearrange("(a n) -> a n", a=1).broadcast_to([P, DM]))):
                sp.dma_start(dst, src).then_inc(small_in, 16)
            for j, name in enumerate(("W_up", "W_gate")):
                sp.dma_start(buf[j][:, :, :].rearrange("p (k q) m -> p k (q m)", k=KT),
                             W[name].rearrange("(k p) f -> p k f", p=P)).then_inc(w_in[j], 16)
            sp.dma_start(buf[2][:, :, :], W["W_down"].rearrange("(k p) m -> p k m", p=P)).then_inc(w_in[2], 16)
            for g in range(len(JOBS) * TILES // GROUP):
                j, k = divmod(g, TILES // GROUP)
                sp.wait_ge(*((evac, GROUP * (g + 1)) if j < 2 else (down_evac, GROUP * (k + 1))))
                if j < 2:
                    dst = scratch_w[j][k * P:(k + 1) * P, :].rearrange("p (q m) -> p q m", q=GROUP)
                else:
                    dst = scratch_w[j][k * GROUP * P:(k + 1) * GROUP * P, :].rearrange("(q p) m -> p q m", p=P)
                sp.dma_start(dst, scaled[g % NS][:, :, :]).then_inc(stored[g % NS], 16)
            for i in range(NS):
                sp.wait_ge(stored[i], 16 * len(JOBS) * TILES // GROUP // NS)

        def butterflies(eng, j, s, mine):
            stride = JOBS[j][1][s]
            src, dst = buf[plan[j][s]], buf[plan[j][s + 1]]
            if s == 0:
                eng.wait_ge(w_in[j], 16)
            done = before[j] + s
            if done:
                eng.wait_ge(plus_done, done)
                eng.wait_ge(minus_done, done)
            (s0, s1), (d0, d1) = halves(src, stride), halves(dst, stride)
            cut = stride * DM * CUT // 8
            if mine == "plus":
                eng.tensor_tensor(d0, s0, s1, ALU.add)
                eng.tensor_tensor(d1[:, :, 0:cut], s0[:, :, 0:cut], s1[:, :, 0:cut], ALU.subtract).then_inc(plus_done, 1)
            else:
                eng.tensor_tensor(d1[:, :, cut:], s0[:, :, cut:], s1[:, :, cut:], ALU.subtract).then_inc(minus_done, 1)

        @block.vector
        def _(dve):
            dve.wait_ge(small_in, 64)
            dve.tensor_scalar(su_ug[:, :], su_ug[:, :], float(DM) ** -0.5, None, ALU.mult).then_inc(su_done, 1)
            dve.tensor_scalar(su_dp[:, :], su_dp[:, :], float(FF) ** -0.5, None, ALU.mult).then_inc(su_done, 1)
            for j in range(len(JOBS)):
                for s in range(len(JOBS[j][1])):
                    butterflies(dve, j, s, "plus")
            for t in range(TILES):
                i = 2 * TILES + t
                dve.wait_ge(mm_done, i + 1)
                wait_buffer(dve, i)
                dve.scalar_tensor_tensor(scaled[i // GROUP % NS][:, t % GROUP, :], ps[i % 4][:, :], su_dp[:, t:t + 1],
                                         wscale[:, :], ALU.mult, ALU.mult).then_inc(down_evac, 1)

        @block.gpsimd
        def _(pool):
            for j in range(len(JOBS)):
                for s in range(len(JOBS[j][1])):
                    butterflies(pool, j, s, "minus")

        @block.tensor
        def _(pe):
            pe.wait_ge(small_in, 64)
            for i in range(len(JOBS) * TILES):
                j, t = divmod(i, TILES)
                if t == 0:
                    pe.wait_ge(plus_done, before[j + 1])
                    pe.wait_ge(minus_done, before[j + 1])
                if i >= 4:
                    pe.wait_ge(*((evac, i - 3) if i - 4 < 2 * TILES else (down_evac, i - 3 - 2 * TILES)))
                pe.matmul(ps[i % 4][:, :], h128[:, :], buf[plan[j][-1]][:, t, :], start=True, stop=True).then_inc(mm_done, 1)

        @block.scalar
        def _(act):
            act.wait_ge(su_done, 2)
            for i in range(2 * TILES):
                j, t = divmod(i, TILES)
                act.wait_ge(mm_done, i + 1)
                wait_buffer(act, i)
                act.activation(scaled[i // GROUP % NS][:, t % GROUP, :], ps[i % 4][:, :], ACT.Copy,
                               scale=su_ug[:, t // 4:t // 4 + 1]).then_inc(evac, 1)


def ffn_block(nc, x2, W, scratch_w, scratch_part, out):
    ctx = ExitStack()
    with ctx:
        def sb(name, shape, dt=F32):
            return ctx.enter_context(nc.sbuf_tensor(name, shape, dt))

        def pb(name):
            return ctx.enter_context(nc.psum_tensor(name, [P, T2], F32))

        def sem(name):
            return ctx.enter_context(nc.semaphore(name))

        wug = [sb(f"wug_{s}", [P, KT, 2 * FH], F32R) for s in ("hi", "lo")]
        wd = [sb(f"wd_{s}", [P, FT, DM], F32R) for s in ("hi", "lo")]
        stage = [sb(f"stage{i}", [P, FH]) for i in range(2)]
        xs = sb("xs", [P, TB2, DM])
        xT = [sb(f"xT_{s}", [P, KT, T2], F32R) for s in ("hi", "lo")]
        prod = [sb(f"prod_{s}", [P, FT, T2], F32R) for s in ("hi", "lo")]
        s_gate = [sb(f"s_gate{i}", [P, T2]) for i in range(2)]
        p = [sb(f"p{i}", [P, T2]) for i in range(2)]
        part = sb("part", [P, TB2, DM])
        res = sb("res", [P, TB2, DM])
        ident = sb("ident2", [P, P])
        scale_ug = sb("scale_ug", [P, 2 * HT])
        half = sb("half2", [P, TB2])
        stats, mv, veps, rstd = (sb(n, [P, TB2, k]) for n, k in (("fst", 6), ("fmv", 2), ("fve", 1), ("frs", 1)))
        ostats, omv, oveps, orstd = (sb(n, [P, TB2, k]) for n, k in (("ost", 6), ("omv", 2), ("ove", 1), ("ors", 1)))
        pT = [pb(f"pT{i}") for i in range(2)]
        pg = [pb(f"pg{i}") for i in range(2)]
        pu = [pb(f"pu{i}") for i in range(2)]
        po = [pb(f"po{i}") for i in range(2)]

        small_in = sem("f_small_in"); half_set = sem("half_set")
        stage_in = [sem("stage_in0"), sem("stage_in1")]
        w_hi = sem("w_hi"); w_lo = sem("w_lo")
        xs_in = sem("xs_in"); res_in = sem("f_res_in"); part_in = sem("part_in")
        st_done = sem("f_st"); mv_done = sem("f_mv"); veps_done = sem("f_veps"); rstd_done = sem("f_rstd"); xn_done = sem("f_xn")
        xT_filled = sem("xT_filled"); x_hi = sem("x_hi"); x_lo = sem("x_lo")
        gate_mm = sem("gate_mm"); up_mm = sem("up_mm"); silu_done = sem("silu_done"); p_done = sem("p_done")
        p_hi = sem("p_hi"); p_lo = sem("p_lo")
        down_mm = sem("down_mm"); o_evac = sem("o_evac"); part_stored = sem("part_stored")
        ost_done = sem("o_st"); omv_done = sem("o_mv"); oveps_done = sem("o_veps"); orstd_done = sem("o_rstd")
        sp_passed, dve_passed, pool_passed = (sem(f"f_{e}_passed") for e in ("sp", "dve", "pool"))
        o_normed = sem("o_normed"); o_done = sem("o_done"); out_stored = sem("out_stored")

        UG = FT
        PIECES = UG + FT // 2
        PC = 2 * P

        def piece(half_no, q):
            if q < UG:
                j, which = q // 2, 1 - q % 2
                src = scratch_w[which][:, half_no * FH + j * PC:half_no * FH + (j + 1) * PC].rearrange("(k p) f -> p k f", p=P)
                return (src, stage[q % 2][:, :].rearrange("p (k f) -> p k f", k=KT),
                        lambda s: wug[s][:, :, which * FH + j * PC:which * FH + (j + 1) * PC])
            ft = 2 * (q - UG)
            src = scratch_w[2][half_no * FH + ft * P:half_no * FH + (ft + 2) * P, :].rearrange("(a p) m -> p a m", p=P)
            return src, stage[q % 2][:, :].rearrange("p (a m) -> p a m", a=2), lambda s: wd[s][:, ft:ft + 2, :]

        def before_tile(half_no, ck, ft):
            if half_no == 0 and ck_is(ck, 0) and ft < UG // 2:
                return [(0, 2 * ft), (0, 2 * ft + 1)]
            return []

        def after_tile(half_no, ck, ft):
            if ck_is(ck, 0) and ft >= UG // 2:
                return [(half_no, UG // 2 + ft)]
            if half_no + 1 < HALVES and ck_is(ck, NCH2 - 1) and ft % 2:
                return [(half_no + 1, ft - 1), (half_no + 1, ft)]
            return []

        def ck_is(ck, value):
            return isinstance(ck, int) and ck == value

        def run(eng, first_front, step):
            first_front(0)
            for half_no in range(HALVES):
                step(half_no, 0, half_no * NCH2, True)
                with eng.Fori(1, NCH2 - 1) as ck:
                    step(half_no, ck, half_no * NCH2, True)
                step(half_no, NCH2 - 1, half_no * NCH2, half_no + 1 < HALVES)

        block = ctx.enter_context(nc.Block())

        @block.sync
        def _(sp):
            sp.dma_start(ident[:, :], W["ident"]).then_inc(small_in, 16)
            sp.dma_start(scale_ug[:, :], W["Wscale_ug"]).then_inc(small_in, 16)

            def load_xs(chunk, step_no):
                if not (isinstance(step_no, int) and step_no == 0):
                    wait_first(sp, xT_filled, KT * step_no, sp_passed)
                sp.dma_start(xs[:, :, :], x2[bass.ds(chunk, 1), :, :].rearrange("c (a p) m -> p (c a) m", p=P)).then_inc(xs_in, 16)

            def step(half_no, ck, base, more):
                i = ck + base
                if more:
                    load_xs(0 if ck_is(ck, NCH2 - 1) else ck + 1, i + 1)
                if half_no and ck_is(ck, 0):
                    wait_first(sp, part_stored, 16 * NCH2, sp_passed)
                rows = lambda t: t[bass.ds(ck, 1), :, :].rearrange("c (a p) m -> p (c a) m", p=P)
                if half_no == 0:
                    wait_first(sp, o_evac, TB2 * (i + 1), sp_passed)
                    sp.dma_start(rows(scratch_part), part[:, :, :]).then_inc(part_stored, 16)
                else:
                    if not (isinstance(ck, int) and ck == 0):
                        wait_first(sp, o_normed, TB2 * ck, sp_passed)
                        wait_first(sp, out_stored, 16 * ck, sp_passed)
                    sp.dma_start(part[:, :, :], rows(scratch_part)).then_inc(part_in, 16)
                    sp.dma_start(res[:, :, :], rows(x2)).then_inc(res_in, 16)
                    wait_first(sp, o_done, TB2 * (ck + 1), sp_passed)
                    sp.dma_start(rows(out), res[:, :, :]).then_inc(out_stored, 16)

            run(sp, lambda step_no: load_xs(0, step_no), step)
            wait_first(sp, out_stored, 16 * NCH2, sp_passed)

        @block.gpsimd
        def _(pool):
            pool.memset(half[:, :], -0.5).then_inc(half_set, 1)
            pool.wait_ge(half_set, 1)

            def loads(half_no, pieces):
                for q in pieces:
                    n = half_no * PIECES + q
                    if n >= 2:
                        pool.wait_ge(w_lo, n - 1)
                    src, dst, _ = piece(half_no, q)
                    pool.dma_start(dst, src).then_inc(stage_in[q % 2], 16)

            def rsqrt(count, m, ve, r, m_sem, v_sem, r_sem):
                wait_first(pool, m_sem, TB2 * count, pool_passed)
                pool.tensor_scalar(ve[:, :, 0], m[:, :, 1], EPS, 1.0, ALU.add, ALU.mult).then_inc(v_sem, 1)
                pool.wait_ge(v_sem, count)
                pool.tensor_tensor(r[:, :, 0], ve[:, :, 0], half[:, :], ALU.pow).then_inc(r_sem, 1)

            def front(step_no):
                rsqrt(step_no + 1, mv, veps, rstd, mv_done, veps_done, rstd_done)

            def first(step_no):
                loads(0, range(2))
                front(step_no)

            def step(half_no, ck, base, more):
                last = half_no + 1 < HALVES and ck_is(ck, NCH2 - 1)
                if half_no == 0 and ck_is(ck, 0):
                    loads(0, range(2, UG))
                if last:
                    loads(half_no + 1, range(4))
                if more:
                    front(ck + base + 1)
                if last:
                    loads(half_no + 1, range(4, UG + 2))
                if ck_is(ck, 0):
                    loads(half_no, range(UG + 2 if half_no else UG, PIECES))
                if half_no:
                    rsqrt(ck + 1, omv, oveps, orstd, omv_done, oveps_done, orstd_done)

            run(pool, first, step)

        @block.tensor
        def _(pe):
            pe.wait_ge(small_in, 32)

            def turn_x(step_no, tiles):
                pe.wait_ge(xn_done, TB2 * (step_no + 1))
                for kt in tiles:
                    if kt >= 2:
                        pe.wait_ge(x_lo, KT * step_no + kt - 1)
                    for tb in range(TB2):
                        mm = pe.transpose(pT[kt % 2][:, tb * P:(tb + 1) * P], xs[:, tb, kt * P:(kt + 1) * P], ident[:, :])
                    mm.then_inc(xT_filled, 1)

            PASSES = ((0, 0), (0, 1), (1, 0))

            def step(half_no, ck, base, more):
                i = ck + base
                pe.wait_ge(x_lo, KT * (i + 1))
                for ft in range(FT):
                    for bank, which, freed, filled in ((pg, 1, silu_done, gate_mm), (pu, 0, p_done, up_mm)):
                        if ft >= 2:
                            pe.wait_ge(freed, FT * i + ft - 1)
                        if half_no == 0 and ck_is(ck, 0) and ft % 2 == 0:
                            pe.wait_ge(w_lo, ft + 2 - which)
                        elif ck_is(ck, 0) and ft == 0:
                            pe.wait_ge(w_lo, half_no * PIECES + UG)
                        for kt in range(KT):
                            for n, (a, b) in enumerate(PASSES):
                                lo = which * FH + ft * P
                                mm = pe.matmul(bank[ft % 2][:, :], wug[a][:, kt, lo:lo + P], xT[b][:, kt, :],
                                               start=(kt == 0 and n == 0), stop=(kt == KT - 1 and n == len(PASSES) - 1))
                        mm.then_inc(filled, 1)
                if more:
                    turn_x(i + 1, range(2))
                if ck_is(ck, 0):
                    pe.wait_ge(w_lo, PIECES * (half_no + 1))
                for tb in range(TB2):
                    if more and tb == 1:
                        turn_x(i + 1, range(2, KT))
                    if tb == 0 and not (isinstance(i, int) and i == 0):
                        pe.wait_ge(o_evac, TB2 * i)
                    elif tb >= 2:
                        pe.wait_ge(o_evac, TB2 * i + tb - 1)
                    for ft in range(FT):
                        if tb == 0:
                            pe.wait_ge(p_lo, FT * i + ft + 1)
                        for n, (a, b) in enumerate(PASSES):
                            mm = pe.matmul(po[tb % 2][:, :], prod[a][:, ft, tb * P:(tb + 1) * P], wd[b][:, ft, :],
                                           start=(ft == 0 and n == 0), stop=(ft == FT - 1 and n == len(PASSES) - 1))
                    mm.then_inc(down_mm, 1)

            run(pe, lambda step_no: turn_x(step_no, range(KT)), step)

        @block.scalar
        def _(act):
            act.wait_ge(small_in, 32)

            def weights(pieces):
                for half_no, q in pieces:
                    act.wait_ge(stage_in[q % 2], 16 * (half_no * PIECES // 2 + q // 2 + 1))
                    if half_no and q < UG:
                        act.wait_ge(up_mm, (NCH2 - 1) * FT + 2 * (q // 2) + 2)
                    if half_no and q == UG:
                        act.wait_ge(down_mm, NCH2 * TB2)
                    _, src, dst = piece(half_no, q)
                    act.activation(dst(0), src, ACT.Copy).then_inc(w_hi, 1)

            def front(step_no):
                for kt in range(KT):
                    act.wait_ge(xT_filled, KT * step_no + kt + 1)
                    act.activation(xT[0][:, kt, :], pT[kt % 2][:, :], ACT.Copy).then_inc(x_hi, 1)

            def step(half_no, ck, base, more):
                i = ck + base
                for ft in range(FT):
                    f = half_no * FT + ft
                    weights(before_tile(half_no, ck, ft))
                    act.wait_ge(gate_mm, FT * i + ft + 1)
                    if ft >= 2:
                        act.wait_ge(p_done, FT * i + ft - 1)
                    act.activation(s_gate[ft % 2][:, :], pg[ft % 2][:, :], ACT.Silu,
                                   scale=scale_ug[:, HT + f:HT + f + 1]).then_inc(silu_done, 1)
                    act.wait_ge(p_done, FT * i + ft + 1)
                    if ft == 0 and not (isinstance(i, int) and i == 0):
                        act.wait_ge(down_mm, TB2 * i)
                    act.activation(prod[0][:, ft, :], p[ft % 2][:, :], ACT.Copy).then_inc(p_hi, 1)
                    weights(after_tile(half_no, ck, ft))
                if more:
                    front(i + 1)
                if half_no == 0:
                    for tb in range(TB2):
                        act.wait_ge(down_mm, TB2 * i + tb + 1)
                        if tb == 0 and not (isinstance(i, int) and i == 0):
                            act.wait_ge(part_stored, 16 * i)
                        act.activation(part[:, tb, :], po[tb % 2][:, :], ACT.Copy).then_inc(o_evac, 1)

            run(act, front, step)

        @block.vector
        def _(dve):
            dve.wait_ge(small_in, 32)

            def weights(pieces):
                for half_no, q in pieces:
                    dve.wait_ge(w_hi, half_no * PIECES + q + 1)
                    _, src, dst = piece(half_no, q)
                    dve.tensor_tensor(dst(1), src, dst(0).bitcast(F32), ALU.subtract).then_inc(w_lo, 1)

            def norm_stats(step_no):
                dve.wait_ge(xs_in, 16 * (step_no + 1))
                for tb in range(TB2):
                    dve.bn_stats(stats[:, tb, :], xs[:, tb, :]).then_inc(st_done, 1)
                for tb in range(TB2):
                    wait_first(dve, st_done, TB2 * step_no + tb + 1, dve_passed)
                    dve.bn_aggr(mv[:, tb, :], stats[:, tb, :]).then_inc(mv_done, 1)

            def norm(step_no):
                dve.wait_ge(rstd_done, step_no + 1)
                for tb in range(TB2):
                    dve.tensor_scalar(xs[:, tb, :], xs[:, tb, :], mv[:, tb, 0:1], rstd[:, tb, :],
                                      ALU.subtract, ALU.mult).then_inc(xn_done, 1)

            def split_x(step_no):
                for kt in range(KT):
                    dve.wait_ge(x_hi, KT * step_no + kt + 1)
                    dve.tensor_tensor(xT[1][:, kt, :], pT[kt % 2][:, :], xT[0][:, kt, :].bitcast(F32),
                                      ALU.subtract).then_inc(x_lo, 1)

            def front(step_no):
                norm_stats(step_no)
                norm(step_no)
                split_x(step_no)

            def step(half_no, ck, base, more):
                i = ck + base
                for ft in range(FT):
                    f = half_no * FT + ft
                    weights(before_tile(half_no, ck, ft))
                    dve.wait_ge(silu_done, FT * i + ft + 1)
                    dve.wait_ge(up_mm, FT * i + ft + 1)
                    if ft >= 2:
                        dve.wait_ge(p_lo, FT * i + ft - 1)
                    dve.scalar_tensor_tensor(p[ft % 2][:, :], pu[ft % 2][:, :], scale_ug[:, f:f + 1], s_gate[ft % 2][:, :],
                                             ALU.mult, ALU.mult).then_inc(p_done, 1)
                    dve.wait_ge(p_hi, FT * i + ft + 1)
                    dve.tensor_tensor(prod[1][:, ft, :], p[ft % 2][:, :], prod[0][:, ft, :].bitcast(F32),
                                      ALU.subtract).then_inc(p_lo, 1)
                    weights(after_tile(half_no, ck, ft))
                    if more and ft == 2:
                        norm_stats(i + 1)
                    if more and ft == 4:
                        norm(i + 1)
                if more:
                    split_x(i + 1)
                if half_no:
                    for tb in range(TB2):
                        if tb == 0:
                            dve.wait_ge(part_in, 16 * (ck + 1))
                        dve.wait_ge(down_mm, TB2 * i + tb + 1)
                        dve.tensor_tensor(part[:, tb, :], po[tb % 2][:, :], part[:, tb, :], ALU.add).then_inc(o_evac, 1)
                        dve.wait_ge(o_evac, TB2 * i + tb + 1)
                        dve.bn_stats(ostats[:, tb, :], part[:, tb, :]).then_inc(ost_done, 1)
                        wait_first(dve, ost_done, TB2 * ck + tb + 1, dve_passed)
                        dve.bn_aggr(omv[:, tb, :], ostats[:, tb, :]).then_inc(omv_done, 1)
                    dve.wait_ge(orstd_done, ck + 1)
                    dve.wait_ge(res_in, 16 * (ck + 1))
                    for tb in range(TB2):
                        dve.tensor_scalar(part[:, tb, :], part[:, tb, :], omv[:, tb, 0:1], orstd[:, tb, :],
                                          ALU.subtract, ALU.mult).then_inc(o_normed, 1)
                    for tb in range(TB2):
                        dve.wait_ge(o_normed, TB2 * ck + tb + 1)
                        dve.tensor_tensor(res[:, tb, :], res[:, tb, :], part[:, tb, :], ALU.add).then_inc(o_done, 1)

            run(dve, front, step)


_INS = ['L0_attn_hidden_states', 'L0_attn_W_in', 'L0_attn_b_in', 'L0_attn_conv_w', 'L0_attn_conv_b', 'L0_attn_W_x',
        'L0_attn_W_dt', 'L0_attn_b_dt', 'L0_attn_W_out', 'L0_attn_b_out', 'L0_attn_a_log', 'L0_attn_d_param',
        'L0_ffn_SU_ug', 'L0_ffn_SU_dp', 'L0_ffn_Wscale_ug', 'L0_ffn_Wscale_dp', 'L0_ffn_W_up', 'L0_ffn_W_gate',
        'L0_ffn_W_down']


def kernel(**inputs):
    import numpy as np
    import concourse.bacc as bacc
    from concourse.bass_utils import run_bass_kernel_spmd

    nc = bacc.Bacc("TRN2", target_bir_lowering=False, num_devices=1)
    arrays, W = {}, {}

    def give(name, a):
        a = np.ascontiguousarray(a)
        arrays[f"in_{name}"] = a
        W[name] = nc.dram_tensor(f"in_{name}", a.shape, mybir.dt.from_np(a.dtype), kind="ExternalInput").ap()

    by_partition = ("b_in", "conv_b", "b_dt", "d_param", "SU_ug", "SU_dp", "Wscale_ug")
    for name in _INS:
        short = name.replace("L0_attn_", "").replace("L0_ffn_", "")
        a = np.asarray(inputs[name])
        if short == "conv_w":
            a = a.reshape(KC, DT, P).transpose(2, 1, 0)
        elif short == "a_log":
            a = a.reshape(DT, P, NST).transpose(1, 0, 2)
        elif short in ("W_up", "W_gate", "W_down"):
            a = a.T
        elif short in by_partition:
            a = a.reshape(-1, P).T
        give(short, a)
    give("ident", np.eye(P, dtype=np.float32))
    h = np.ones((1, 1), np.float32)
    while len(h) < P:
        h = np.block([[h, h], [h, -h]])
    give("h128", h)
    give("ones", np.ones((1, P), np.float32))
    out = nc.dram_tensor("out", (TOK, DM), F32, kind="ExternalOutput").ap()
    scratch_bc = nc.dram_tensor("scratch_bc", (NCH, 2 * NST, T), F32, kind="Internal").ap()
    x = W["hidden_states"].rearrange("b l m -> (b l) m").rearrange("(c t) m -> c t m", t=T)
    x2 = nc.dram_tensor("scratch_x2", (TOK, DM), F32, kind="Internal").ap()
    scratch_w = [nc.dram_tensor(f"scratch_w_{n}", shape, F32, kind="Internal").ap()
                 for n, shape in (("up", (DM, FF)), ("gate", (DM, FF)), ("down", (FF, DM)))]
    scratch_part = nc.dram_tensor("scratch_part", (NCH2, T2, DM), F32, kind="Internal").ap()
    hadamard_block(nc, W, scratch_w)
    mamba_block(nc, x, W, scratch_bc, x2.rearrange("(c t) m -> c t m", t=T))
    ffn_block(nc, x2.rearrange("(c t) m -> c t m", t=T2), W, scratch_w, scratch_part,
              out.rearrange("(c t) m -> c t m", t=T2))
    r = run_bass_kernel_spmd(nc, [arrays], core_ids=[0])
    return r.results[0]["out"].reshape(BATCH, SEQ, DM)
```
